# Optimizing a Trainium2 kernel written in Bass

```python
import numpy as np
import jax
import jax.numpy as jnp

def _softmax(x, axis=-1):
    return jax.nn.softmax(x, axis=axis)

def _gelu(x):
    return jax.nn.gelu(x, approximate=True)

def _silu(x):
    return jax.nn.silu(x)

def _sigmoid(x):
    return jax.nn.sigmoid(x)

def _layernorm(x, axis=-1, eps=1e-05):
    m = jnp.mean(x, axis=axis, keepdims=True)
    v = jnp.var(x, axis=axis, keepdims=True)
    return (x - m) / jnp.sqrt(v + eps)

def _scatter_add(tgt, idx, src, axis=0):
    return tgt.at[idx].add(src)

def _segment_sum(src, seg, n):
    return jax.ops.segment_sum(src, seg, n)
kernel_name = 'mk_decoder_postln_d1_seqx_r4_291969'

def setup_inputs(seed: int=0):
    np.random.seed(seed)
    _w = jnp.asarray

    def _rec_inputs():
        import jax
        import jax.numpy as jnp
        _rk = jax.random.key(seed)
        x = 7.22e-05 + 1 * jax.random.normal(jax.random.fold_in(_rk, 1), (4, 512, 512), jnp.float32)
        _lenS = 512 - jax.random.randint(jax.random.fold_in(_rk, 7), (4,), 0, max(1, 512 // 4) + 1, jnp.int32)
        _lenS2 = 512 - jax.random.randint(jax.random.fold_in(_rk, 8), (4,), 0, max(1, 512 // 4) + 1, jnp.int32)
        _ctx_512P = jax.random.normal(jax.random.fold_in(_rk, 11), (4, 16, 128), jnp.float32)
        _ctx_512c = jax.random.dirichlet(jax.random.fold_in(_rk, 511), 0.3 * jnp.ones((16,), jnp.float32), (4, 512))
        _ctx_512t = jnp.einsum('bsk,bkd->bsd', _ctx_512c, _ctx_512P)
        _ctx_512t = _ctx_512t * jax.lax.rsqrt(jnp.mean(jnp.square(_ctx_512t)) + 1e-12) * 0.953939
        ctx_512 = -0.000514642 + 1.00011 * (_ctx_512t + 0.3 * jax.random.normal(jax.random.fold_in(_rk, 611), (4, 512, 128), jnp.float32))
        return (x, ctx_512)
    x, ctx_512 = _rec_inputs()

    def _L0_attn_setup():
        import jax, jax.numpy as jnp
        import numpy as np
        B, T, D = (1, 512, 512)
        H, DK, DV, M = (16, 64, 128, 64)
        KEY_DIM, VALUE_DIM = (H * DK, H * DV)
        EPS = 1e-05
        CLAMP_MIN, CLAMP_MAX = (-32.0, 32.0)
        XAVIER_GAIN = 2.0 ** (-2.5)

        def _chunk_abc(q, k, v, s):
            scale = q.shape[-1] ** (-0.5)
            z = jax.lax.cumlogsumexp(s, axis=2)
            g = jnp.exp(jnp.concatenate([z[:, :, :1], z[:, :, :-1]], axis=2) - z)
            p = jnp.exp(s - z)
            tfirst = lambda x: jnp.moveaxis(x, 2, 0)
            qT, kT, vT, pT, gT = map(tfirst, (q * scale, k, v, p, g))
            b, h = (q.shape[0], q.shape[1])
            hk0 = jnp.zeros((b, h, q.shape[-1], s.shape[-1]), q.dtype)

            def step_k(hk, x):
                q_t, k_t, p_t, g_t = x
                hk = hk * g_t[:, :, None, :] + k_t[..., None] * p_t[:, :, None, :]
                return (hk, jnp.einsum('bhk,bhkm->bhm', q_t, hk))
            _, okT = jax.lax.scan(step_k, hk0, (qT, kT, pT, gT))
            pvT = jax.nn.softmax(okT, axis=-1)
            hv0 = jnp.zeros((b, h, s.shape[-1], v.shape[-1]), q.dtype)

            def step_v(hv, x):
                pv_t, v_t, p_t, g_t = x
                hv = hv * g_t[..., None] + p_t[..., None] * v_t[:, :, None, :]
                return (hv, jnp.einsum('bhm,bhmv->bhv', pv_t, hv))
            _, ovT = jax.lax.scan(step_v, hv0, (pvT, vT, pT, gT))
            return jnp.moveaxis(ovT, 0, 2)
        key = jax.random.key(seed)
        ks = jax.random.split(key, 8)

        def w(k, fan_in, fan_out):
            std = XAVIER_GAIN * np.sqrt(2.0 / (fan_in + fan_out))
            return jax.random.normal(k, (fan_in, fan_out), jnp.float32) * std
        return {'hidden_states': jax.random.normal(ks[0], (B, T, D), jnp.float32), 'Wq': w(ks[1], D, KEY_DIM), 'Wk': w(ks[2], D, KEY_DIM), 'Wv': w(ks[3], D, VALUE_DIM), 'Wg': w(ks[4], D, VALUE_DIM), 'Ws': w(ks[5], D, H * M), 'Wo': w(ks[6], VALUE_DIM, D), 'g_norm_weight': jnp.ones((DV,), jnp.float32)}
    _L0_attn_all = _L0_attn_setup()
    _L0_attn_in = {k: v for k, v in _L0_attn_all.items() if k in ('Wq', 'Wk', 'Wv', 'Wg', 'Ws', 'Wo', 'g_norm_weight')}
    del _L0_attn_all

    def _L0_xattn_setup():
        import jax, jax.numpy as jnp
        import numpy as np
        B, S, E = (2, 512, 512)
        QH, KVH = (32, 8)
        D = E // QH
        G = QH // KVH
        DROPOUT = 1.0
        key = jax.random.key(seed)
        k1, k2, k3 = jax.random.split(key, 3)
        q = jax.random.normal(k1, (B, S, E), dtype=jnp.float32)
        k = jax.random.normal(k2, (B, S, E // G), dtype=jnp.float32)
        v = jax.random.normal(k3, (B, S, E // G), dtype=jnp.float32)
        return {'q': q, 'k': k, 'v': v}
    _L0_xattn_all = _L0_xattn_setup()
    _L0_xattn_in = {k: v for k, v in _L0_xattn_all.items() if k in ()}
    del _L0_xattn_all

    def _L0_ffn_setup():
        import jax, jax.numpy as jnp
        import numpy as np
        HIDDEN = 512
        INTER = 1408
        B, S = (2, 512)

        def _ternary(key, shape):
            return jax.random.randint(key, shape, -1, 2).astype(jnp.float32)
        key = jax.random.key(seed)
        ks = jax.random.split(key, 7)
        x = jax.random.normal(ks[0], (B, S, HIDDEN), dtype=jnp.float32)
        gate_w = _ternary(ks[1], (INTER, HIDDEN))
        up_w = _ternary(ks[2], (INTER, HIDDEN))
        down_w = _ternary(ks[3], (HIDDEN, INTER))
        gate_s = jax.random.uniform(ks[4], (INTER,), minval=0.01, maxval=0.1, dtype=jnp.float32)
        up_s = jax.random.uniform(ks[5], (INTER,), minval=0.01, maxval=0.1, dtype=jnp.float32)
        down_s = jax.random.uniform(ks[6], (HIDDEN,), minval=0.01, maxval=0.1, dtype=jnp.float32)
        return {'x': x, 'gate_w': gate_w, 'up_w': up_w, 'down_w': down_w, 'gate_s': gate_s, 'up_s': up_s, 'down_s': down_s}
    _L0_ffn_all = _L0_ffn_setup()
    _L0_ffn_in = {k: v for k, v in _L0_ffn_all.items() if k in ('gate_w', 'up_w', 'down_w', 'gate_s', 'up_s', 'down_s')}
    del _L0_ffn_all
    return {'x': x, 'ctx_512': ctx_512, 'L0_attn_Wq': _L0_attn_in['Wq'], 'L0_attn_Wk': _L0_attn_in['Wk'], 'L0_attn_Wv': _L0_attn_in['Wv'], 'L0_attn_Wg': _L0_attn_in['Wg'], 'L0_attn_Ws': _L0_attn_in['Ws'], 'L0_attn_Wo': _L0_attn_in['Wo'], 'L0_attn_g_norm_weight': _L0_attn_in['g_norm_weight'], 'L0_ffn_gate_w': _L0_ffn_in['gate_w'], 'L0_ffn_up_w': _L0_ffn_in['up_w'], 'L0_ffn_down_w': _L0_ffn_in['down_w'], 'L0_ffn_gate_s': _L0_ffn_in['gate_s'], 'L0_ffn_up_s': _L0_ffn_in['up_s'], 'L0_ffn_down_s': _L0_ffn_in['down_s']}

def reference(x, ctx_512, L0_attn_Wq, L0_attn_Wk, L0_attn_Wv, L0_attn_Wg, L0_attn_Ws, L0_attn_Wo, L0_attn_g_norm_weight, L0_ffn_gate_w, L0_ffn_up_w, L0_ffn_down_w, L0_ffn_gate_s, L0_ffn_up_s, L0_ffn_down_s):
    import jax
    import jax.numpy as jnp

    def _L0_attn_ref(hidden_states, Wq, Wk, Wv, Wg, Ws, Wo, g_norm_weight):
        import jax, jax.numpy as jnp
        import numpy as np
        B, T, D = (1, 512, 512)
        H, DK, DV, M = (16, 64, 128, 64)
        KEY_DIM, VALUE_DIM = (H * DK, H * DV)
        EPS = 1e-05
        CLAMP_MIN, CLAMP_MAX = (-32.0, 32.0)
        XAVIER_GAIN = 2.0 ** (-2.5)

        def _chunk_abc(q, k, v, s):
            scale = q.shape[-1] ** (-0.5)
            z = jax.lax.cumlogsumexp(s, axis=2)
            g = jnp.exp(jnp.concatenate([z[:, :, :1], z[:, :, :-1]], axis=2) - z)
            p = jnp.exp(s - z)
            tfirst = lambda x: jnp.moveaxis(x, 2, 0)
            qT, kT, vT, pT, gT = map(tfirst, (q * scale, k, v, p, g))
            b, h = (q.shape[0], q.shape[1])
            hk0 = jnp.zeros((b, h, q.shape[-1], s.shape[-1]), q.dtype)

            def step_k(hk, x):
                q_t, k_t, p_t, g_t = x
                hk = hk * g_t[:, :, None, :] + k_t[..., None] * p_t[:, :, None, :]
                return (hk, jnp.einsum('bhk,bhkm->bhm', q_t, hk))
            _, okT = jax.lax.scan(step_k, hk0, (qT, kT, pT, gT))
            pvT = jax.nn.softmax(okT, axis=-1)
            hv0 = jnp.zeros((b, h, s.shape[-1], v.shape[-1]), q.dtype)

            def step_v(hv, x):
                pv_t, v_t, p_t, g_t = x
                hv = hv * g_t[..., None] + p_t[..., None] * v_t[:, :, None, :]
                return (hv, jnp.einsum('bhm,bhmv->bhv', pv_t, hv))
            _, ovT = jax.lax.scan(step_v, hv0, (pvT, vT, pT, gT))
            return jnp.moveaxis(ovT, 0, 2)
        b, t, _ = hidden_states.shape
        to_heads = lambda x, d: jnp.transpose(x.reshape(b, t, H, d), (0, 2, 1, 3))
        q = to_heads(hidden_states @ Wq, DK)
        k = to_heads(hidden_states @ Wk, DK)
        v = to_heads(hidden_states @ Wv, DV)
        s = jnp.clip(to_heads(hidden_states @ Ws, M), CLAMP_MIN, CLAMP_MAX)
        o = jnp.transpose(_chunk_abc(q, k, v, s), (0, 2, 1, 3))
        g = (hidden_states @ Wg).reshape(b, t, H, DV)
        o = o * jax.lax.rsqrt(jnp.mean(jnp.square(o), axis=-1, keepdims=True) + EPS) * g_norm_weight
        o = o * (g * jax.nn.sigmoid(g))
        return o.reshape(b, t, VALUE_DIM) @ Wo

    def _L0_xattn_ref(q, k, v):
        import jax, jax.numpy as jnp
        import numpy as np
        B, S, E = (2, 512, 512)
        QH, KVH = (32, 8)
        D = E // QH
        G = QH // KVH
        DROPOUT = 1.0
        b, s, _ = q.shape
        qh = q.reshape(b, s, KVH, G, D).transpose(0, 2, 3, 1, 4)
        kh = k.reshape(b, s, KVH, D).transpose(0, 2, 1, 3)
        vh = v.reshape(b, s, KVH, D).transpose(0, 2, 1, 3)
        scale = 1.0 / jnp.sqrt(jnp.float32(D))
        scores = jnp.einsum('bkgsd,bktd->bkgst', qh, kh) * scale
        attn = jax.nn.softmax(scores, axis=-1) / DROPOUT
        out = jnp.einsum('bkgst,bktd->bkgsd', attn, vh)
        return out.transpose(0, 3, 1, 2, 4).reshape(b, s, E)

    def _L0_ffn_ref(x, gate_w, up_w, down_w, gate_s, up_s, down_s):
        import jax, jax.numpy as jnp
        import numpy as np
        HIDDEN = 512
        INTER = 1408
        B, S = (2, 512)

        def _ternary(key, shape):
            return jax.random.randint(key, shape, -1, 2).astype(jnp.float32)
        b, s, h = x.shape
        xf = x.reshape(b * s, h)
        g = jnp.einsum('th,ih->ti', xf, gate_w) * gate_s
        u = jnp.einsum('th,ih->ti', xf, up_w) * up_s
        hdn = jax.nn.silu(g) * u
        out = jnp.einsum('ti,hi->th', hdn, down_w) * down_s
        return out.reshape(b, s, -1)
    x = _layernorm(x + _L0_attn_ref(x, L0_attn_Wq, L0_attn_Wk, L0_attn_Wv, L0_attn_Wg, L0_attn_Ws, L0_attn_Wo, L0_attn_g_norm_weight), axis=-1)
    x = _layernorm(x + _L0_xattn_ref(x, ctx_512, ctx_512), axis=-1)
    x = _layernorm(x + _L0_ffn_ref(x, L0_ffn_gate_w, L0_ffn_up_w, L0_ffn_down_w, L0_ffn_gate_s, L0_ffn_up_s, L0_ffn_down_s), axis=-1)
    return x

_drawn_inputs = setup_inputs


def setup_inputs(seed=0):
    import zlib

    import numpy as np

    out = dict(_drawn_inputs(seed))
    spreads = {'L0_attn_g_norm_weight': (1.0, 0.6)}
    factors = {'L0_attn_Wq': 8.0,
     'L0_attn_Wk': 8.0,
     'L0_attn_Wv': 3.925,
     'L0_attn_Wg': 3.9,
     'L0_attn_Ws': 8.0,
     'L0_attn_Wo': 3.909}
    for name, (base, spread) in spreads.items():
        noise = np.random.default_rng([zlib.crc32(name.encode()), seed]).standard_normal(out[name].shape)
        drawn = base * np.exp(spread * noise) if base else spread * noise
        out[name] = jnp.asarray(drawn.astype(out[name].dtype))
    for name, factor in factors.items():
        out[name] = (out[name] * factor).astype(out[name].dtype)
    return out
```

```python
import concourse.bass as bass
from concourse import mybir
from contextlib import ExitStack

F32 = mybir.dt.float32
F32R = mybir.dt.float32r
ALU = mybir.AluOpType
ACT = mybir.ActivationFunctionType
AX = mybir.AxisListType

P = 128
B = 4
T = 512
D = 512
KT = D // P
TT = T // P
NTT = B * TT
EPS = 1e-5

PAIRS = 8
DK = 64
DV = 128
NSTEP = PAIRS * B
QK_SCALE = DK ** -0.5
CLAMP = 32.0
PROJ = 7

CHUNKS = [[(0, 0)], [(3, 0), (1, P)], [(2, 0)]]
CHUNK_AT = [0, 512, 1024]
CHUNK_LEN = [512, 512, 256]
KEY_AT = {i: CHUNK_AT[c] + at for c, tiles in enumerate(CHUNKS) for i, at in tiles}
CAUSAL = 1280

QH = 32
KVH = 8
DH = 16
X_SCALE = DH ** -0.5
ROWS = 64
MAXROW = 3 * DH
UNITS = B * 4

INTER = 1408
IC = INTER // P


def wait(eng, sem, value):
    if isinstance(value, int) and value <= 0:
        return
    eng.wait_ge(sem, value)


def mm3(pe, out, w, x, start, stop):
    (w_hi, w_lo), (x_hi, x_lo) = w, x
    pe.matmul(out, w_lo, x_hi, start=start, stop=False)
    pe.matmul(out, w_hi, x_lo, start=False, stop=False)
    return pe.matmul(out, w_hi, x_hi, start=False, stop=stop)


def phase_attention(nc, x, Wq, Wk, Wv, Wg, Ws, Wo, gw, acc, ident):
    with ExitStack() as ctx:
        def sb(name, shape, dt=F32):
            return ctx.enter_context(nc.sbuf_tensor("a_" + name, shape, dt))

        def sem(name):
            return ctx.enter_context(nc.semaphore("a_" + name))

        xT_hi = sb("xT_hi", [P, KT, B * T], F32R)
        xT_lo = sb("xT_lo", [P, KT, B * T], F32R)
        raw_qks = sb("raw_qks", [P, KT, 3, P])
        raw_vg = sb("raw_vg", [P, KT, 2, 2 * DV])
        raw_wo = sb("raw_wo", [P, 2, D])
        qks_hi = sb("qks_hi", [P, KT, 3, P], F32R)
        qks_lo = sb("qks_lo", [P, KT, 3, P], F32R)
        vg_hi = sb("vg_hi", [P, KT, 4 * DV], F32R)
        vg_lo = sb("vg_lo", [P, KT, 4 * DV], F32R)
        wo_hi = sb("wo_hi", [P, 2, D], F32R)
        wo_lo = sb("wo_lo", [P, 2, D], F32R)
        qT = sb("qT", [P, T])
        kT = sb("kT", [P, T])
        eT = sb("eT", [P, 2, T])
        e = sb("e", [P, TT, P])
        rz = sb("rz", [P, T])
        v = sb("v", [P, 2, TT, 2 * DV])
        gate = sb("gate", [P, 2, TT, 2 * DV])
        causal = sb("causal", [P, 2, CAUSAL])
        okn = sb("okn", [P, T])
        pv = sb("pv", [P, 2 * TT, DK])
        wT = okn
        og = sb("og", [P, 2 * TT, DV])
        squares = pv[:, :, :].bitcast(mybir.dt.bfloat16)
        oT_hi = sb("oT_hi", [P, 2, T], F32R)
        oT_lo = sb("oT_lo", [P, 2, T], F32R)
        mask = sb("mask", [P, 4, P])
        gw_half = sb("gw_half", [P, 1])
        mx = sb("mx", [P, 2 * TT])
        rowsum = sb("rowsum", [P, 2 * TT])
        rs = sb("rs", [P, 2 * TT])
        ss = sb("ss", [P, 2 * TT])
        f1 = sb("f1", [P, 2 * TT])
        f2 = sb("f2", [P, 2 * TT])
        zero = sb("zero", [P, 1, 1])
        eps = sb("eps", [P, 2 * TT])
        minus_half = sb("minus_half", [P, 2 * TT])
        ps = ctx.enter_context(nc.psum_tensor("a_ps", [P, 8, 512], F32))
        pj = [ps[:, 0, :], ps[:, 1, :]]
        ch = [ps[:, 2, :], ps[:, 3, :]]
        tb = ps[:, 4, :]
        okb = ps[:, 5, :]
        ob = [ps[:, 6, :], ps[:, 7, :]]

        x_in = [sem(f"x_in{b}") for b in range(B)]
        gw_in = sem("gw_in")
        gw_ready = sem("gw_ready")
        zeroed = sem("zeroed")
        const_ready = sem("const_ready")
        xt_done = sem("xt_done")
        xhi_ready = sem("xhi_ready")
        xlo_ready = sem("xlo_ready")
        raw_qks_in = sem("raw_qks_in")
        raw_vg_in = sem("raw_vg_in")
        raw_wo_in = sem("raw_wo_in")
        qks_hi_ready = sem("qks_hi_ready")
        vg_hi_ready = sem("vg_hi_ready")
        wo_hi_ready = sem("wo_hi_ready")
        qks_ready = sem("qks_ready")
        vg_ready = sem("vg_ready")
        wo_ready = sem("wo_ready")
        proj_done = sem("proj_done")
        chunk_done = sem("chunk_done")
        oT_done = sem("oT_done")
        wo_done = sem("wo_done")
        okT_done = sem("okT_done")
        ok_done = sem("ok_done")
        pvT_done = sem("pvT_done")
        o_done = sem("o_done")
        e_done = sem("e_done")
        qk_ready = sem("qk_ready")
        eT_ready = sem("eT_ready")
        v_ready = sem("v_ready")
        tanh_ready = sem("tanh_ready")
        chunk_act = sem("chunk_act")
        oThi_ready = sem("oThi_ready")
        pv_ready = sem("pv_ready")
        sq_done = sem("sq_done")
        e_ready = sem("e_ready")
        clip_done = sem("clip_done")
        gate_ready = sem("gate_ready")
        scan_done = sem("scan_done")
        rz_ready = sem("rz_ready")
        chunk_dve = sem("chunk_dve")
        oTlo_ready = sem("oTlo_ready")
        added = sem("added")
        okn_ready = sem("okn_ready")
        mx_ready = sem("mx_ready")
        sub_ready = sem("sub_ready")
        sum_ready = sem("sum_ready")
        rs_ready = sem("rs_ready")
        wT_ready = sem("wT_ready")
        og_ready = sem("og_ready")
        masked = sem("masked")
        fac = sem("fac")
        ogs_ready = sem("ogs_ready")

        FAC = 5

        block = ctx.enter_context(nc.Block())

        def load_pair(sp, p):
            for w, m in enumerate((Wq, Wk, Ws)):
                sp.dma_start(raw_qks[:, :, w, :],
                             m[:, bass.ts(p, P)].rearrange("(k p) c -> p k c", p=P)).then_inc(raw_qks_in, 16)
            for w, m in enumerate((Wv, Wg)):
                sp.dma_start(raw_vg[:, :, w, :],
                             m[:, bass.ts(p, 2 * DV)].rearrange("(k p) c -> p k c", p=P)).then_inc(raw_vg_in, 16)
            sp.dma_start(raw_wo[:, :, :],
                         Wo[bass.ts(p, 2 * DV), :].rearrange("(k p) c -> p k c", p=P)).then_inc(raw_wo_in, 16)

        @block.sync
        def _(sp):
            for b in range(B):
                sp.dma_start(acc[:, TT * b:TT * (b + 1), :],
                             x[b].rearrange("(t p) d -> p t d", p=P)).then_inc(x_in[b], 16)
                if b == 0:
                    load_pair(sp, 0)
            sp.dma_start(gw_half[:, :], gw.rearrange("(p o) -> p o", o=1)).then_inc(gw_in, 16)
            with sp.Fori(1, PAIRS) as p:
                sp.wait_ge(qks_ready, p)
                sp.wait_ge(vg_ready, p)
                sp.wait_ge(wo_ready, p)
                load_pair(sp, p)

        @block.gpsimd
        def _(pool):
            nc.gpsimd.memset(ident[:, :], 0.0).then_inc(zeroed, 1)
            nc.gpsimd.memset(mask[:, :, :], 1.0).then_inc(zeroed, 1)
            nc.gpsimd.memset(minus_half[:, :], -0.5).then_inc(zeroed, 1)
            nc.gpsimd.memset(zero[:, :, :], 0.0).then_inc(zeroed, 1)
            nc.gpsimd.memset(eps[:, :], EPS).then_inc(zeroed, 1)
            pool.wait_ge(zeroed, 5)
            nc.gpsimd.affine_select(out=ident[:, :], in_=ident[:, :], compare_op=ALU.not_equal, fill=1.0, base=0,
                                    pattern=[[-1, P]], channel_multiplier=1).then_inc(const_ready, 1)
            nc.gpsimd.affine_select(out=mask[:, 0:2, :], in_=mask[:, 0:2, :], compare_op=ALU.is_ge, fill=0.0, base=0,
                                    pattern=[[0, 2], [1, P]], channel_multiplier=-1).then_inc(const_ready, 1)
            pool.wait_ge(gw_in, 16)
            nc.gpsimd.tensor_scalar(gw_half[:, :], gw_half[:, :], 0.5, None, ALU.mult).then_inc(gw_ready, 1)

            def split(raw, hi, lo, hi_ready, ready, k):
                nc.gpsimd.tensor_tensor(hi, raw, zero[:, :, :].broadcast_to(raw.shape), ALU.add).then_inc(hi_ready, 1)
                pool.wait_ge(hi_ready, k)
                nc.gpsimd.tensor_tensor(lo, raw, hi.bitcast(F32), ALU.subtract).then_inc(ready, 1)

            def split_qks(p):
                pool.wait_ge(raw_qks_in, (p + 1) * 48)
                split(raw_qks[:, :, :, :].rearrange("p k w c -> p k (w c)"),
                      qks_hi[:, :, :, :].rearrange("p k w c -> p k (w c)"),
                      qks_lo[:, :, :, :].rearrange("p k w c -> p k (w c)"), qks_hi_ready, qks_ready, p + 1)

            def split_vg(p):
                pool.wait_ge(raw_vg_in, (p + 1) * 32)
                split(raw_vg[:, :, :, :].rearrange("p k w c -> p k (w c)"), vg_hi[:, :, :], vg_lo[:, :, :],
                      vg_hi_ready, vg_ready, p + 1)

            def split_wo(p):
                pool.wait_ge(raw_wo_in, (p + 1) * 16)
                split(raw_wo[:, :, :], wo_hi[:, :, :], wo_lo[:, :, :], wo_hi_ready, wo_ready, p + 1)

            def mask_diagonals(n, which):
                for h in range(2):
                    wait(pool, chunk_act, 4 * n + 2 * which + h + 1)
                    nc.gpsimd.tensor_tensor(causal[:, h, 0:P], causal[:, h, 0:P], mask[:, 0, :],
                                            ALU.mult).then_inc(masked, 1)

            def step(n, p, j, last):
                mask_diagonals(n, 0)
                mask_diagonals(n, 1)
                if j == 2 and not last:
                    pool.wait_ge(proj_done, PROJ * (n + 1) + 3)
                    split_qks(p + 1)
                wait(pool, sq_done, 2 * n + 2)
                wait(pool, rs_ready, n + 1)
                nc.gpsimd.tensor_tensor(f1[:, :], rs[:, :], rs[:, :], ALU.mult).then_inc(fac, 1)
                pool.wait_ge(fac, FAC * n + 1)
                nc.gpsimd.tensor_tensor(f2[:, :], f1[:, :], ss[:, :], ALU.mult).then_inc(fac, 1)
                pool.wait_ge(fac, FAC * n + 2)
                nc.gpsimd.tensor_tensor(f1[:, :], f2[:, :], eps[:, :], ALU.add).then_inc(fac, 1)
                pool.wait_ge(fac, FAC * n + 3)
                nc.gpsimd.tensor_tensor(f2[:, :], f1[:, :], minus_half[:, :], ALU.pow).then_inc(fac, 1)
                pool.wait_ge(fac, FAC * n + 4)
                nc.gpsimd.tensor_tensor(f1[:, :], f2[:, :], rs[:, :], ALU.mult).then_inc(fac, 1)
                pool.wait_ge(fac, FAC * n + 5)
                wait(pool, og_ready, 2 * n + 2)
                nc.gpsimd.tensor_tensor(og[:, :, :], og[:, :, :],
                                        f1[:, :].rearrange("p (g o) -> p g o", o=1).broadcast_to([P, 2 * TT, DV]),
                                        ALU.mult).then_inc(ogs_ready, 1)
                if j == 2 and not last:
                    pool.wait_ge(proj_done, PROJ * (n + 1) + PROJ)
                    split_vg(p + 1)
                if j == 0 and not (isinstance(n, int) and n == 0):
                    pool.wait_ge(wo_done, 4 * n)
                    split_wo(p)

            split_qks(0)
            split_vg(0)
            split_wo(0)
            for j in range(B):
                step(j, 0, j, False)
            with pool.Fori(1, PAIRS - 1) as p:
                for j in range(B):
                    step(p * B + j, p, j, False)
            for j in range(B):
                step((PAIRS - 1) * B + j, PAIRS - 1, j, True)

        @block.tensor
        def _(pe):
            def transpose4(bank, blocks):
                for i, src in enumerate(blocks):
                    last = pe.transpose(bank[:, i * P:(i + 1) * P], src, ident[:, :])
                return last

            def project(m, i, b, pair):
                bank = pj[(b + i) % 2]
                if i < 2:
                    wait(pe, gate_ready, 4 * m - 1 + i)
                elif i < 4:
                    pe.wait_ge(qk_ready, 2 * m + i - 1)
                elif i == 4:
                    pe.wait_ge(clip_done, m + 1)
                else:
                    pe.wait_ge(gate_ready, 4 * m + i - 4)
                if i == 0:
                    pe.wait_ge(qks_ready, pair + 1)
                if i == 3:
                    pe.wait_ge(vg_ready, pair + 1)
                for k in range(KT):
                    if i < 3:
                        mm = mm3(pe, bank, (qks_hi[:, k, i, :], qks_lo[:, k, i, :]),
                                 (xT_hi[:, k, b * T:(b + 1) * T], xT_lo[:, k, b * T:(b + 1) * T]), k == 0, k == KT - 1)
                    else:
                        t = b * T + (i - 3) * P
                        mm = mm3(pe, bank, (xT_hi[:, k, t:t + P], xT_lo[:, k, t:t + P]),
                                 (vg_hi[:, k, :], vg_lo[:, k, :]), k == 0, k == KT - 1)
                mm.then_inc(proj_done, 1)

            def chunks(n, which, left, right):
                for c in range(3):
                    for h in range(2):
                        if c == 0:
                            wait(pe, chunk_dve, 8 * n + 4 * which - 1 + h)
                        elif c == 1:
                            pe.wait_ge(chunk_act, 4 * n + 2 * which + h + 1)
                        else:
                            pe.wait_ge(chunk_dve, 8 * n + 4 * which + h + 1)
                        r = slice(DK * h, DK * (h + 1))
                        for i, at in CHUNKS[c]:
                            w = T - i * P
                            mm = pe.matmul(ch[h][:, at:at + w], left[r, i * P:(i + 1) * P], right[r, i * P:T],
                                           start=True, stop=True)
                        mm.then_inc(chunk_done, 1)

            def out_rows(n, done=False):
                wait(pe, ogs_ready, n)
                for h in range(2):
                    if h == 0:
                        pe.wait_ge(sub_ready if done else e_ready, n if done else n + 1)
                    else:
                        wait(pe, wT_ready, n)
                    transpose4(tb if h == 0 else okb,
                               [og[:, 2 * t + h, :] for t in range(TT)]).then_inc(oT_done, 1)

            def project_out(n, pair):
                pe.wait_ge(wo_ready, pair + 1)
                wait(pe, oTlo_ready, 2 * n)
                for t in range(TT):
                    if t < 2:
                        wait(pe, og_ready, 2 * (n - 1) + 2)
                    else:
                        wait(pe, added, 4 * (n - 1) + t - 1)
                    for h in range(2):
                        mm = mm3(pe, ob[t % 2], (oT_hi[:, h, t * P:(t + 1) * P], oT_lo[:, h, t * P:(t + 1) * P]),
                                 (wo_hi[:, h, :], wo_lo[:, h, :]), h == 0, h == 1)
                    mm.then_inc(wo_done, 1)

            def slots(n):
                pe.wait_ge(masked, 4 * n + 2)
                pe.wait_ge(chunk_dve, 8 * n + 4)
                wait(pe, oTlo_ready, 2 * n)
                for i in range(TT):
                    for h in range(2):
                        mm = pe.matmul(okb[DK * h:DK * (h + 1), i * P:T], e[:, i, DK * h:DK * (h + 1)],
                                       causal[:, h, KEY_AT[i]:KEY_AT[i] + T - i * P],
                                       start=(i == 0), stop=(i == TT - 1))
                mm.then_inc(okT_done, 1)

            def values(n, j):
                pe.wait_ge(masked, 4 * n + 4)
                pe.wait_ge(chunk_dve, 8 * n + 8)
                pe.wait_ge(v_ready, 4 * n + 4)
                wait(pe, added, 4 * n)
                for t in range(TT):
                    for h in range(2):
                        for i in range(t + 1):
                            at = KEY_AT[i] + (t - i) * P
                            c = (2 * (t % 2) + h) * P
                            mm = pe.matmul(ob[t // 2][:, c:c + P], causal[:, h, at:at + P],
                                           v[:, j % 2, i, h * DV:(h + 1) * DV], start=(i == 0), stop=(i == t))
                    if t % 2:
                        mm.then_inc(o_done, 1)

            def transpose_e(m, b):
                pe.wait_ge(eT_ready, m + 1)
                wait(pe, sub_ready, m)
                transpose4(tb, [eT[:, b % 2, i * P:(i + 1) * P] for i in range(TT)]).then_inc(e_done, 1)

            def step(n, p, j, first, last):
                b1, pair1 = (j + 1) % B, p if j < B - 1 else p + 1
                pe.wait_ge(qk_ready, 2 * n + 2)
                chunks(n, 0, kT, qT)
                if not first:
                    out_rows(n)
                if not last:
                    project(n + 1, 0, b1, pair1)
                if not first:
                    project_out(n, p if j else p - 1)
                pe.wait_ge(e_ready, n + 1)
                slots(n)
                if not last:
                    project(n + 1, 1, b1, pair1)
                pe.wait_ge(okn_ready, n + 1)
                wait(pe, oThi_ready, 2 * n)
                transpose4(tb, [okn[:, t * P:(t + 1) * P] for t in range(TT)]).then_inc(ok_done, 1)
                if not last:
                    project(n + 1, 2, b1, pair1)
                    project(n + 1, 3, b1, pair1)
                pe.wait_ge(pv_ready, n + 1)
                transpose4(okb, [pv[:, 2 * t:2 * t + 2, :].rearrange("p h m -> p (h m)") for t in range(TT)])\
                    .then_inc(pvT_done, 1)
                if not last:
                    project(n + 1, 4, b1, pair1)
                pe.wait_ge(wT_ready, n + 1)
                chunks(n, 1, eT[:, j % 2, :], wT)
                if not last:
                    project(n + 1, 5, b1, pair1)
                values(n, j)
                if not last:
                    project(n + 1, 6, b1, pair1)
                    transpose_e(n + 1, b1)

            pe.wait_ge(const_ready, 1)
            for b in range(B):
                pe.wait_ge(x_in[b], 16)
                for k in range(KT):
                    u = b * KT + k
                    if u >= 8:
                        pe.wait_ge(xlo_ready, u - 7)
                    transpose4(ps[:, u % 8, :], [acc[:, TT * b + t, k * P:(k + 1) * P] for t in range(TT)])\
                        .then_inc(xt_done, 1)
            pe.wait_ge(xlo_ready, B * KT)
            for i in range(PROJ):
                project(0, i, 0, 0)
            transpose_e(0, 0)
            for j in range(B):
                step(j, 0, j, j == 0, False)
            with pe.Fori(1, PAIRS - 1) as p:
                for j in range(B):
                    step(p * B + j, p, j, False, False)
            for j in range(B):
                step((PAIRS - 1) * B + j, PAIRS - 1, j, False, j == B - 1)
            out_rows(NSTEP, True)
            project_out(NSTEP, PAIRS - 1)

        @block.scalar
        def _(act):
            def copy_proj(m, i, b):
                act.wait_ge(proj_done, PROJ * m + i + 1)
                bank = pj[(b + i) % 2]
                if i < 2:
                    nc.scalar.copy((qT, kT)[i][:, :], bank).then_inc(qk_ready, 1)
                elif i == 2:
                    act.wait_ge(clip_done, m + 1)
                    nc.scalar.activation(eT[:, b % 2, :], eT[:, b % 2, :], ACT.Exp).then_inc(eT_ready, 1)
                else:
                    nc.scalar.copy(v[:, b % 2, i - 3, :], bank[:, 0:2 * DV]).then_inc(v_ready, 1)
                    wait(act, og_ready, 2 * (m - 1))
                    nc.scalar.activation(gate[:, b % 2, i - 3, :], bank[:, 2 * DV:4 * DV], ACT.Tanh,
                                         scale=0.5).then_inc(tanh_ready, 1)

            def copy_chunk0(n, which):
                for h in range(2):
                    wait(act, chunk_done, 12 * n + 6 * which + h + 1)
                    nc.scalar.copy(causal[:, h, 0:CHUNK_LEN[0]], ch[h]).then_inc(chunk_act, 1)

            def copy_oT(n):
                for h in range(2):
                    wait(act, oT_done, 2 * (n - 1) + h + 1)
                    nc.scalar.activation(oT_hi[:, h, :], tb if h == 0 else okb, ACT.Copy,
                                         scale=gw_half[:, 0:1]).then_inc(oThi_ready, 1)

            def copy_e(m):
                act.wait_ge(e_done, m + 1)
                nc.scalar.copy(e[:, :, :].rearrange("p i c -> p (i c)"), tb).then_inc(e_ready, 1)

            def step(n, j, first, last):
                b1 = (j + 1) % B
                copy_chunk0(n, 0)
                if not first:
                    copy_oT(n)
                if not last:
                    copy_proj(n + 1, 0, b1)
                    copy_proj(n + 1, 1, b1)
                act.wait_ge(sub_ready, n + 1)
                nc.scalar.activation(pv[:, :, :], pv[:, :, :], ACT.Exp, scale=QK_SCALE).then_inc(pv_ready, 1)
                if not last:
                    copy_proj(n + 1, 2, b1)
                    copy_proj(n + 1, 3, b1)
                    copy_proj(n + 1, 4, b1)
                copy_chunk0(n, 1)
                if not last:
                    copy_proj(n + 1, 5, b1)
                for half in range(2):
                    act.wait_ge(o_done, 2 * n + half + 1)
                    for g in range(4):
                        sq = nc.scalar.activation(squares[:, 4 * half + g, :], ob[half][:, g * P:(g + 1) * P], ACT.Square, scale=DV ** -0.5,
                                                  accum_out=ss[:, 4 * half + g:4 * half + g + 1])
                    sq.then_inc(sq_done, 1)
                if not last:
                    copy_proj(n + 1, 6, b1)
                    copy_e(n + 1)

            for u in range(B * KT):
                act.wait_ge(xt_done, u + 1)
                b, k = u // KT, u % KT
                nc.scalar.copy(xT_hi[:, k, b * T:(b + 1) * T], ps[:, u % 8, :]).then_inc(xhi_ready, 1)
            for i in range(PROJ):
                copy_proj(0, i, 0)
            copy_e(0)
            act.wait_ge(gw_ready, 1)
            for j in range(B):
                step(j, j, j == 0, False)
            with act.Fori(1, PAIRS - 1) as p:
                for j in range(B):
                    step(p * B + j, j, False, False)
            for j in range(B):
                step((PAIRS - 1) * B + j, j, False, j == B - 1)
            copy_oT(NSTEP)

        @block.vector
        def _(dve):
            def clip(m, b):
                dve.wait_ge(proj_done, PROJ * m + 3)
                nc.vector.tensor_scalar(eT[:, b % 2, :], pj[b % 2], CLAMP, -CLAMP, ALU.min, ALU.max)\
                    .then_inc(clip_done, 1)

            def gating(m, i, b):
                dve.wait_ge(tanh_ready, 4 * m + i - 2)
                nc.vector.scalar_tensor_tensor(out=gate[:, b % 2, i - 3, :], in0=gate[:, b % 2, i - 3, :], scalar=1.0,
                                               in1=pj[(b + i) % 2][:, 2 * DV:4 * DV], op0=ALU.add, op1=ALU.mult)\
                    .then_inc(gate_ready, 1)

            def inverse_z(m, b):
                dve.wait_ge(eT_ready, m + 1)
                nc.vector.tensor_tensor_scan(rz[:, :], eT[:, b % 2, :], eT[:, b % 2, :], 0.0, ALU.add, ALU.bypass)\
                    .then_inc(scan_done, 1)
                dve.wait_ge(scan_done, m + 1)
                nc.vector.reciprocal(rz[:, :], rz[:, :]).then_inc(rz_ready, 1)

            def mask_chunks(n, which):
                for c in (1, 2):
                    for h in range(2):
                        dve.wait_ge(chunk_done, 12 * n + 6 * which + 2 * c + h + 1)
                        m = mask[:, 0:4, :] if c == 1 else mask[:, 1:3, :]
                        nc.vector.tensor_tensor(causal[:, h, CHUNK_AT[c]:CHUNK_AT[c] + CHUNK_LEN[c]],
                                                ch[h][:, 0:CHUNK_LEN[c]], m.rearrange("p a t -> p (a t)"),
                                                ALU.mult).then_inc(chunk_dve, 1)

            def low_oT(n):
                for h in range(2):
                    wait(dve, oThi_ready, 2 * (n - 1) + h + 1)
                    nc.vector.scalar_tensor_tensor(out=oT_lo[:, h, :], in0=tb if h == 0 else okb,
                                                   scalar=gw_half[:, 0:1], in1=oT_hi[:, h, :].bitcast(F32),
                                                   op0=ALU.mult, op1=ALU.subtract).then_inc(oTlo_ready, 1)

            def add_out(n, b):
                for t in range(TT):
                    wait(dve, wo_done, 4 * (n - 1) + t + 1)
                    a = acc[:, TT * b + t, :]
                    nc.vector.tensor_tensor(a, a, ob[t % 2], ALU.add).then_inc(added, 1)

            def step(n, j, first, last):
                b1 = (j + 1) % B
                mask_chunks(n, 0)
                if not first:
                    low_oT(n)
                    add_out(n, (j - 1) % B)
                dve.wait_ge(okT_done, n + 1)
                dve.wait_ge(rz_ready, n + 1)
                nc.vector.tensor_tensor(okn[:, :], okb, rz[:, :], ALU.mult).then_inc(okn_ready, 1)
                dve.wait_ge(ok_done, n + 1)
                scores = tb.rearrange("p (g m) -> p g m", m=DK)
                nc.vector.tensor_reduce(mx[:, :], scores, AX.X, ALU.max).then_inc(mx_ready, 1)
                dve.wait_ge(mx_ready, n + 1)
                nc.vector.tensor_tensor(pv[:, :, :], scores,
                                        mx[:, :].rearrange("p (g o) -> p g o", o=1).broadcast_to([P, 2 * TT, DK]),
                                        ALU.subtract).then_inc(sub_ready, 1)
                if not last:
                    clip(n + 1, b1)
                    gating(n + 1, 3, b1)
                dve.wait_ge(pv_ready, n + 1)
                nc.vector.tensor_reduce(rowsum[:, :], pv[:, :, :], AX.X, ALU.add).then_inc(sum_ready, 1)
                dve.wait_ge(pvT_done, n + 1)
                nc.vector.tensor_tensor(wT[:, :], okb, rz[:, :], ALU.mult).then_inc(wT_ready, 1)
                dve.wait_ge(sum_ready, n + 1)
                nc.vector.reciprocal(rs[:, :], rowsum[:, :]).then_inc(rs_ready, 1)
                if not last:
                    gating(n + 1, 4, b1)
                mask_chunks(n, 1)
                if not last:
                    gating(n + 1, 5, b1)
                for half in range(2):
                    dve.wait_ge(sq_done, 2 * n + half + 1)
                    nc.vector.tensor_tensor(og[:, 4 * half:4 * half + 4, :].rearrange("p g c -> p (g c)"), ob[half],
                                            gate[:, j % 2, 2 * half:2 * half + 2, :].rearrange("p t c -> p (t c)"),
                                            ALU.mult).then_inc(og_ready, 1)
                if not last:
                    gating(n + 1, 6, b1)
                    inverse_z(n + 1, b1)

            for u in range(B * KT):
                dve.wait_ge(xhi_ready, u + 1)
                b, k = u // KT, u % KT
                hi = xT_hi[:, k, b * T:(b + 1) * T].bitcast(F32)
                nc.vector.tensor_tensor(xT_lo[:, k, b * T:(b + 1) * T], ps[:, u % 8, :], hi, ALU.subtract)\
                    .then_inc(xlo_ready, 1)
            clip(0, 0)
            for i in range(3, PROJ):
                gating(0, i, 0)
            inverse_z(0, 0)
            dve.wait_ge(const_ready, 2)
            for j in range(B):
                step(j, j, j == 0, False)
            with dve.Fori(1, PAIRS - 1) as p:
                for j in range(B):
                    step(p * B + j, j, False, False)
            for j in range(B):
                step((PAIRS - 1) * B + j, j, False, j == B - 1)
            low_oT(NSTEP)
            add_out(NSTEP, B - 1)


class Norm:

    def __init__(self, ctx, nc, name, acc):
        self.nc, self.acc = nc, acc
        self.stats = ctx.enter_context(nc.sbuf_tensor(name + "_stats", [P, B, TT, 6], F32))
        self.mv = ctx.enter_context(nc.sbuf_tensor(name + "_mv", [P, B, TT, 2], F32))
        self.rstd = ctx.enter_context(nc.sbuf_tensor(name + "_rstd", [P, B, TT], F32))
        self.eps = ctx.enter_context(nc.sbuf_tensor(name + "_eps", [P, TT], F32))
        self.minus_half = ctx.enter_context(nc.sbuf_tensor(name + "_minus_half", [P, TT], F32))
        self.const_ready = ctx.enter_context(nc.semaphore(name + "_const"))
        self.stats_ready = ctx.enter_context(nc.semaphore(name + "_stats_ready"))
        self.mv_ready = ctx.enter_context(nc.semaphore(name + "_mv_ready"))
        self.var_ready = ctx.enter_context(nc.semaphore(name + "_var_ready"))
        self.rstd_ready = ctx.enter_context(nc.semaphore(name + "_rstd_ready"))
        self.done = ctx.enter_context(nc.semaphore(name + "_done"))

    def constants(self):
        self.nc.gpsimd.memset(self.eps[:, :], EPS).then_inc(self.const_ready, 1)
        self.nc.gpsimd.memset(self.minus_half[:, :], -0.5).then_inc(self.const_ready, 1)

    def statistics(self, dve, b):
        nc = self.nc
        for t in range(TT):
            nc.vector.bn_stats(self.stats[:, b, t, :], self.acc[:, TT * b + t, :]).then_inc(self.stats_ready, 1)
        for t in range(TT):
            dve.wait_ge(self.stats_ready, TT * b + t + 1)
            nc.vector.bn_aggr(self.mv[:, b, t, :], self.stats[:, b, t, :]).then_inc(self.mv_ready, 1)

    def inverse_deviation(self, pool, b):
        nc = self.nc
        pool.wait_ge(self.const_ready, 2)
        pool.wait_ge(self.mv_ready, TT * (b + 1))
        nc.gpsimd.tensor_tensor(self.rstd[:, b, :], self.mv[:, b, :, 1], self.eps[:, :], ALU.add)\
            .then_inc(self.var_ready, 1)
        pool.wait_ge(self.var_ready, b + 1)
        nc.gpsimd.tensor_tensor(self.rstd[:, b, :], self.rstd[:, b, :], self.minus_half[:, :], ALU.pow)\
            .then_inc(self.rstd_ready, 1)

    def apply(self, dve, b):
        dve.wait_ge(self.rstd_ready, b + 1)
        for t in range(TT):
            a = self.acc[:, TT * b + t, :]
            self.nc.vector.tensor_scalar(a, a, self.mv[:, b, t, 0:1], self.rstd[:, b, t:t + 1],
                                         ALU.subtract, ALU.mult).then_inc(self.done, 1)


def phase_cross(nc, ctx_in, acc, ident):
    with ExitStack() as ctx:
        def sb(name, shape, dt=F32):
            return ctx.enter_context(nc.sbuf_tensor("x_" + name, shape, dt))

        def sem(name):
            return ctx.enter_context(nc.semaphore("x_" + name))

        norm = Norm(ctx, nc, "x_norm", acc)
        cin = sb("cin", [P, NTT, KVH * DH])
        xrows = sb("xrows", [P, 2, TT, P])
        krows = sb("krows", [P, 2, TT, 2 * DH])
        cv = sb("cv", [P, 4, TT, 2, 32])
        xq = sb("xq", [P, 2, TT, 8, ROWS])
        kn = sb("kn", [P, 2, TT, 2, 2, ROWS])
        qs = sb("qs", [P, 4, 4, T], F32R)
        ks = sb("ks", [P, 4, 2, T], F32R)
        prob = sb("prob", [P, 4, 2, T])
        nm = sb("nm", [P, 2, TT, 2, 4])
        mhl = sb("mhl", [P, 2, TT, 2, 2, 4])
        mT = sb("mT", [16, 2, T])
        avs = sb("avs", [P, 2, T])
        rec = sb("rec", [P, 2, TT, 4])
        avn = sb("avn", [P, 2, TT, 4, DH])
        zero = sb("zero", [P, 1])
        ps = ctx.enter_context(nc.psum_tensor("x_ps", [P, 8, 512], F32))
        mxb = [ps[:, 0, :], ps[:, 1, :]]
        exb = [ps[:, 2:4, :], ps[:, 4:6, :]]
        avb = ps[:, 6, :]
        trb = ps[:, 7, :]

        cin_in = sem("cin_in")
        rows_in = [sem(f"rows_in{i}") for i in range(2)]
        cleared = sem("cleared")
        const_ready = sem("const_ready")
        ops_hi = sem("ops_hi")
        ops_ready = sem("ops_ready")
        opsT_done = sem("opsT_done")
        opsT_ready = sem("opsT_ready")
        max_done = sem("max_done")
        max_read = sem("max_read")
        mhi_ready = sem("mhi_ready")
        mhl_ready = sem("mhl_ready")
        mT_done = sem("mT_done")
        mT_ready = sem("mT_ready")
        mrow_in = sem("mrow_in")
        score_done = sem("score_done")
        exp_done = sem("exp_done")
        av_done = sem("av_done")
        avs_ready = sem("avs_ready")
        avT_done = sem("avT_done")
        rec_ready = sem("rec_ready")
        avn_ready = sem("avn_ready")
        added = sem("added")

        block = ctx.enter_context(nc.Block())

        def each_batch(eng, body):
            body(0, True, False)
            with eng.Fori(1, B - 1) as b:
                body(b, False, False)
            body(B - 1, False, True)

        @block.sync
        def _(sp):
            sp.dma_start(cin[:, :, :], ctx_in.rearrange("b (t p) d -> p (b t) d", p=P)).then_inc(cin_in, 16)

            def put_max_rows(u, q):
                sp.wait_ge(mT_ready, u + 1)
                for par in range(2):
                    for part in range(2):
                        sp.dma_start(qs[ROWS * par + MAXROW + part:ROWS * par + MAXROW + part + 1, q, :, :].bitcast(F32),
                                     mT[8 * par + 4 * part:8 * par + 4 * part + 4, q % 2, :]).then_inc(mrow_in, 16)

            def get_rows(u, b, q):
                wait(sp, ops_ready, u - 1)
                for rows, src in ((xrows, acc), (krows, cin)):
                    w = rows.shape[3]
                    sp.dma_start(rows[:, q % 2, :, :], src[:, bass.ds(b * TT, TT), w * q:w * (q + 1)])\
                        .then_inc(rows_in[q % 2], 16)

            sp.wait_ge(norm.done, TT)
            sp.wait_ge(cin_in, 16)
            for q in range(4):
                get_rows(q, 0, q)
            sp.wait_ge(norm.done, NTT)
            put_max_rows(0, 0)

            def body(b, first, last):
                for q in range(4):
                    if not (last and q == 3):
                        put_max_rows(b * 4 + q + 1, (q + 1) % 4)
                    if not last:
                        get_rows(b * 4 + q + 4, b + 1, q)

            each_batch(sp, body)

        @block.gpsimd
        def _(pool):
            norm.constants()
            nc.gpsimd.memset(zero[:, :], 0.0).then_inc(cleared, 1)
            nc.gpsimd.memset(xq[:, :, :, :, :], 0.0).then_inc(cleared, 1)
            nc.gpsimd.memset(kn[:, :, :, :, :, :], 0.0).then_inc(cleared, 1)
            nc.gpsimd.memset(cv[:, :, :, :, :], 0.0).then_inc(cleared, 1)
            pool.wait_ge(cleared, 4)
            for s in range(2):
                nc.gpsimd.memset(kn[:, s, :, :, :, MAXROW:MAXROW + 2].rearrange("p t h c m -> p (t h c) m"), 1.0)\
                    .then_inc(const_ready, 1)
            nc.gpsimd.memset(cv[:, :, :, :, DH:DH + 1].rearrange("p q t h c -> p (q t h) c"), 1.0).then_inc(const_ready, 1)
            pool.wait_ge(const_ready, 3)

            def copy(out, in_):
                z = zero[:, :]
                for _ in range(len(in_.shape) - 2):
                    z = z.rearrange("p (o z) -> p o z", o=1) if len(z.shape) == 2 else \
                        z.rearrange("p a (o z) -> p a o z", o=1)
                return nc.gpsimd.tensor_tensor(out, in_, z.broadcast_to(in_.shape), ALU.add)

            def operands(u, b, q):
                wait(pool, opsT_done, 6 * (u - 1))
                pool.wait_ge(rows_in[q % 2], 32 * (2 * b + q // 2 + 1))
                rows = xrows[:, q % 2].rearrange("p t (h c) -> p t h c", c=DH)
                x = xq[:, q % 2]
                keys = krows[:, q % 2].rearrange("p t (h c) -> p t h c", c=DH)
                k = kn[:, q % 2]
                wait(pool, av_done, 16 * (u - 3))
                copy(cv[:, q, :, :, 0:DH], keys)
                copy(x[:, :, :, 0:DH].bitcast(F32R), rows)
                copy(x[:, :, :, DH:2 * DH].bitcast(F32R), rows)
                for c in range(2):
                    copy(k[:, :, :, c, 0:DH].bitcast(F32R), keys)
                    last = copy(k[:, :, :, c, 2 * DH:3 * DH].bitcast(F32R), keys)
                last.then_inc(ops_hi, 1)
                pool.wait_ge(ops_hi, u + 1)
                nc.gpsimd.tensor_tensor(x[:, :, :, 2 * DH:3 * DH].bitcast(F32R), rows, x[:, :, :, 0:DH], ALU.subtract)
                for c in range(2):
                    last = nc.gpsimd.tensor_tensor(k[:, :, :, c, DH:2 * DH].bitcast(F32R), keys,
                                                   k[:, :, :, c, 0:DH], ALU.subtract)
                last.then_inc(ops_ready, 1)

            def split_max(u, q):
                pool.wait_ge(max_read, 32 * (u + 1))
                wait(pool, mT_done, u - 1)
                m = mhl[:, q % 2]
                copy(m[:, :, :, 0, :].bitcast(F32R), nm[:, q % 2]).then_inc(mhi_ready, 1)
                pool.wait_ge(mhi_ready, u + 1)
                nc.gpsimd.tensor_tensor(m[:, :, :, 1, :].bitcast(F32R), nm[:, q % 2], m[:, :, :, 0, :], ALU.subtract)\
                    .then_inc(mhl_ready, 1)

            for b in range(B):
                norm.inverse_deviation(pool, b)
            for q in range(3):
                operands(q, 0, q)
            split_max(0, 0)

            def body(b, first, last):
                for q in range(4):
                    u = b * 4 + q
                    if not (last and q == 3):
                        split_max(u + 1, (q + 1) % 4)
                    if not (last and q >= 1):
                        operands(u + 3, b if q == 0 else b + 1, (q + 3) % 4)

            each_batch(pool, body)

        @block.tensor
        def _(pe):
            def transpose_operands(u, q, i):
                if i == 0:
                    pe.wait_ge(ops_ready, u + 1)
                for t in range(TT):
                    if i < 2:
                        src = kn[:, q % 2, t, i, :, :].rearrange("p c r -> p (c r)")
                    else:
                        src = xq[:, q % 2, t, 2 * (i - 2):2 * (i - 2) + 2, :].rearrange("p h r -> p (h r)")
                    mm = pe.transpose(trb[:, t * P:(t + 1) * P], src, ident[:, :])
                mm.then_inc(opsT_done, 1)

            def max_scores(u, q, i):
                tile, st = i // 4, i % 4
                if st == 0:
                    pe.wait_ge(opsT_ready, 6 * u + 3 + tile)
                for par in range(2):
                    wait(pe, max_read, 32 * u + 2 * i + par - 1)
                    r = slice(ROWS * par, ROWS * (par + 1))
                    pe.matmul(mxb[par], qs[r, q, tile, st * P:(st + 1) * P], ks[r, q, tile // 2, :],
                              start=True, stop=True).then_inc(max_done, 1)

            def transpose_max(u, q):
                pe.wait_ge(mhl_ready, u + 1)
                for t in range(TT):
                    mm = pe.transpose(trb[0:16, t * P:(t + 1) * P],
                                      mhl[:, q % 2, t].rearrange("p a b c -> p (a b c)"), ident[:, :])
                mm.then_inc(mT_done, 1)

            def scores(u, q, s):
                g, t, pair = s // 8, s // 2 % 4, s % 2
                if s == 0:
                    pe.wait_ge(mrow_in, 64 * (u + 1))
                wait(pe, exp_done, 16 * u + s - 1)
                for par in range(2):
                    r = slice(ROWS * par, ROWS * (par + 1))
                    mm = pe.matmul(exb[s % 2][:, par, :], ks[r, q, g, t * P:(t + 1) * P], qs[r, q, 2 * g + pair, :],
                                   start=True, stop=True)
                mm.then_inc(score_done, 1)

            def weighted(u, b, q, s):
                g, t, pair = s // 8, s // 2 % 4, s % 2
                pe.wait_ge(exp_done, 16 * u + s + 1)
                if s % 8 == 0:
                    wait(pe, avs_ready, 2 * u + g)
                for par in range(2):
                    c = 32 * (2 * pair + par)
                    mm = pe.matmul(avb[c:c + 32, :], cv[:, q, t, g, :], prob[:, s % 4, par, :],
                                   start=(t == 0), stop=(t == TT - 1))
                mm.then_inc(av_done, 1)

            def transpose_weighted(u, g):
                pe.wait_ge(avs_ready, 2 * u + g + 1)
                for t in range(TT):
                    mm = pe.transpose(trb[:, t * P:(t + 1) * P], avs[:, g, t * P:(t + 1) * P], ident[:, :])
                mm.then_inc(avT_done, 1)

            for u in range(2):
                for i in range(6):
                    wait(pe, opsT_ready, 6 * u + i)
                    transpose_operands(u, u, i)
            for i in range(24):
                max_scores(i // 16, i // 16, i % 16)
            pe.wait_ge(opsT_ready, 12)
            transpose_max(0, 0)

            def body(b, first, last):
                for q in range(4):
                    u = b * 4 + q
                    for s in range(16):
                        scores(u, q, s)
                        ahead = 1 if s < 8 else 2
                        if not (last and q + ahead > 3):
                            max_scores(u + ahead, (q + ahead) % 4, (s + 8) % 16)
                        if s:
                            weighted(u, b, q, s - 1)
                        elif not (first and q == 0):
                            weighted(u - 1, b if q else b - 1, (q - 1) % 4, 15)
                        if s == 1 and not (first and q == 0):
                            wait(pe, avn_ready, 2 * u - 1)
                            wait(pe, mT_ready, u + 1)
                            transpose_weighted(u - 1, 1)
                        if 2 <= s < 8 and not (last and q > 1):
                            if s == 2:
                                wait(pe, avn_ready, 2 * u)
                                wait(pe, mT_ready, u + 1)
                            else:
                                pe.wait_ge(opsT_ready, 6 * (u + 2) + s - 2)
                            transpose_operands(u + 2, (q + 2) % 4, s - 2)
                        if s == 10 and not (last and q == 3):
                            if last and q > 1:
                                wait(pe, avn_ready, 2 * u)
                            else:
                                pe.wait_ge(opsT_ready, 6 * (u + 3))
                            transpose_max(u + 1, (q + 1) % 4)
                        if s == 12:
                            if last and q == 3:
                                wait(pe, avn_ready, 2 * u)
                            else:
                                pe.wait_ge(mT_ready, u + 2)
                            transpose_weighted(u, 0)

            each_batch(pe, body)
            weighted(UNITS - 1, B - 1, 3, 15)
            pe.wait_ge(avn_ready, 2 * UNITS - 1)
            transpose_weighted(UNITS - 1, 1)

        @block.scalar
        def _(act):
            def copy_operand(u, q, i):
                act.wait_ge(opsT_done, 6 * u + i + 1)
                nc.scalar.copy(ks[:, q, i, :] if i < 2 else qs[:, q, i - 2, :], trb).then_inc(opsT_ready, 1)

            def copy_max(u, q):
                act.wait_ge(mT_done, u + 1)
                wait(act, mrow_in, 64 * (u - 1))
                nc.scalar.copy(mT[:, q % 2, :], trb[0:16, :]).then_inc(mT_ready, 1)

            def copy_weighted(u, g):
                act.wait_ge(av_done, 16 * u + 8 * g + 8)
                wait(act, avT_done, 2 * u + g - 1)
                nc.scalar.copy(avs[:, g, :], avb).then_inc(avs_ready, 1)

            for u in range(2):
                for i in range(6):
                    copy_operand(u, u, i)
            copy_max(0, 0)

            def body(b, first, last):
                for q in range(4):
                    u = b * 4 + q
                    for s in range(16):
                        act.wait_ge(score_done, 16 * u + s + 1)
                        wait(act, av_done, 16 * u + s - 3)
                        nc.scalar.activation(prob[:, s % 4, :, :], exb[s % 2], ACT.Exp, scale=X_SCALE)\
                            .then_inc(exp_done, 1)
                        if s == 0 and not (first and q == 0):
                            copy_weighted(u - 1, 1)
                        if 2 <= s < 8 and not (last and q > 1):
                            copy_operand(u + 2, (q + 2) % 4, s - 2)
                        if s == 8:
                            copy_weighted(u, 0)
                        if s == 10 and not (last and q == 3):
                            copy_max(u + 1, (q + 1) % 4)

            each_batch(act, body)
            copy_weighted(UNITS - 1, 1)

        @block.vector
        def _(dve):
            def reduce_max(u, q, i):
                if i == 0:
                    wait(dve, mhl_ready, u - 1)
                for par in range(2):
                    dve.wait_ge(max_done, 32 * u + 2 * i + par + 1)
                    nc.vector.tensor_reduce(nm[:, q % 2, i % 4, par, i // 4:i // 4 + 1], mxb[par], AX.X, ALU.max,
                                            negate=True).then_inc(max_read, 1)

            def normalise(u, g):
                dve.wait_ge(avT_done, 2 * u + g + 1)
                rows = trb.rearrange("p (t h c) -> p t h c", t=TT, h=4)
                nc.vector.reciprocal(rec[:, g, :, :], rows[:, :, :, DH]).then_inc(rec_ready, 1)
                dve.wait_ge(rec_ready, 2 * u + g + 1)
                nc.vector.tensor_tensor(avn[:, g], rows[:, :, :, 0:DH],
                                        rec[:, g].rearrange("p t (h o) -> p t h o", o=1).broadcast_to([P, TT, 4, DH]),
                                        ALU.mult).then_inc(avn_ready, 1)

            def add(u, b, q, g):
                dve.wait_ge(avn_ready, 2 * u + g + 1)
                a = acc[:, bass.ds(b * TT, TT), P * q + 64 * g:P * q + 64 * (g + 1)]
                nc.vector.tensor_tensor(a, a, avn[:, g].rearrange("p t h c -> p t (h c)"), ALU.add).then_inc(added, 1)

            for b in range(B):
                norm.statistics(dve, b)
                norm.apply(dve, b)
            for i in range(24):
                reduce_max(i // 16, i // 16, i % 16)

            def body(b, first, last):
                for q in range(4):
                    u = b * 4 + q
                    for s in range(16):
                        ahead = 1 if s < 8 else 2
                        if not (last and q + ahead > 3):
                            reduce_max(u + ahead, (q + ahead) % 4, (s + 8) % 16)
                        if s == 1 and not (first and q == 0):
                            normalise(u - 1, 1)
                        if s == 2 and not (first and q == 0):
                            add(u - 1, b if q else b - 1, (q - 1) % 4, 1)
                        if s == 12:
                            normalise(u, 0)
                        if s == 13:
                            add(u, b, q, 0)

            each_batch(dve, body)
            normalise(UNITS - 1, 1)
            add(UNITS - 1, B - 1, 3, 1)


def phase_ffn(nc, gate_w, up_w, down_w, gate_s, up_s, down_s, out, acc, ident):
    with ExitStack() as ctx:
        def sb(name, shape, dt=F32):
            return ctx.enter_context(nc.sbuf_tensor("f_" + name, shape, dt))

        def sem(name):
            return ctx.enter_context(nc.semaphore("f_" + name))

        norm = Norm(ctx, nc, "f_norm", acc)
        last_norm = Norm(ctx, nc, "f_last", acc)
        xT_hi = sb("xT_hi", [P, KT, B * T], F32R)
        xT_lo = sb("xT_lo", [P, KT, B * T], F32R)
        raw_gu = sb("raw_gu", [P, 2, D])
        raw_down = sb("raw_down", [P, KT, P])
        down = sb("down", [P, KT, P])
        gu_hi = sb("gu_hi", [P, 2, D], F32R)
        gu_lo = sb("gu_lo", [P, 2, D], F32R)
        down_hi = sb("down_hi", [P, D], F32R)
        down_lo = sb("down_lo", [P, D], F32R)
        gs_half = sb("gs_half", [P, IC])
        us = sb("us", [P, IC])
        both = sb("both", [P, IC])
        ds = sb("ds", [P, KT])
        half = sb("half", [P, IC])
        now = sb("now", [P, 2])
        h = sb("h", [P, 2, T])
        h_hi = sb("h_hi", [P, 2, T], F32R)
        h_lo = sb("h_lo", [P, 2, T], F32R)
        ps = ctx.enter_context(nc.psum_tensor("f_ps", [P, 8, 512], F32))
        gub = [[ps[:, 0, :], ps[:, 1, :]], [ps[:, 2, :], ps[:, 3, :]]]
        dnb = [ps[:, 4, :], ps[:, 5, :]]
        trb = [ps[:, 6, :], ps[:, 7, :]]

        scales_in = sem("scales_in")
        half_ready = sem("half_ready")
        scales_ready = sem("scales_ready")
        raw_gu_in = sem("raw_gu_in")
        raw_down_in = sem("raw_down_in")
        down_scaled = sem("down_scaled")
        scale_now = sem("scale_now")
        xt_done = sem("xt_done")
        xhi_ready = sem("xhi_ready")
        xlo_ready = sem("xlo_ready")
        guT_done = sem("guT_done")
        downT_done = sem("downT_done")
        gu_hi_ready = sem("gu_hi_ready")
        gu_lo_ready = sem("gu_lo_ready")
        down_hi_ready = sem("down_hi_ready")
        down_lo_ready = sem("down_lo_ready")
        gu_done = sem("gu_done")
        tanh_ready = sem("tanh_ready")
        silu_ready = sem("silu_ready")
        h_ready = sem("h_ready")
        h_hi_ready = sem("h_hi_ready")
        h_lo_ready = sem("h_lo_ready")
        down_done = sem("down_done")
        added = sem("added")
        stored = sem("stored")

        block = ctx.enter_context(nc.Block())

        def each_chunk(eng, body):
            body(0, True, False)
            with eng.Fori(1, IC - 1) as c:
                body(c, False, False)
            body(IC - 1, False, True)

        @block.sync
        def _(sp):
            def load(c):
                for w, m in enumerate((gate_w, up_w)):
                    sp.dma_start(raw_gu[:, w, :], m[bass.ts(c, P), :]).then_inc(raw_gu_in, 16)
                sp.dma_start(raw_down[:, :, :],
                             down_w[:, bass.ts(c, P)].rearrange("(k p) i -> p k i", p=P)).then_inc(raw_down_in, 16)

            load(0)
            sp.dma_start(gs_half[:, :], gate_s.rearrange("(c p) -> p c", p=P), allow_slow_non_contiguous=True).then_inc(scales_in, 16)
            sp.dma_start(us[:, :], up_s.rearrange("(c p) -> p c", p=P), allow_slow_non_contiguous=True).then_inc(scales_in, 16)
            sp.dma_start(ds[:, :], down_s.rearrange("(c p) -> p c", p=P), allow_slow_non_contiguous=True).then_inc(scales_in, 16)
            with sp.Fori(1, IC) as c:
                sp.wait_ge(guT_done, 2 * c)
                sp.wait_ge(down_scaled, c)
                load(c)
            for b in range(B):
                sp.wait_ge(last_norm.done, TT * (b + 1))
                sp.dma_start(out[b].rearrange("(t p) d -> p t d", p=P),
                             acc[:, TT * b:TT * (b + 1), :]).then_inc(stored, 16)
            sp.wait_ge(stored, 16 * B)

        @block.gpsimd
        def _(pool):
            norm.constants()
            last_norm.constants()
            nc.gpsimd.memset(half[:, :], 0.5).then_inc(half_ready, 1)
            for b in range(B):
                norm.inverse_deviation(pool, b)
            pool.wait_ge(half_ready, 1)
            pool.wait_ge(scales_in, 48)
            nc.gpsimd.tensor_tensor(gs_half[:, :], gs_half[:, :], half[:, :], ALU.mult).then_inc(scales_ready, 1)
            pool.wait_ge(scales_ready, 1)
            nc.gpsimd.tensor_tensor(both[:, :], gs_half[:, :], us[:, :], ALU.mult).then_inc(scales_ready, 1)

            def scale_down(c):
                pool.wait_ge(raw_down_in, 16 * (c + 1))
                wait(pool, downT_done, c)
                nc.gpsimd.tensor_tensor(down[:, :, :], raw_down[:, :, :],
                                        ds[:, :].rearrange("p (k o) -> p k o", o=1).broadcast_to([P, KT, P]),
                                        ALU.mult).then_inc(down_scaled, 1)

            def low_h(v, b):
                pool.wait_ge(h_hi_ready, v + 1)
                nc.gpsimd.tensor_tensor(h_lo[:, b % 2, :], h[:, b % 2, :], h_hi[:, b % 2, :].bitcast(F32),
                                        ALU.subtract).then_inc(h_lo_ready, 1)

            scale_down(0)

            def body(c, first, last):
                for b in range(B):
                    low_h(c * B + b, b)
                    if b == 0 and not last:
                        scale_down(c + 1)
                    if last:
                        last_norm.inverse_deviation(pool, b)

            each_chunk(pool, body)

        @block.tensor
        def _(pe):
            def transpose_gu(c):
                pe.wait_ge(raw_gu_in, 32 * (c + 1))
                for w in range(2):
                    if w == 0:
                        wait(pe, down_lo_ready, c)
                    else:
                        wait(pe, gu_lo_ready, 2 * c)
                    for k in range(KT):
                        mm = pe.transpose(trb[w][:, k * P:(k + 1) * P], raw_gu[:, w, k * P:(k + 1) * P], ident[:, :])
                    mm.then_inc(guT_done, 1)

            def transpose_down(c):
                pe.wait_ge(down_scaled, c + 1)
                pe.wait_ge(gu_lo_ready, 2 * c + 1)
                for k in range(KT):
                    mm = pe.transpose(trb[0][:, k * P:(k + 1) * P], down[:, k, :], ident[:, :])
                mm.then_inc(downT_done, 1)

            def gate_up(v, c, b):
                pe.wait_ge(gu_lo_ready, 2 * c + 2)
                wait(pe, h_ready, v - 1)
                for w in range(2):
                    for k in range(KT):
                        mm = mm3(pe, gub[b % 2][w],
                                 (gu_hi[:, w, k * P:(k + 1) * P], gu_lo[:, w, k * P:(k + 1) * P]),
                                 (xT_hi[:, k, b * T:(b + 1) * T], xT_lo[:, k, b * T:(b + 1) * T]), k == 0, k == KT - 1)
                    mm.then_inc(gu_done, 1)

            def project_down(v, c, b):
                pe.wait_ge(down_lo_ready, c + 1)
                pe.wait_ge(h_lo_ready, v + 1)
                for t in range(TT):
                    wait(pe, added, 4 * v + t - 1)
                    s = slice(t * P, (t + 1) * P)
                    mm3(pe, dnb[t % 2], (h_hi[:, b % 2, s], h_lo[:, b % 2, s]), (down_hi[:, :], down_lo[:, :]),
                        True, True).then_inc(down_done, 1)

            transposes = 0
            for b in range(B):
                pe.wait_ge(norm.done, TT * (b + 1))
                for k in range(KT):
                    u = b * KT + k
                    if u >= 6:
                        pe.wait_ge(xlo_ready, u - 5)
                    for t in range(TT):
                        mm = pe.transpose(ps[:, u % 6, t * P:(t + 1) * P], acc[:, TT * b + t, k * P:(k + 1) * P],
                                          ident[:, :])
                    mm.then_inc(xt_done, 1)
            transpose_gu(0)
            transpose_down(0)
            pe.wait_ge(xlo_ready, B * KT)
            gate_up(0, 0, 0)

            def body(c, first, last):
                for b in range(B):
                    v = c * B + b
                    if b == 3 and not last:
                        transpose_down(c + 1)
                    if not (last and b == 3):
                        gate_up(v + 1, c if b < 3 else c + 1, (b + 1) % B)
                    if b == 2 and not last:
                        transpose_gu(c + 1)
                    project_down(v, c, b)

            each_chunk(pe, body)

        @block.scalar
        def _(act):
            def high_gu(c):
                for w in range(2):
                    act.wait_ge(guT_done, 2 * c + w + 1)
                    nc.scalar.copy(gu_hi[:, w, :], trb[w]).then_inc(gu_hi_ready, 1)

            def high_down(c):
                act.wait_ge(downT_done, c + 1)
                wait(act, down_done, 16 * c)
                nc.scalar.copy(down_hi[:, :], trb[0]).then_inc(down_hi_ready, 1)

            def tanh(v, c, b):
                act.wait_ge(gu_done, 2 * v + 1)
                wait(act, h_lo_ready, v - 1)
                wait(act, scale_now, c + 1)
                nc.scalar.activation(h[:, b % 2, :], gub[b % 2][0], ACT.Tanh, scale=now[:, 0:1])\
                    .then_inc(tanh_ready, 1)

            def high_h(v, b):
                act.wait_ge(h_ready, v + 1)
                wait(act, down_done, 4 * (v - 1))
                nc.scalar.copy(h_hi[:, b % 2, :], h[:, b % 2, :]).then_inc(h_hi_ready, 1)

            for u in range(B * KT):
                act.wait_ge(xt_done, u + 1)
                b, k = u // KT, u % KT
                nc.scalar.copy(xT_hi[:, k, b * T:(b + 1) * T], ps[:, u % 6, :]).then_inc(xhi_ready, 1)
            high_gu(0)
            high_down(0)
            tanh(0, 0, 0)
            high_h(0, 0)

            def body(c, first, last):
                for b in range(B):
                    v = c * B + b
                    if not (last and b == 3):
                        tanh(v + 1, c if b < 3 else c + 1, (b + 1) % B)
                    if b == 2 and not last:
                        high_gu(c + 1)
                    if not (last and b == 3):
                        high_h(v + 1, (b + 1) % B)
                    if b == 3 and not last:
                        high_down(c + 1)

            each_chunk(act, body)

        @block.vector
        def _(dve):
            def low_gu(c):
                for w in range(2):
                    dve.wait_ge(gu_hi_ready, 2 * c + w + 1)
                    nc.vector.tensor_tensor(gu_lo[:, w, :], trb[w], gu_hi[:, w, :].bitcast(F32), ALU.subtract)\
                        .then_inc(gu_lo_ready, 1)

            def low_down(c):
                dve.wait_ge(down_hi_ready, c + 1)
                nc.vector.tensor_tensor(down_lo[:, :], trb[0], down_hi[:, :].bitcast(F32), ALU.subtract)\
                    .then_inc(down_lo_ready, 1)

            def inner(v, c, b):
                dve.wait_ge(tanh_ready, v + 1)
                nc.vector.scalar_tensor_tensor(out=h[:, b % 2, :], in0=h[:, b % 2, :], scalar=1.0,
                                               in1=gub[b % 2][0], op0=ALU.add, op1=ALU.mult).then_inc(silu_ready, 1)
                dve.wait_ge(silu_ready, v + 1)
                dve.wait_ge(gu_done, 2 * v + 2)
                nc.vector.scalar_tensor_tensor(out=h[:, b % 2, :], in0=gub[b % 2][1], scalar=now[:, 1:2],
                                               in1=h[:, b % 2, :], op0=ALU.mult, op1=ALU.mult).then_inc(h_ready, 1)

            def take_scales(c):
                nc.vector.tensor_copy(now[:, 0:1], gs_half[:, bass.ds(c, 1)])
                nc.vector.tensor_copy(now[:, 1:2], both[:, bass.ds(c, 1)]).then_inc(scale_now, 1)

            def add_out(v, b):
                for t in range(TT):
                    dve.wait_ge(down_done, 4 * v + t + 1)
                    a = acc[:, TT * b + t, :]
                    nc.vector.tensor_tensor(a, a, dnb[t % 2], ALU.add).then_inc(added, 1)

            for b in range(B):
                norm.statistics(dve, b)
                norm.apply(dve, b)
                for k in range(KT):
                    dve.wait_ge(xhi_ready, b * KT + k + 1)
                    nc.vector.tensor_tensor(xT_lo[:, k, b * T:(b + 1) * T], ps[:, (b * KT + k) % 6, :],
                                            xT_hi[:, k, b * T:(b + 1) * T].bitcast(F32), ALU.subtract)\
                        .then_inc(xlo_ready, 1)
            low_gu(0)
            low_down(0)
            dve.wait_ge(scales_ready, 2)
            take_scales(0)
            inner(0, 0, 0)

            def body(c, first, last):
                for b in range(B):
                    v = c * B + b
                    if b == 3 and not last:
                        take_scales(c + 1)
                    if not (last and b == 3):
                        inner(v + 1, c if b < 3 else c + 1, (b + 1) % B)
                    if b == 2 and not last:
                        low_gu(c + 1)
                    add_out(v, b)
                    if b == 3 and not last:
                        low_down(c + 1)
                    if last:
                        dve.wait_ge(added, 4 * (c * B + b) + 4)
                        last_norm.statistics(dve, b)
                        last_norm.apply(dve, b)

            each_chunk(dve, body)


def decoder_layer(nc, x, ctx_in, Wq, Wk, Wv, Wg, Ws, Wo, gw, gate_w, up_w, down_w, gate_s, up_s, down_s, out):
    with ExitStack() as ctx:
        acc = ctx.enter_context(nc.sbuf_tensor("acc", [P, NTT, D], F32))
        ident = ctx.enter_context(nc.sbuf_tensor("ident", [P, P], F32))
        phase_attention(nc, x, Wq, Wk, Wv, Wg, Ws, Wo, gw, acc, ident)
        phase_cross(nc, ctx_in, acc, ident)
        phase_ffn(nc, gate_w, up_w, down_w, gate_s, up_s, down_s, out, acc, ident)


_INS = ['x', 'ctx_512', 'L0_attn_Wq', 'L0_attn_Wk', 'L0_attn_Wv', 'L0_attn_Wg', 'L0_attn_Ws', 'L0_attn_Wo',
        'L0_attn_g_norm_weight', 'L0_ffn_gate_w', 'L0_ffn_up_w', 'L0_ffn_down_w', 'L0_ffn_gate_s', 'L0_ffn_up_s',
        'L0_ffn_down_s']
_OUTS = [((4, 512, 512), 'float32')]


def kernel(**inputs):
    import numpy as _np
    import concourse.bacc as _bacc
    from concourse import mybir as _mybir
    from concourse.bass_utils import run_bass_kernel_spmd as _run

    nc = _bacc.Bacc("TRN2", target_bir_lowering=False, num_devices=1)
    arrays, args = {}, []
    for name in _INS:
        a = _np.ascontiguousarray(inputs[name])
        arrays[f"in_{name}_dram"] = a
        args.append(nc.dram_tensor(f"in_{name}_dram", a.shape, _mybir.dt.from_np(a.dtype), kind="ExternalInput").ap())
    for i, (shape, dtype) in enumerate(_OUTS):
        dt = _mybir.dt.from_np(_np.dtype(dtype))
        args.append(nc.dram_tensor(f"out_{i}_dram", shape, dt, kind="ExternalOutput").ap())
    decoder_layer(nc, *args)
    r = _run(nc, [arrays], core_ids=[0])
    return r.results[0]["out_0_dram"]
```

```python
import concourse.bass as bass
from concourse import mybir
from contextlib import ExitStack

F32 = mybir.dt.float32
F32R = mybir.dt.float32r
ALU = mybir.AluOpType
ACT = mybir.ActivationFunctionType
AX = mybir.AxisListType

P = 128
B = 4
T = 512
D = 512
KT = D // P
TT = T // P
NTT = B * TT
EPS = 1e-5

PAIRS = 8
DK = 64
DV = 128
NSTEP = PAIRS * B
QK_SCALE = DK ** -0.5
CLAMP = 32.0
PROJ = 7
S, VG, Q, K = 0, 1, 5, 6

CHUNKS = [[(0, 0, 0)], [(1, 0, P)], [(3, P, 2 * P), (2, 0, 2 * P)]]
CHUNK_AT = [0, 512, 896]
CHUNK_LEN = [512, 384, 384]
KEY_AT = [0, 512, 896, 896 + 2 * P]
CAUSAL = 1280

QH = 32
KVH = 8
DH = 16
X_SCALE = DH ** -0.5
ROWS = 64
TILES = 5
MAXROW = 3 * DH
UNITS = B * 4

INTER = 1408
IC = INTER // P


def wait(eng, sem, value):
    if isinstance(value, int) and value <= 0:
        return
    eng.wait_ge(sem, value)


def mm3(pe, out, w, x, start, stop):
    (w_hi, w_lo), (x_hi, x_lo) = w, x
    pe.matmul(out, w_lo, x_hi, start=start, stop=False)
    pe.matmul(out, w_hi, x_lo, start=False, stop=False)
    return pe.matmul(out, w_hi, x_hi, start=False, stop=stop)


class Norm:

    def __init__(self, ctx, nc, name, acc, slots):
        self.nc, self.acc = nc, acc
        self.stats = ctx.enter_context(nc.sbuf_tensor(name + "_stats", [P, slots, TT, 6], F32))
        self.mv = ctx.enter_context(nc.sbuf_tensor(name + "_mv", [P, slots, TT, 2], F32))
        self.rstd = ctx.enter_context(nc.sbuf_tensor(name + "_rstd", [P, slots, TT], F32))
        self.eps = ctx.enter_context(nc.sbuf_tensor(name + "_eps", [P, TT], F32))
        self.minus_half = ctx.enter_context(nc.sbuf_tensor(name + "_minus_half", [P, TT], F32))
        self.const_ready = ctx.enter_context(nc.semaphore(name + "_const"))
        self.stats_ready = ctx.enter_context(nc.semaphore(name + "_stats_ready"))
        self.mv_ready = ctx.enter_context(nc.semaphore(name + "_mv_ready"))
        self.var_ready = ctx.enter_context(nc.semaphore(name + "_var_ready"))
        self.rstd_ready = ctx.enter_context(nc.semaphore(name + "_rstd_ready"))
        self.done = ctx.enter_context(nc.semaphore(name + "_done"))

    def constants(self):
        self.nc.gpsimd.memset(self.eps[:, :], EPS).then_inc(self.const_ready, 1)
        self.nc.gpsimd.memset(self.minus_half[:, :], -0.5).then_inc(self.const_ready, 1)

    def rows(self, b, t):
        return self.acc[:, bass.ds(b * TT + t, 1), :].rearrange("p o d -> p (o d)")

    def statistics(self, b, slot):
        for t in range(TT):
            last = self.nc.vector.bn_stats(self.stats[:, slot, t, :], self.rows(b, t))
        last.then_inc(self.stats_ready, 1)

    def aggregate(self, slot):
        for t in range(TT):
            last = self.nc.vector.bn_aggr(self.mv[:, slot, t, :], self.stats[:, slot, t, :])
        last.then_inc(self.mv_ready, 1)

    def inverse_deviation(self, pool, slot, turn):
        nc = self.nc
        pool.wait_ge(self.mv_ready, turn + 1)
        nc.gpsimd.tensor_tensor(self.rstd[:, slot, :], self.mv[:, slot, :, 1], self.eps[:, :], ALU.add)\
            .then_inc(self.var_ready, 1)
        pool.wait_ge(self.var_ready, turn + 1)
        nc.gpsimd.tensor_tensor(self.rstd[:, slot, :], self.rstd[:, slot, :], self.minus_half[:, :], ALU.pow)\
            .then_inc(self.rstd_ready, 1)

    def apply(self, dve, b, slot, turn):
        dve.wait_ge(self.rstd_ready, turn + 1)
        for t in range(TT):
            a = self.rows(b, t)
            self.nc.vector.tensor_scalar(a, a, self.mv[:, slot, t, 0:1], self.rstd[:, slot, t:t + 1],
                                         ALU.subtract, ALU.mult).then_inc(self.done, 1)


def phase_attention(nc, x, Wq, Wk, Wv, Wg, Ws, Wo, gw, acc, ident, norm):
    with ExitStack() as ctx:
        def sb(name, shape, dt=F32):
            return ctx.enter_context(nc.sbuf_tensor("a_" + name, shape, dt))

        def sem(name):
            return ctx.enter_context(nc.semaphore("a_" + name))

        xT_hi = sb("xT_hi", [P, KT, B * T], F32R)
        xT_lo = sb("xT_lo", [P, KT, B * T], F32R)
        raw_qks = sb("raw_qks", [P, KT, 3, P])
        raw_wo = raw_qks[:, :, :, :].rearrange("p k w c -> p (k w c)")[:, 0:2 * D].rearrange("p (k c) -> p k c", k=2)
        raw_vg = sb("raw_vg", [P, KT, 2, 2 * DV])
        qks_hi = sb("qks_hi", [P, KT, 3, P], F32R)
        qks_lo = sb("qks_lo", [P, KT, 3, P], F32R)
        vg_hi = sb("vg_hi", [P, KT, 4 * DV], F32R)
        vg_lo = sb("vg_lo", [P, KT, 4 * DV], F32R)
        wo_hi = sb("wo_hi", [P, 2, D], F32R)
        wo_lo = sb("wo_lo", [P, 2, D], F32R)
        left = sb("left", [P, 2, T], F32R)
        right_hi = sb("right_hi", [P, 2, T], F32R)
        right_lo = sb("right_lo", [P, 2, T], F32R)
        eT = sb("eT", [P, T])
        e = sb("e", [P, TT, P])
        rz = sb("rz", [P, T])
        v = sb("v", [P, 2, TT, 2 * DV])
        gate = sb("gate", [P, 2, TT, 2 * DV])
        causal = sb("causal", [P, 2, CAUSAL])
        og = sb("og", [P, 2 * TT, DV])
        flat = og[:, :, :].rearrange("p g c -> p (g c)")
        okn = flat[:, 0:T]
        wT = okn
        pv = flat[:, T:2 * T].rearrange("p (g m) -> p g m", m=DK)
        squares = og[:, :, :].bitcast(mybir.dt.bfloat16)
        oT_hi = sb("oT_hi", [P, 2, T], F32R)
        oT_lo = sb("oT_lo", [P, 2, T], F32R)
        mask = sb("mask", [P, 5, P])
        gw_half = sb("gw_half", [P, 1])
        mx = sb("mx", [P, 2 * TT])
        rowsum = sb("rowsum", [P, 2 * TT])
        rs = sb("rs", [P, 2 * TT])
        ss = sb("ss", [P, 2 * TT])
        f1 = sb("f1", [P, 2 * TT])
        f2 = sb("f2", [P, 2 * TT])
        zero = sb("zero", [P, 1, 1])
        eps = sb("eps", [P, 2 * TT])
        minus_half = sb("minus_half", [P, 2 * TT])
        ps = ctx.enter_context(nc.psum_tensor("a_ps", [P, 8, 512], F32))
        pj = [ps[:, 0, :], ps[:, 1, :]]
        ch = [ps[:, 2, :], ps[:, 3, :]]
        tb = ps[:, 4, :]
        okb = ps[:, 5, :]
        ob = [ps[:, 6, :], ps[:, 7, :]]
        HALF = [slice(0, DK), slice(DK, P)]

        x_in = [sem(f"x_in{b}") for b in range(B)]
        gw_in = sem("gw_in")
        gw_ready = sem("gw_ready")
        zeroed = sem("zeroed")
        const_ready = sem("const_ready")
        xt_done = sem("xt_done")
        xhi_ready = sem("xhi_ready")
        xlo_ready = sem("xlo_ready")
        raw_qks_in = sem("raw_qks_in")
        raw_vg_in = sem("raw_vg_in")
        raw_wo_in = sem("raw_wo_in")
        s_hi_ready = sem("s_hi_ready")
        qk_hi_ready = sem("qk_hi_ready")
        vg_hi_ready = sem("vg_hi_ready")
        wo_hi_ready = sem("wo_hi_ready")
        s_ready = sem("s_ready")
        qk_ready = sem("qk_ready")
        vg_ready = sem("vg_ready")
        wo_ready = sem("wo_ready")
        proj_done = sem("proj_done")
        chunk_done = sem("chunk_done")
        oT_done = sem("oT_done")
        wo_done = sem("wo_done")
        okT_done = sem("okT_done")
        ok_done = sem("ok_done")
        pvT_done = sem("pvT_done")
        o_done = sem("o_done")
        e_done = sem("e_done")
        left_hi_ready = sem("left_hi_ready")
        right_hi_ready = sem("right_hi_ready")
        eT_ready = sem("eT_ready")
        v_ready = sem("v_ready")
        tanh_ready = sem("tanh_ready")
        chunk_act = sem("chunk_act")
        oThi_ready = sem("oThi_ready")
        pv_ready = sem("pv_ready")
        sq_done = sem("sq_done")
        e_ready = sem("e_ready")
        left_ready = sem("left_ready")
        right_ready = sem("right_ready")
        clip_done = sem("clip_done")
        gate_ready = sem("gate_ready")
        scan_done = sem("scan_done")
        rz_ready = sem("rz_ready")
        chunk_dve = sem("chunk_dve")
        oTlo_ready = sem("oTlo_ready")
        added = sem("added")
        okn_ready = sem("okn_ready")
        mx_ready = sem("mx_ready")
        sub_ready = sem("sub_ready")
        sum_ready = sem("sum_ready")
        rs_ready = sem("rs_ready")
        wT_ready = sem("wT_ready")
        og_ready = sem("og_ready")
        masked = sem("masked")
        fac = sem("fac")
        ogs_ready = sem("ogs_ready")

        FAC = 5

        def each_pair(eng, step):
            for j in range(B):
                step(j, 0, j, j == 0, False)
            with eng.Fori(1, PAIRS - 1) as p:
                for j in range(B):
                    step(p * B + j, p, j, False, False)
            for j in range(B):
                step((PAIRS - 1) * B + j, PAIRS - 1, j, False, j == B - 1)

        def at(n, k):
            return isinstance(n, int) and n == k

        block = ctx.enter_context(nc.Block())

        def load_projections(sp, p):
            for w, m in enumerate((Ws, Wq, Wk)):
                sp.dma_start(raw_qks[:, :, w, :],
                             m[:, bass.ts(p, P)].rearrange("(k p) c -> p k c", p=P)).then_inc(raw_qks_in, 16)
            for w, m in enumerate((Wv, Wg)):
                sp.dma_start(raw_vg[:, :, w, :],
                             m[:, bass.ts(p, 2 * DV)].rearrange("(k p) c -> p k c", p=P)).then_inc(raw_vg_in, 16)

        def load_output(sp, p):
            sp.wait_ge(qk_ready, p + 1)
            sp.dma_start(raw_wo, Wo[bass.ts(p, 2 * DV), :].rearrange("(k p) c -> p k c", p=P)).then_inc(raw_wo_in, 16)

        @block.sync
        def _(sp):
            for b in range(B):
                sp.dma_start(acc[:, TT * b:TT * (b + 1), :],
                             x[b].rearrange("(t p) d -> p t d", p=P)).then_inc(x_in[b], 16)
                if b == 0:
                    load_projections(sp, 0)
            sp.dma_start(gw_half[:, :], gw.rearrange("(p o) -> p o", o=1)).then_inc(gw_in, 16)
            load_output(sp, 0)
            with sp.Fori(1, PAIRS) as p:
                sp.wait_ge(wo_ready, p)
                sp.wait_ge(vg_ready, p)
                load_projections(sp, p)
                load_output(sp, p)

        @block.gpsimd
        def _(pool):
            nc.gpsimd.memset(ident[:, :], 0.0).then_inc(zeroed, 1)
            nc.gpsimd.memset(mask[:, :, :], 1.0).then_inc(zeroed, 1)
            nc.gpsimd.memset(minus_half[:, :], -0.5).then_inc(zeroed, 1)
            nc.gpsimd.memset(zero[:, :, :], 0.0).then_inc(zeroed, 1)
            nc.gpsimd.memset(eps[:, :], EPS).then_inc(zeroed, 1)
            norm.constants()
            pool.wait_ge(zeroed, 5)
            pool.wait_ge(norm.const_ready, 2)
            nc.gpsimd.affine_select(out=ident[:, :], in_=ident[:, :], compare_op=ALU.not_equal, fill=1.0, base=0,
                                    pattern=[[-1, P]], channel_multiplier=1).then_inc(const_ready, 1)
            for m in (0, 2):
                nc.gpsimd.affine_select(out=mask[:, m, :], in_=mask[:, m, :], compare_op=ALU.is_ge, fill=0.0,
                                        base=0, pattern=[[1, P]], channel_multiplier=-1).then_inc(const_ready, 1)

            def split(raw, hi, lo, hi_ready, ready, k):
                nc.gpsimd.tensor_tensor(hi, raw, zero[:, :, :].broadcast_to(raw.shape), ALU.add).then_inc(hi_ready, 1)
                pool.wait_ge(hi_ready, k)
                nc.gpsimd.tensor_tensor(lo, raw, hi.bitcast(F32), ALU.subtract).then_inc(ready, 1)

            def split_s(p):
                pool.wait_ge(raw_qks_in, (p + 1) * 48)
                split(raw_qks[:, :, 0, :], qks_hi[:, :, 0, :], qks_lo[:, :, 0, :], s_hi_ready, s_ready, p + 1)

            def split_qk(p):
                split(raw_qks[:, :, 1:3, :].rearrange("p k w c -> p k (w c)"),
                      qks_hi[:, :, 1:3, :].rearrange("p k w c -> p k (w c)"),
                      qks_lo[:, :, 1:3, :].rearrange("p k w c -> p k (w c)"), qk_hi_ready, qk_ready, p + 1)

            def split_vg(p):
                pool.wait_ge(raw_vg_in, (p + 1) * 32)
                split(raw_vg[:, :, :, :].rearrange("p k w c -> p k (w c)"), vg_hi[:, :, :], vg_lo[:, :, :],
                      vg_hi_ready, vg_ready, p + 1)

            def split_wo(p):
                pool.wait_ge(raw_wo_in, (p + 1) * 16)
                split(raw_wo, wo_hi[:, :, :], wo_lo[:, :, :], wo_hi_ready, wo_ready, p + 1)

            def mask_diagonals(n, which):
                for h in range(2):
                    wait(pool, chunk_act, 4 * n + 2 * which + h + 1)
                    nc.gpsimd.tensor_tensor(causal[:, h, 0:P], causal[:, h, 0:P], mask[:, 0, :],
                                            ALU.mult).then_inc(masked, 1)

            def factor(n):
                wait(pool, sq_done, 2 * n + 2)
                wait(pool, rs_ready, n + 1)
                nc.gpsimd.tensor_tensor(f1[:, :], rs[:, :], rs[:, :], ALU.mult).then_inc(fac, 1)
                pool.wait_ge(fac, FAC * n + 1)
                nc.gpsimd.tensor_tensor(f2[:, :], f1[:, :], ss[:, :], ALU.mult).then_inc(fac, 1)
                pool.wait_ge(fac, FAC * n + 2)
                nc.gpsimd.tensor_tensor(f1[:, :], f2[:, :], eps[:, :], ALU.add).then_inc(fac, 1)
                pool.wait_ge(fac, FAC * n + 3)
                nc.gpsimd.tensor_tensor(f2[:, :], f1[:, :], minus_half[:, :], ALU.pow).then_inc(fac, 1)
                pool.wait_ge(fac, FAC * n + 4)
                nc.gpsimd.tensor_tensor(f1[:, :], f2[:, :], rs[:, :], ALU.mult).then_inc(fac, 1)

            def scale_o(n):
                wait(pool, fac, FAC * n)
                wait(pool, og_ready, 2 * n)
                nc.gpsimd.tensor_tensor(og[:, :, :], og[:, :, :],
                                        f1[:, :].rearrange("p (g o) -> p g o", o=1).broadcast_to([P, 2 * TT, DV]),
                                        ALU.mult).then_inc(ogs_ready, 1)

            def step(n, p, j, first, last):
                last_pair = at(p, PAIRS - 1)
                mask_diagonals(n, 0)
                if not first:
                    scale_o(n)
                if last_pair and j:
                    norm.inverse_deviation(pool, j - 1, j - 1)
                if j == 3 and not last_pair:
                    pool.wait_ge(proj_done, PROJ * (n + 1))
                    split_qk(p + 1)
                mask_diagonals(n, 1)
                if j == 0 and not at(p, 0):
                    pool.wait_ge(wo_done, 4 * n)
                    split_wo(p)
                if j == 2 and not last_pair:
                    pool.wait_ge(proj_done, PROJ * (n + 1) + Q)
                    split_s(p + 1)
                    split_vg(p + 1)
                factor(n)

            split_s(0)
            split_vg(0)
            split_qk(0)
            pool.wait_ge(gw_in, 16)
            nc.gpsimd.tensor_scalar(gw_half[:, :], gw_half[:, :], 0.5, None, ALU.mult).then_inc(gw_ready, 1)
            split_wo(0)
            each_pair(pool, step)
            scale_o(NSTEP)
            norm.inverse_deviation(pool, B - 1, B - 1)

        @block.tensor
        def _(pe):
            def transpose4(bank, blocks):
                for i, src in enumerate(blocks):
                    last = pe.transpose(bank[:, i * P:(i + 1) * P], src, ident[:, :])
                return last

            def transpose_x(b):
                pe.wait_ge(x_in[b], 16)
                for k in range(KT):
                    wait(pe, xlo_ready, b * KT + k - 1)
                    transpose4(ch[k % 2], [acc[:, TT * b + t, k * P:(k + 1) * P] for t in range(TT)])\
                        .then_inc(xt_done, 1)

            def project(m, i, b, pair):
                bank = pj[(b + i) % 2]
                if i == S:
                    wait(pe, right_ready, 2 * m)
                    pe.wait_ge(s_ready, pair + 1)
                elif i == VG:
                    wait(pe, left_ready, 2 * m)
                    pe.wait_ge(vg_ready, pair + 1)
                elif i == VG + 1:
                    pe.wait_ge(clip_done, m + 1)
                else:
                    pe.wait_ge(gate_ready, 4 * m + i - 2)
                if i == Q:
                    pe.wait_ge(qk_ready, pair + 1)
                for k in range(KT):
                    if i in (S, Q, K):
                        w = (S, Q, K).index(i)
                        mm = mm3(pe, bank, (qks_hi[:, k, w, :], qks_lo[:, k, w, :]),
                                 (xT_hi[:, k, b * T:(b + 1) * T], xT_lo[:, k, b * T:(b + 1) * T]), k == 0, k == KT - 1)
                    else:
                        t = b * T + (i - VG) * P
                        mm = mm3(pe, bank, (xT_hi[:, k, t:t + P], xT_lo[:, k, t:t + P]),
                                 (vg_hi[:, k, :], vg_lo[:, k, :]), k == 0, k == KT - 1)
                mm.then_inc(proj_done, 1)

            def chunks(n, which):
                for c in range(3):
                    for h in range(2):
                        bank = (okb, tb)[h] if c == 1 else ch[h]
                        if c == 0:
                            wait(pe, chunk_dve, 8 * n + 4 * which - 1 + h)
                        elif c == 2:
                            pe.wait_ge(chunk_act, 4 * n + 2 * which + h + 1)
                        for i, col, first in CHUNKS[c]:
                            out = bank[:, col:col + T - first]
                            pe.matmul(out, left[:, h, i * P:(i + 1) * P], right_hi[:, h, first:T],
                                      start=True, stop=False)
                            mm = pe.matmul(out, left[:, h, i * P:(i + 1) * P], right_lo[:, h, first:T],
                                           start=False, stop=True)
                        mm.then_inc(chunk_done, 1)

            def out_rows(n):
                wait(pe, ogs_ready, n)
                for h in range(2):
                    transpose4(ob[h], [og[:, 2 * t + h, :] for t in range(TT)]).then_inc(oT_done, 1)

            def project_out(n, pair):
                pe.wait_ge(wo_ready, pair + 1)
                wait(pe, oTlo_ready, 2 * n)
                for t in range(TT):
                    if t >= 2:
                        wait(pe, added, 4 * (n - 1) + t - 1)
                    for h in range(2):
                        mm = mm3(pe, ob[t % 2], (oT_hi[:, h, t * P:(t + 1) * P], oT_lo[:, h, t * P:(t + 1) * P]),
                                 (wo_hi[:, h, :], wo_lo[:, h, :]), h == 0, h == 1)
                    mm.then_inc(wo_done, 1)

            def slots(n):
                pe.wait_ge(masked, 4 * n + 2)
                pe.wait_ge(chunk_dve, 8 * n + 4)
                for i in range(TT):
                    for h in range(2):
                        mm = pe.matmul(okb[DK * h:DK * (h + 1), i * P:T], e[:, i, DK * h:DK * (h + 1)],
                                       causal[:, h, KEY_AT[i]:KEY_AT[i] + T - i * P],
                                       start=(i == 0), stop=(i == TT - 1))
                mm.then_inc(okT_done, 1)

            def values(n, j):
                pe.wait_ge(masked, 4 * n + 4)
                pe.wait_ge(chunk_dve, 8 * n + 8)
                pe.wait_ge(v_ready, 4 * n + 4)
                wait(pe, added, 4 * n)
                for t in range(TT):
                    for h in range(2):
                        for i in range(t + 1):
                            at = KEY_AT[i] + (t - i) * P
                            c = (2 * (t % 2) + h) * P
                            mm = pe.matmul(ob[t // 2][:, c:c + P], causal[:, h, at:at + P],
                                           v[:, j % 2, i, h * DV:(h + 1) * DV], start=(i == 0), stop=(i == t))
                    if t % 2:
                        mm.then_inc(o_done, 1)

            def transpose_e(m):
                pe.wait_ge(eT_ready, m + 1)
                wait(pe, chunk_dve, 8 * m)
                transpose4(tb, [eT[:, i * P:(i + 1) * P] for i in range(TT)]).then_inc(e_done, 1)

            def step(n, p, j, first, last):
                b1, pair1 = (j + 1) % B, p if j < B - 1 else p + 1

                def next_project(*groups):
                    for i in groups:
                        if not last:
                            project(n + 1, i, b1, pair1)

                pe.wait_ge(left_ready, 2 * (2 * n) + 2)
                pe.wait_ge(right_ready, 2 * (2 * n) + 2)
                pe.wait_ge(e_ready, n + 1)
                chunks(n, 0)
                next_project(S)
                slots(n)
                if not first:
                    out_rows(n)
                next_project(VG)
                pe.wait_ge(okn_ready, n + 1)
                transpose4(tb, [okn[:, t * P:(t + 1) * P] for t in range(TT)]).then_inc(ok_done, 1)
                next_project(VG + 1)
                if at(n, 0) or at(n, 1):
                    transpose_x(n + 2)
                if not first:
                    project_out(n, p if j else p - 1)
                pe.wait_ge(pv_ready, n + 1)
                transpose4(okb, [pv[:, 2 * t:2 * t + 2, :].rearrange("p h m -> p (h m)") for t in range(TT)])\
                    .then_inc(pvT_done, 1)
                next_project(VG + 2, VG + 3)
                pe.wait_ge(left_ready, 2 * (2 * n) + 4)
                pe.wait_ge(right_ready, 2 * (2 * n) + 4)
                if at(n, 0) or at(n, 1):
                    pe.wait_ge(xlo_ready, (n + 3) * KT)
                chunks(n, 1)
                next_project(Q, K)
                if not last:
                    transpose_e(n + 1)
                values(n, j)

            pe.wait_ge(const_ready, 1)
            transpose_x(0)
            pe.wait_ge(xlo_ready, KT)
            for i in range(PROJ):
                project(0, i, 0, 0)
                if i == VG:
                    transpose_x(1)
            transpose_e(0)
            pe.wait_ge(xlo_ready, 2 * KT)
            each_pair(pe, step)
            out_rows(NSTEP)
            project_out(NSTEP, PAIRS - 1)

        @block.scalar
        def _(act):
            def high_x(b):
                for k in range(KT):
                    act.wait_ge(xt_done, b * KT + k + 1)
                    nc.scalar.copy(xT_hi[:, k, b * T:(b + 1) * T], ch[k % 2]).then_inc(xhi_ready, 1)

            def high_left(src):
                for h in range(2):
                    nc.scalar.copy(left[HALF[h], h, :], src[HALF[h], :]).then_inc(left_hi_ready, 1)

            def high_right(src):
                for h in range(2):
                    for half in (h, 1 - h):
                        nc.scalar.copy(right_hi[HALF[half], h, :], src[HALF[h], :]).then_inc(right_hi_ready, 1)

            def copy_proj(m, i, b):
                act.wait_ge(proj_done, PROJ * m + i + 1)
                bank = pj[(b + i) % 2]
                if i == Q:
                    high_right(bank)
                elif i == K:
                    high_left(bank)
                elif i == S:
                    act.wait_ge(clip_done, m + 1)
                    nc.scalar.activation(eT[:, :], eT[:, :], ACT.Exp).then_inc(eT_ready, 1)
                else:
                    nc.scalar.copy(v[:, b % 2, i - VG, :], bank[:, 0:2 * DV]).then_inc(v_ready, 1)
                    wait(act, og_ready, 2 * (m - 1))
                    nc.scalar.activation(gate[:, b % 2, i - VG, :], bank[:, 2 * DV:4 * DV], ACT.Tanh,
                                         scale=0.5).then_inc(tanh_ready, 1)

            def copy_chunk0(n, which):
                for h in range(2):
                    wait(act, chunk_done, 12 * n + 6 * which + h + 1)
                    nc.scalar.copy(causal[:, h, 0:CHUNK_LEN[0]], ch[h]).then_inc(chunk_act, 1)

            def copy_oT(n):
                for h in range(2):
                    wait(act, oT_done, 2 * (n - 1) + h + 1)
                    nc.scalar.activation(oT_hi[:, h, :], ob[h], ACT.Copy,
                                         scale=gw_half[:, 0:1]).then_inc(oThi_ready, 1)

            def copy_e(m):
                act.wait_ge(e_done, m + 1)
                nc.scalar.copy(e[:, :, :].rearrange("p i c -> p (i c)"), tb).then_inc(e_ready, 1)

            def step(n, p, j, first, last):
                b1 = (j + 1) % B

                def next_proj(*groups):
                    for i in groups:
                        if not last:
                            copy_proj(n + 1, i, b1)

                copy_chunk0(n, 0)
                act.wait_ge(chunk_done, 12 * n + 6)
                high_left(eT)
                next_proj(S)
                if not first:
                    copy_oT(n)
                next_proj(VG)
                act.wait_ge(sub_ready, n + 1)
                nc.scalar.activation(pv, pv, ACT.Exp, scale=QK_SCALE).then_inc(pv_ready, 1)
                next_proj(VG + 1)
                if at(n, 0) or at(n, 1):
                    high_x(n + 2)
                act.wait_ge(wT_ready, n + 1)
                high_right(wT)
                next_proj(VG + 2, VG + 3)
                copy_chunk0(n, 1)
                act.wait_ge(chunk_done, 12 * n + 12)
                next_proj(Q, K)
                if not last:
                    copy_e(n + 1)
                for half in range(2):
                    act.wait_ge(o_done, 2 * n + half + 1)
                    for g in range(4):
                        sq = nc.scalar.activation(squares[:, 4 * half + g, 0:DV],
                                                  ob[half][:, g * P:(g + 1) * P], ACT.Square, scale=DV ** -0.5,
                                                  accum_out=ss[:, 4 * half + g:4 * half + g + 1])
                    sq.then_inc(sq_done, 1)

            high_x(0)
            for i in range(PROJ):
                copy_proj(0, i, 0)
                if i == VG:
                    high_x(1)
            copy_e(0)
            act.wait_ge(gw_ready, 1)
            each_pair(act, step)
            copy_oT(NSTEP)

        @block.vector
        def _(dve):
            def low_x(b):
                for k in range(KT):
                    dve.wait_ge(xhi_ready, b * KT + k + 1)
                    nc.vector.tensor_tensor(xT_lo[:, k, b * T:(b + 1) * T], ch[k % 2],
                                            xT_hi[:, k, b * T:(b + 1) * T].bitcast(F32), ALU.subtract)\
                        .then_inc(xlo_ready, 1)

            def low_left(src, turn):
                for h in range(2):
                    dve.wait_ge(left_hi_ready, 2 * turn + h + 1)
                    nc.vector.tensor_tensor(left[HALF[1 - h], h, :], src[HALF[h], :],
                                            left[HALF[h], h, :].bitcast(F32), ALU.subtract).then_inc(left_ready, 1)

            def low_right(src, turn):
                for h in range(2):
                    dve.wait_ge(right_hi_ready, 4 * turn + 2 * h + 2)
                    for half in (h, 1 - h):
                        low = nc.vector.tensor_tensor(right_lo[HALF[half], h, :], src[HALF[h], :],
                                                      right_hi[HALF[h], h, :].bitcast(F32), ALU.subtract)
                    low.then_inc(right_ready, 1)

            def clip(m, b):
                dve.wait_ge(proj_done, PROJ * m + 1)
                nc.vector.tensor_scalar(eT[:, :], pj[b % 2], CLAMP, -CLAMP, ALU.min, ALU.max).then_inc(clip_done, 1)

            def gating(m, i, b):
                dve.wait_ge(tanh_ready, 4 * m + i)
                nc.vector.scalar_tensor_tensor(out=gate[:, b % 2, i - VG, :], in0=gate[:, b % 2, i - VG, :],
                                               scalar=1.0, in1=pj[(b + i) % 2][:, 2 * DV:4 * DV], op0=ALU.add,
                                               op1=ALU.mult).then_inc(gate_ready, 1)

            def inverse_z(m):
                dve.wait_ge(eT_ready, m + 1)
                nc.vector.tensor_tensor_scan(rz[:, :], eT[:, :], eT[:, :], 0.0, ALU.add, ALU.bypass)\
                    .then_inc(scan_done, 1)
                dve.wait_ge(scan_done, m + 1)
                nc.vector.reciprocal(rz[:, 0:T // 2], rz[:, 0:T // 2]).then_inc(rz_ready, 1)

            def inverse_z_rest():
                nc.vector.reciprocal(rz[:, T // 2:T], rz[:, T // 2:T]).then_inc(rz_ready, 1)

            def mask_chunks(n, which):
                for c in (1, 2):
                    for h in range(2):
                        dve.wait_ge(chunk_done, 12 * n + 6 * which + 2 * c + h + 1)
                        m = mask[:, 2:5, :] if c == 1 else mask[:, 0:3, :]
                        bank = (okb, tb)[h] if c == 1 else ch[h]
                        nc.vector.tensor_tensor(causal[:, h, CHUNK_AT[c]:CHUNK_AT[c] + CHUNK_LEN[c]],
                                                bank[:, 0:CHUNK_LEN[c]], m.rearrange("p a t -> p (a t)"),
                                                ALU.mult).then_inc(chunk_dve, 1)

            def low_oT(n):
                for h in range(2):
                    wait(dve, oThi_ready, 2 * (n - 1) + h + 1)
                    nc.vector.scalar_tensor_tensor(out=oT_lo[:, h, :], in0=ob[h],
                                                   scalar=gw_half[:, 0:1], in1=oT_hi[:, h, :].bitcast(F32),
                                                   op0=ALU.mult, op1=ALU.subtract).then_inc(oTlo_ready, 1)

            def add_out(n, b):
                for t in range(TT):
                    wait(dve, wo_done, 4 * (n - 1) + t + 1)
                    a = acc[:, TT * b + t, :]
                    nc.vector.tensor_tensor(a, a, ob[t % 2], ALU.add).then_inc(added, 1)

            def statistics(n, b):
                dve.wait_ge(added, 4 * n)
                norm.statistics(b, b)
                dve.wait_ge(norm.stats_ready, b + 1)
                norm.aggregate(b)

            def step(n, p, j, first, last):
                b1 = (j + 1) % B
                norm_now = at(p, PAIRS - 1) and j > 0
                mask_chunks(n, 0)
                low_left(eT, 2 * n + 1)
                if not last:
                    dve.wait_ge(left_ready, 4 * n + 4)
                    clip(n + 1, b1)
                if not first:
                    low_oT(n)
                dve.wait_ge(okT_done, n + 1)
                dve.wait_ge(rz_ready, 2 * n + 2)
                nc.vector.tensor_tensor(okn, okb, rz[:, :], ALU.mult).then_inc(okn_ready, 1)
                if not last:
                    gating(n + 1, VG, b1)
                dve.wait_ge(ok_done, n + 1)
                scores = tb.rearrange("p (g m) -> p g m", m=DK)
                nc.vector.tensor_reduce(mx[:, :], scores, AX.X, ALU.max).then_inc(mx_ready, 1)
                dve.wait_ge(mx_ready, n + 1)
                nc.vector.tensor_tensor(pv, scores,
                                        mx[:, :].rearrange("p (g o) -> p g o", o=1).broadcast_to([P, 2 * TT, DK]),
                                        ALU.subtract).then_inc(sub_ready, 1)
                if not last:
                    gating(n + 1, VG + 1, b1)
                if at(n, 0) or at(n, 1):
                    low_x(n + 2)
                dve.wait_ge(pv_ready, n + 1)
                nc.vector.tensor_reduce(rowsum[:, :], pv, AX.X, ALU.add).then_inc(sum_ready, 1)
                if not first:
                    add_out(n, (j - 1) % B)
                dve.wait_ge(pvT_done, n + 1)
                nc.vector.tensor_tensor(wT, okb, rz[:, :], ALU.mult).then_inc(wT_ready, 1)
                dve.wait_ge(sum_ready, n + 1)
                nc.vector.reciprocal(rs[:, :], rowsum[:, :]).then_inc(rs_ready, 1)
                dve.wait_ge(wT_ready, n + 1)
                low_right(wT, 2 * n + 1)
                if norm_now:
                    statistics(n, j - 1)
                if not last:
                    gating(n + 1, VG + 2, b1)
                    gating(n + 1, VG + 3, b1)
                mask_chunks(n, 1)
                if norm_now:
                    norm.apply(dve, j - 1, j - 1, j - 1)
                if not last:
                    inverse_z(n + 1)
                    low_right(pj[(b1 + Q) % 2], 2 * n + 2)
                    low_left(pj[(b1 + K) % 2], 2 * n + 2)
                    inverse_z_rest()
                for half in range(2):
                    dve.wait_ge(sq_done, 2 * n + half + 1)
                    nc.vector.tensor_tensor(og[:, 4 * half:4 * half + 4, :].rearrange("p g c -> p (g c)"), ob[half],
                                            gate[:, j % 2, 2 * half:2 * half + 2, :].rearrange("p t c -> p (t c)"),
                                            ALU.mult).then_inc(og_ready, 1)

            low_x(0)
            clip(0, 0)
            for i in range(4):
                gating(0, VG + i, 0)
                if i == 0:
                    low_x(1)
            low_right(pj[Q % 2], 0)
            low_left(pj[K % 2], 0)
            inverse_z(0)
            inverse_z_rest()
            dve.wait_ge(const_ready, 3)
            each_pair(dve, step)
            low_oT(NSTEP)
            add_out(NSTEP, B - 1)
            statistics(NSTEP, B - 1)
            norm.apply(dve, B - 1, B - 1, B - 1)


def phase_cross(nc, ctx_in, acc, ident, norm):
    with ExitStack() as ctx:
        def sb(name, shape, dt=F32):
            return ctx.enter_context(nc.sbuf_tensor("x_" + name, shape, dt))

        def sem(name):
            return ctx.enter_context(nc.semaphore("x_" + name))

        xrows = sb("xrows", [P, 2, TT, P])
        krows = sb("krows", [P, 2, TT, 2 * DH])
        cv = sb("cv", [P, 4, TT, 2, 32])
        xq = sb("xq", [P, 2, TT, 8, ROWS])
        kn = sb("kn", [P, 2, TT, 2, ROWS])
        qs = sb("qs", [P, 4, 4, T], F32R)
        ks = sb("ks", [P, 4, 2, 2, T], F32R)
        prob = sb("prob", [P, 4, 2, T])
        nm = sb("nm", [P, 2, TT, 2, 4])
        mhl = sb("mhl", [P, 2, TT, 2, 2, 4])
        mT = sb("mT", [16, 2, T])
        avs = sb("avs", [P, 2, T])
        rec = sb("rec", [P, 2, TT, 4])
        avn = sb("avn", [P, 2, TT, 4, DH])
        zero = sb("zero", [P, 1])
        ps = ctx.enter_context(nc.psum_tensor("x_ps", [P, 8, 512], F32))
        mxb = [ps[:, 0, :], ps[:, 1, :]]
        exb = [ps[:, 2:4, :], ps[:, 4:6, :]]
        avb = ps[:, 6, :]
        trb = ps[:, 7, :]
        HALF = [slice(0, ROWS), slice(ROWS, P)]

        rows_in = [sem(f"rows_in{i}") for i in range(2)]
        keys_in = [sem(f"keys_in{i}") for i in range(2)]
        cleared = sem("cleared")
        const_ready = sem("const_ready")
        halves_clear = sem("halves_clear")
        values_ready = sem("values_ready")
        ops_hi = sem("ops_hi")
        ops_ready = sem("ops_ready")
        opsT_done = sem("opsT_done")
        opsT_ready = sem("opsT_ready")
        max_done = sem("max_done")
        max_read = sem("max_read")
        mhi_ready = sem("mhi_ready")
        mhl_ready = sem("mhl_ready")
        mT_done = sem("mT_done")
        mT_ready = sem("mT_ready")
        mrow_in = sem("mrow_in")
        score_done = sem("score_done")
        exp_done = sem("exp_done")
        av_done = sem("av_done")
        avs_ready = sem("avs_ready")
        avT_done = sem("avT_done")
        rec_ready = sem("rec_ready")
        avn_ready = sem("avn_ready")
        added = sem("added")

        block = ctx.enter_context(nc.Block())

        def each_batch(eng, body):
            body(0, True, False)
            with eng.Fori(1, B - 1) as b:
                body(b, False, False)
            body(B - 1, False, True)

        @block.sync
        def _(sp):
            def put_max_rows(u, q):
                sp.wait_ge(mT_ready, u + 1)
                for par in range(2):
                    for part in range(2):
                        sp.dma_start(qs[ROWS * par + MAXROW + part:ROWS * par + MAXROW + part + 1, q, :, :].bitcast(F32),
                                     mT[8 * par + 4 * part:8 * par + 4 * part + 4, q % 2, :]).then_inc(mrow_in, 16)

            def get_rows(u, b, q):
                wait(sp, ops_ready, u - 1)
                wait(sp, values_ready, u - 1)
                if not (isinstance(u, int) and u < 3):
                    sp.dma_start(xrows[:, q % 2, :, :], acc[:, bass.ds(b * TT, TT), P * q:P * (q + 1)])\
                        .then_inc(rows_in[q % 2], 16)
                sp.dma_start(krows[:, q % 2, :, :], keys[:, bass.ds(b * TT, TT), 2 * DH * q:2 * DH * (q + 1)])\
                    .then_inc(keys_in[q % 2], 16)

            keys = ctx_in.rearrange("b (t p) d -> p (b t) d", p=P)
            for q in range(4):
                get_rows(q, 0, q)
            put_max_rows(0, 0)

            def body(b, first, last):
                for q in range(4):
                    if not (last and q == 3):
                        put_max_rows(b * 4 + q + 1, (q + 1) % 4)
                    if not last:
                        get_rows(b * 4 + q + 4, b + 1, q)

            each_batch(sp, body)

        @block.gpsimd
        def _(pool):
            nc.gpsimd.memset(zero[:, :], 0.0).then_inc(cleared, 1)
            for buf in range(2):
                nc.gpsimd.memset(xq[:, buf, :, :, MAXROW:ROWS].rearrange("p t h r -> p (t h) r"), 0.0).then_inc(cleared, 1)
                nc.gpsimd.memset(kn[:, buf, :, :, MAXROW + 2:ROWS].rearrange("p t g r -> p (t g) r"), 0.0)\
                    .then_inc(cleared, 1)
                nc.gpsimd.memset(kn[:, buf, :, :, MAXROW:MAXROW + 2].rearrange("p t g r -> p (t g) r"), 1.0)\
                    .then_inc(cleared, 1)
            pool.wait_ge(cleared, 7)

            def plus_zero(out, in_):
                z = zero[:, :]
                for _ in range(len(in_.shape) - 2):
                    z = z.rearrange("p (o z) -> p o z", o=1) if len(z.shape) == 2 else \
                        z.rearrange("p a (o z) -> p a o z", o=1)
                return nc.gpsimd.tensor_tensor(out, in_, z.broadcast_to(in_.shape), ALU.add)

            def rounded(out, in_):
                return plus_zero(out.bitcast(F32R), in_)

            def operands(u, b, q):
                wait(pool, opsT_done, TILES * (u - 1))
                pool.wait_ge(keys_in[q % 2], 16 * (2 * b + q // 2 + 1))
                if isinstance(u, int) and u < 3:
                    rows = acc[:, 0:TT, P * q:P * (q + 1)]
                else:
                    pool.wait_ge(rows_in[q % 2], 16 * (2 * b + q // 2 + 1 - (2 - q % 2)))
                    rows = xrows[:, q % 2]
                rows = rows.rearrange("p t (h c) -> p t h c", c=DH)
                x = xq[:, q % 2]
                keys = krows[:, q % 2].rearrange("p t (h c) -> p t h c", c=DH)
                k = kn[:, q % 2]
                rounded(x[:, :, :, 0:DH], rows)
                rounded(x[:, :, :, DH:2 * DH], rows)
                rounded(k[:, :, :, 0:DH], keys)
                rounded(k[:, :, :, 2 * DH:3 * DH], keys).then_inc(ops_hi, 1)
                pool.wait_ge(ops_hi, u + 1)
                nc.gpsimd.tensor_tensor(x[:, :, :, 2 * DH:3 * DH].bitcast(F32R), rows, x[:, :, :, 0:DH], ALU.subtract)
                nc.gpsimd.tensor_tensor(k[:, :, :, DH:2 * DH].bitcast(F32R), keys, k[:, :, :, 0:DH], ALU.subtract)\
                    .then_inc(ops_ready, 1)
                wait(pool, av_done, 8 * (u - 3))
                plus_zero(cv[:, q, :, :, 0:DH], keys).then_inc(values_ready, 1)

            def split_max(u, q):
                pool.wait_ge(max_read, 32 * (u + 1))
                wait(pool, mT_done, u - 1)
                m = mhl[:, q % 2]
                rounded(m[:, :, :, 0, :], nm[:, q % 2]).then_inc(mhi_ready, 1)
                pool.wait_ge(mhi_ready, u + 1)
                nc.gpsimd.tensor_tensor(m[:, :, :, 1, :].bitcast(F32R), nm[:, q % 2], m[:, :, :, 0, :], ALU.subtract)\
                    .then_inc(mhl_ready, 1)

            for q in range(3):
                if q == 1:
                    nc.gpsimd.memset(cv[:, :, :, :, DH + 1:32].rearrange("p q t g c -> p (q t g) c"), 0.0)\
                        .then_inc(const_ready, 1)
                    nc.gpsimd.memset(cv[:, :, :, :, DH:DH + 1].rearrange("p q t g c -> p (q t g) c"), 1.0)\
                        .then_inc(const_ready, 1)
                operands(q, 0, q)
            split_max(0, 0)

            def body(b, first, last):
                for q in range(4):
                    u = b * 4 + q
                    if not (last and q == 3):
                        split_max(u + 1, (q + 1) % 4)
                    if not (last and q >= 1):
                        operands(u + 3, b if q == 0 else b + 1, (q + 3) % 4)
                    if q == 0 and not first:
                        norm.inverse_deviation(pool, 0, B + b - 1)

            each_batch(pool, body)
            norm.inverse_deviation(pool, 0, 2 * B - 1)

        @block.tensor
        def _(pe):
            def transpose_operands(u, q, i):
                if i == 0:
                    pe.wait_ge(ops_ready, u + 1)
                for t in range(TT):
                    src = kn[:, q % 2, t, :, :] if i == 0 else xq[:, q % 2, t, 2 * (i - 1):2 * i, :]
                    src = src.rearrange("p h r -> p (h r)")
                    mm = pe.transpose(trb[:, t * P:(t + 1) * P], src, ident[:, :])
                mm.then_inc(opsT_done, 1)

            def max_scores(u, q, i, par):
                tile, st = i // 4, i % 4
                if st == 0 and par == 0:
                    pe.wait_ge(opsT_ready, TILES * u + tile + 2)
                wait(pe, max_read, 32 * u + 2 * i + par - 1)
                pe.matmul(mxb[par], qs[:, q, tile, st * P:(st + 1) * P], ks[:, q, tile // 2, par, :],
                          start=True, stop=True).then_inc(max_done, 1)

            def transpose_max(u, q):
                pe.wait_ge(mhl_ready, u + 1)
                for t in range(TT):
                    mm = pe.transpose(trb[0:16, t * P:(t + 1) * P],
                                      mhl[:, q % 2, t].rearrange("p a b c -> p (a b c)"), ident[:, :])
                mm.then_inc(mT_done, 1)

            def scores(u, q, s):
                g, t, pair = s // 8, s // 2 % 4, s % 2
                if s == 0:
                    pe.wait_ge(mrow_in, 64 * (u + 1))
                wait(pe, exp_done, 16 * u + s - 1)
                for par in range(2):
                    mm = pe.matmul(exb[s % 2][:, par, :], ks[:, q, g, par, t * P:(t + 1) * P],
                                   qs[:, q, 2 * g + pair, :], start=True, stop=True)
                mm.then_inc(score_done, 1)

            def weighted(u, q, s):
                g, t = s // 8, s // 2 % 4
                pe.wait_ge(exp_done, 16 * u + s + 2)
                if s == 0:
                    pe.wait_ge(values_ready, u + 1)
                if s % 8 == 0:
                    wait(pe, avs_ready, 2 * u + g)
                for i in range(4):
                    mm = pe.matmul(avb[32 * i:32 * (i + 1), :], cv[:, q, t, g, :], prob[:, (s + i // 2) % 4, i % 2, :],
                                   start=(t == 0), stop=(t == TT - 1))
                mm.then_inc(av_done, 1)

            def transpose_weighted(u, g):
                pe.wait_ge(avs_ready, 2 * u + g + 1)
                for t in range(TT):
                    mm = pe.transpose(trb[:, t * P:(t + 1) * P], avs[:, g, t * P:(t + 1) * P], ident[:, :])
                mm.then_inc(avT_done, 1)

            for u in range(2):
                for i in range(TILES):
                    wait(pe, opsT_ready, TILES * u + i)
                    transpose_operands(u, u, i)
                pe.wait_ge(halves_clear, 2 * u + 2)
                for i in range(16 if u == 0 else 8):
                    for par in range(2):
                        max_scores(u, u, i, par)
            pe.wait_ge(const_ready, 2)
            pe.wait_ge(opsT_ready, 2 * TILES)
            transpose_max(0, 0)

            def body(b, first, last):
                for q in range(4):
                    u = b * 4 + q
                    for s in range(16):
                        ahead = 1 if s < 8 else 2
                        if not (last and q + ahead > 3):
                            max_scores(u + ahead, (q + ahead) % 4, (s + 8) % 16, 0)
                        scores(u, q, s)
                        if not (last and q + ahead > 3):
                            max_scores(u + ahead, (q + ahead) % 4, (s + 8) % 16, 1)
                        if s % 2 and s > 1:
                            weighted(u, q, s - 3)
                        elif s == 1 and not (first and q == 0):
                            weighted(u - 1, (q - 1) % 4, 14)
                        if s == 3 and not (first and q == 0):
                            wait(pe, avn_ready, 2 * u - 1)
                            wait(pe, mT_ready, u + 1)
                            transpose_weighted(u - 1, 1)
                        if 5 <= s < 5 + TILES and not (last and q > 1):
                            if s == 5:
                                wait(pe, avn_ready, 2 * u)
                                wait(pe, mT_ready, u + 1)
                            else:
                                pe.wait_ge(opsT_ready, TILES * (u + 2) + s - 5)
                            transpose_operands(u + 2, (q + 2) % 4, s - 5)
                        if s == 10 and not (last and q == 3):
                            if last and q > 1:
                                wait(pe, avn_ready, 2 * u)
                            else:
                                pe.wait_ge(opsT_ready, TILES * (u + 3))
                            transpose_max(u + 1, (q + 1) % 4)
                        if s == 13:
                            if last and q == 3:
                                wait(pe, avn_ready, 2 * u)
                            else:
                                pe.wait_ge(mT_ready, u + 2)
                            transpose_weighted(u, 0)

            each_batch(pe, body)
            weighted(UNITS - 1, 3, 14)
            pe.wait_ge(avn_ready, 2 * UNITS - 1)
            transpose_weighted(UNITS - 1, 1)

        @block.scalar
        def _(act):
            def copy_operand(u, q, i):
                act.wait_ge(opsT_done, TILES * u + i + 1)
                if i == 0:
                    for g in range(2):
                        for c in range(2):
                            last = nc.scalar.copy(ks[HALF[c], q, g, c, :], trb[HALF[g], :])
                else:
                    last = nc.scalar.copy(qs[:, q, i - 1, :], trb)
                last.then_inc(opsT_ready, 1)

            def copy_max(u, q):
                act.wait_ge(mT_done, u + 1)
                wait(act, mrow_in, 64 * (u - 1))
                nc.scalar.copy(mT[:, q % 2, :], trb[0:16, :]).then_inc(mT_ready, 1)

            def copy_weighted(u, g):
                act.wait_ge(av_done, 8 * u + 4 * g + 4)
                wait(act, avT_done, 2 * u + g - 1)
                nc.scalar.copy(avs[:, g, :], avb).then_inc(avs_ready, 1)

            for u in range(2):
                for i in range(TILES):
                    copy_operand(u, u, i)
            copy_max(0, 0)

            def body(b, first, last):
                for q in range(4):
                    u = b * 4 + q
                    for s in range(16):
                        act.wait_ge(score_done, 16 * u + s + 1)
                        if s % 2 == 0:
                            wait(act, av_done, 8 * u + s // 2 - 1)
                        nc.scalar.activation(prob[:, s % 4, :, :], exb[s % 2], ACT.Exp, scale=X_SCALE)\
                            .then_inc(exp_done, 1)
                        if s == 2 and not (first and q == 0):
                            copy_weighted(u - 1, 1)
                        if 5 <= s < 5 + TILES and not (last and q > 1):
                            copy_operand(u + 2, (q + 2) % 4, s - 5)
                        if s == 10:
                            copy_weighted(u, 0)
                        if s == 10 and not (last and q == 3):
                            copy_max(u + 1, (q + 1) % 4)

            each_batch(act, body)
            copy_weighted(UNITS - 1, 1)

        @block.vector
        def _(dve):
            def reduce_max(u, q, i):
                if i == 0:
                    wait(dve, mhl_ready, u - 1)
                for par in range(2):
                    dve.wait_ge(max_done, 32 * u + 2 * i + par + 1)
                    nc.vector.tensor_reduce(nm[:, q % 2, i % 4, par, i // 4:i // 4 + 1], mxb[par], AX.X, ALU.max,
                                            negate=True).then_inc(max_read, 1)

            def normalise(u, g):
                dve.wait_ge(avT_done, 2 * u + g + 1)
                rows = trb.rearrange("p (t h c) -> p t h c", t=TT, h=4)
                nc.vector.reciprocal(rec[:, g, :, :], rows[:, :, :, DH]).then_inc(rec_ready, 1)
                dve.wait_ge(rec_ready, 2 * u + g + 1)
                nc.vector.tensor_tensor(avn[:, g], rows[:, :, :, 0:DH],
                                        rec[:, g].rearrange("p t (h o) -> p t h o", o=1).broadcast_to([P, TT, 4, DH]),
                                        ALU.mult).then_inc(avn_ready, 1)

            def add(u, b, q, g):
                dve.wait_ge(avn_ready, 2 * u + g + 1)
                a = acc[:, bass.ds(b * TT, TT), P * q + 64 * g:P * q + 64 * (g + 1)]
                nc.vector.tensor_tensor(a, a, avn[:, g].rearrange("p t h c -> p t (h c)"), ALU.add).then_inc(added, 1)

            for units in (slice(0, 1), slice(1, 4)):
                for c in range(2):
                    nc.vector.memset(ks[HALF[1 - c], units, :, c, :].bitcast(F32), 0.0).then_inc(halves_clear, 1)
            for i in range(24):
                reduce_max(i // 16, i // 16, i % 16)

            def body(b, first, last):
                for q in range(4):
                    u = b * 4 + q
                    for s in range(16):
                        ahead = 1 if s < 8 else 2
                        norm_now = q == 0 and not first
                        if norm_now and s == 6:
                            dve.wait_ge(added, 2 * u)
                        if norm_now and s == 7:
                            dve.wait_ge(norm.stats_ready, B + b)
                        if not (last and q + ahead > 3):
                            reduce_max(u + ahead, (q + ahead) % 4, (s + 8) % 16)
                        if s == 4 and not (first and q == 0):
                            normalise(u - 1, 1)
                        if s == 5 and not (first and q == 0):
                            add(u - 1, b if q else b - 1, (q - 1) % 4, 1)
                        if norm_now and s == 6:
                            norm.statistics(b - 1, 0)
                        if norm_now and s == 7:
                            norm.aggregate(0)
                        if norm_now and s == 10:
                            norm.apply(dve, b - 1, 0, B + b - 1)
                        if s == 13:
                            normalise(u, 0)
                        if s == 14:
                            add(u, b, q, 0)

            each_batch(dve, body)
            normalise(UNITS - 1, 1)
            add(UNITS - 1, B - 1, 3, 1)
            dve.wait_ge(added, 2 * UNITS)
            norm.statistics(B - 1, 0)
            dve.wait_ge(norm.stats_ready, 2 * B)
            norm.aggregate(0)
            norm.apply(dve, B - 1, 0, 2 * B - 1)


def phase_ffn(nc, gate_w, up_w, down_w, gate_s, up_s, down_s, out, acc, ident, norm):
    with ExitStack() as ctx:
        def sb(name, shape, dt=F32):
            return ctx.enter_context(nc.sbuf_tensor("f_" + name, shape, dt))

        def sem(name):
            return ctx.enter_context(nc.semaphore("f_" + name))

        xT_hi = sb("xT_hi", [P, KT, B * T], F32R)
        xT_lo = sb("xT_lo", [P, KT, B * T], F32R)
        raw_gu = sb("raw_gu", [P, 2, D])
        raw_down = sb("raw_down", [P, KT, P])
        down = sb("down", [P, KT, P])
        gu_hi = sb("gu_hi", [P, 2, D], F32R)
        gu_lo = sb("gu_lo", [P, 2, D], F32R)
        down_hi = sb("down_hi", [P, D], F32R)
        down_lo = sb("down_lo", [P, D], F32R)
        gs_half = sb("gs_half", [P, IC])
        us = sb("us", [P, IC])
        both = sb("both", [P, IC])
        ds = sb("ds", [P, KT])
        half = sb("half", [P, IC])
        now = sb("now", [P, 2])
        h = sb("h", [P, 2, T])
        h_hi = sb("h_hi", [P, 2, T], F32R)
        h_lo = sb("h_lo", [P, 2, T], F32R)
        ps = ctx.enter_context(nc.psum_tensor("f_ps", [P, 8, 512], F32))
        gub = [[ps[:, 0, :], ps[:, 1, :]], [ps[:, 2, :], ps[:, 3, :]]]
        dnb = [ps[:, 4, :], ps[:, 5, :]]
        trb = [ps[:, 6, :], ps[:, 7, :]]

        scales_in = sem("scales_in")
        half_ready = sem("half_ready")
        scales_ready = sem("scales_ready")
        raw_gu_in = sem("raw_gu_in")
        raw_down_in = sem("raw_down_in")
        down_scaled = sem("down_scaled")
        scale_now = sem("scale_now")
        xt_done = sem("xt_done")
        xhi_ready = sem("xhi_ready")
        xlo_ready = sem("xlo_ready")
        guT_done = sem("guT_done")
        downT_done = sem("downT_done")
        gu_hi_ready = sem("gu_hi_ready")
        gu_lo_ready = sem("gu_lo_ready")
        down_hi_ready = sem("down_hi_ready")
        down_lo_ready = sem("down_lo_ready")
        gu_done = sem("gu_done")
        tanh_ready = sem("tanh_ready")
        silu_ready = sem("silu_ready")
        h_ready = sem("h_ready")
        h_hi_ready = sem("h_hi_ready")
        h_lo_ready = sem("h_lo_ready")
        down_done = sem("down_done")
        added = sem("added")
        stored = sem("stored")

        block = ctx.enter_context(nc.Block())

        def each_chunk(eng, body):
            body(0, True, False)
            with eng.Fori(1, IC - 1) as c:
                body(c, False, False)
            body(IC - 1, False, True)

        @block.sync
        def _(sp):
            def load(c):
                for w, m in enumerate((gate_w, up_w)):
                    sp.dma_start(raw_gu[:, w, :], m[bass.ts(c, P), :]).then_inc(raw_gu_in, 16)
                sp.dma_start(raw_down[:, :, :],
                             down_w[:, bass.ts(c, P)].rearrange("(k p) i -> p k i", p=P)).then_inc(raw_down_in, 16)

            load(0)
            sp.dma_start(gs_half[:, :], gate_s.rearrange("(c p) -> p c", p=P), allow_slow_non_contiguous=True).then_inc(scales_in, 16)
            sp.dma_start(us[:, :], up_s.rearrange("(c p) -> p c", p=P), allow_slow_non_contiguous=True).then_inc(scales_in, 16)
            sp.dma_start(ds[:, :], down_s.rearrange("(c p) -> p c", p=P), allow_slow_non_contiguous=True).then_inc(scales_in, 16)
            with sp.Fori(1, IC) as c:
                sp.wait_ge(guT_done, 2 * c)
                sp.wait_ge(down_scaled, c)
                load(c)
            for b in range(B):
                sp.wait_ge(norm.done, TT * (2 * B + b + 1))
                sp.dma_start(out[b].rearrange("(t p) d -> p t d", p=P),
                             acc[:, TT * b:TT * (b + 1), :]).then_inc(stored, 16)
            sp.wait_ge(stored, 16 * B)

        @block.gpsimd
        def _(pool):
            nc.gpsimd.memset(half[:, :], 0.5).then_inc(half_ready, 1)
            pool.wait_ge(half_ready, 1)
            pool.wait_ge(scales_in, 48)
            nc.gpsimd.tensor_tensor(gs_half[:, :], gs_half[:, :], half[:, :], ALU.mult).then_inc(scales_ready, 1)
            pool.wait_ge(scales_ready, 1)
            nc.gpsimd.tensor_tensor(both[:, :], gs_half[:, :], us[:, :], ALU.mult).then_inc(scales_ready, 1)

            def scale_down(c):
                pool.wait_ge(raw_down_in, 16 * (c + 1))
                wait(pool, downT_done, c)
                nc.gpsimd.tensor_tensor(down[:, :, :], raw_down[:, :, :],
                                        ds[:, :].rearrange("p (k o) -> p k o", o=1).broadcast_to([P, KT, P]),
                                        ALU.mult).then_inc(down_scaled, 1)

            def low_h(v, b):
                pool.wait_ge(h_hi_ready, v + 1)
                nc.gpsimd.tensor_tensor(h_lo[:, b % 2, :], h[:, b % 2, :], h_hi[:, b % 2, :].bitcast(F32),
                                        ALU.subtract).then_inc(h_lo_ready, 1)

            scale_down(0)

            def body(c, first, last):
                for b in range(B):
                    low_h(c * B + b, b)
                    if b == 0 and not last:
                        scale_down(c + 1)
                    if last:
                        norm.inverse_deviation(pool, b, 2 * B + b)

            each_chunk(pool, body)

        @block.tensor
        def _(pe):
            def transpose_gu(c):
                pe.wait_ge(raw_gu_in, 32 * (c + 1))
                for w in range(2):
                    if w == 0:
                        wait(pe, down_lo_ready, c)
                    else:
                        wait(pe, gu_lo_ready, 2 * c)
                    for k in range(KT):
                        mm = pe.transpose(trb[w][:, k * P:(k + 1) * P], raw_gu[:, w, k * P:(k + 1) * P], ident[:, :])
                    mm.then_inc(guT_done, 1)

            def transpose_down(c):
                pe.wait_ge(down_scaled, c + 1)
                pe.wait_ge(gu_lo_ready, 2 * c + 1)
                for k in range(KT):
                    mm = pe.transpose(trb[0][:, k * P:(k + 1) * P], down[:, k, :], ident[:, :])
                mm.then_inc(downT_done, 1)

            def gate_up(v, c, b):
                pe.wait_ge(gu_lo_ready, 2 * c + 2)
                wait(pe, h_ready, v - 1)
                for w in range(2):
                    for k in range(KT):
                        mm = mm3(pe, gub[b % 2][w],
                                 (gu_hi[:, w, k * P:(k + 1) * P], gu_lo[:, w, k * P:(k + 1) * P]),
                                 (xT_hi[:, k, b * T:(b + 1) * T], xT_lo[:, k, b * T:(b + 1) * T]), k == 0, k == KT - 1)
                    mm.then_inc(gu_done, 1)

            def project_down(v, c, b):
                pe.wait_ge(down_lo_ready, c + 1)
                pe.wait_ge(h_lo_ready, v + 1)
                for t in range(TT):
                    wait(pe, added, 4 * v + t - 1)
                    s = slice(t * P, (t + 1) * P)
                    mm3(pe, dnb[t % 2], (h_hi[:, b % 2, s], h_lo[:, b % 2, s]), (down_hi[:, :], down_lo[:, :]),
                        True, True).then_inc(down_done, 1)

            def transpose_x(b):
                for k in range(KT):
                    u = b * KT + k
                    if u == KT:
                        pe.wait_ge(down_lo_ready, 1)
                    wait(pe, xlo_ready, u - 1)
                    for t in range(TT):
                        mm = pe.transpose(trb[k % 2][:, t * P:(t + 1) * P], acc[:, TT * b + t, k * P:(k + 1) * P],
                                          ident[:, :])
                    mm.then_inc(xt_done, 1)

            transpose_x(0)
            pe.wait_ge(xlo_ready, KT)
            transpose_gu(0)
            transpose_down(0)
            gate_up(0, 0, 0)

            def body(c, first, last):
                for b in range(B):
                    v = c * B + b
                    if first and b < B - 1:
                        transpose_x(b + 1)
                        pe.wait_ge(xlo_ready, (b + 2) * KT)
                    if b == 3 and not last:
                        transpose_down(c + 1)
                    if not (last and b == 3):
                        gate_up(v + 1, c if b < 3 else c + 1, (b + 1) % B)
                    if b == 2 and not last:
                        transpose_gu(c + 1)
                    project_down(v, c, b)

            each_chunk(pe, body)

        @block.scalar
        def _(act):
            def high_gu(c):
                for w in range(2):
                    act.wait_ge(guT_done, 2 * c + w + 1)
                    nc.scalar.copy(gu_hi[:, w, :], trb[w]).then_inc(gu_hi_ready, 1)

            def high_down(c):
                act.wait_ge(downT_done, c + 1)
                wait(act, down_done, 16 * c)
                nc.scalar.copy(down_hi[:, :], trb[0]).then_inc(down_hi_ready, 1)

            def tanh(v, c, b):
                act.wait_ge(gu_done, 2 * v + 1)
                wait(act, h_lo_ready, v - 1)
                wait(act, scale_now, c + 1)
                nc.scalar.activation(h[:, b % 2, :], gub[b % 2][0], ACT.Tanh, scale=now[:, 0:1])\
                    .then_inc(tanh_ready, 1)

            def high_h(v, b):
                act.wait_ge(h_ready, v + 1)
                wait(act, down_done, 4 * (v - 1))
                nc.scalar.copy(h_hi[:, b % 2, :], h[:, b % 2, :]).then_inc(h_hi_ready, 1)

            def high_x(b):
                for k in range(KT):
                    act.wait_ge(xt_done, b * KT + k + 1)
                    nc.scalar.copy(xT_hi[:, k, b * T:(b + 1) * T], trb[k % 2]).then_inc(xhi_ready, 1)

            high_x(0)
            high_gu(0)
            high_down(0)
            tanh(0, 0, 0)
            high_h(0, 0)

            def body(c, first, last):
                for b in range(B):
                    v = c * B + b
                    if first and b < B - 1:
                        high_x(b + 1)
                    if not (last and b == 3):
                        tanh(v + 1, c if b < 3 else c + 1, (b + 1) % B)
                    if b == 2 and not last:
                        high_gu(c + 1)
                    if not (last and b == 3):
                        high_h(v + 1, (b + 1) % B)
                    if b == 3 and not last:
                        high_down(c + 1)

            each_chunk(act, body)

        @block.vector
        def _(dve):
            def low_gu(c):
                for w in range(2):
                    dve.wait_ge(gu_hi_ready, 2 * c + w + 1)
                    nc.vector.tensor_tensor(gu_lo[:, w, :], trb[w], gu_hi[:, w, :].bitcast(F32), ALU.subtract)\
                        .then_inc(gu_lo_ready, 1)

            def low_down(c):
                dve.wait_ge(down_hi_ready, c + 1)
                nc.vector.tensor_tensor(down_lo[:, :], trb[0], down_hi[:, :].bitcast(F32), ALU.subtract)\
                    .then_inc(down_lo_ready, 1)

            def inner(v, c, b):
                dve.wait_ge(tanh_ready, v + 1)
                nc.vector.scalar_tensor_tensor(out=h[:, b % 2, :], in0=h[:, b % 2, :], scalar=1.0,
                                               in1=gub[b % 2][0], op0=ALU.add, op1=ALU.mult).then_inc(silu_ready, 1)
                dve.wait_ge(silu_ready, v + 1)
                dve.wait_ge(gu_done, 2 * v + 2)
                nc.vector.scalar_tensor_tensor(out=h[:, b % 2, :], in0=gub[b % 2][1], scalar=now[:, 1:2],
                                               in1=h[:, b % 2, :], op0=ALU.mult, op1=ALU.mult).then_inc(h_ready, 1)

            def take_scales(c):
                nc.vector.tensor_copy(now[:, 0:1], gs_half[:, bass.ds(c, 1)])
                nc.vector.tensor_copy(now[:, 1:2], both[:, bass.ds(c, 1)]).then_inc(scale_now, 1)

            def add_out(v, b):
                for t in range(TT):
                    dve.wait_ge(down_done, 4 * v + t + 1)
                    a = acc[:, TT * b + t, :]
                    nc.vector.tensor_tensor(a, a, dnb[t % 2], ALU.add).then_inc(added, 1)

            def low_x(b):
                for k in range(KT):
                    dve.wait_ge(xhi_ready, b * KT + k + 1)
                    nc.vector.tensor_tensor(xT_lo[:, k, b * T:(b + 1) * T], trb[k % 2],
                                            xT_hi[:, k, b * T:(b + 1) * T].bitcast(F32), ALU.subtract)\
                        .then_inc(xlo_ready, 1)

            low_x(0)
            low_gu(0)
            low_down(0)
            dve.wait_ge(scales_ready, 2)
            take_scales(0)
            inner(0, 0, 0)

            def body(c, first, last):
                for b in range(B):
                    v = c * B + b
                    if first and b < B - 1:
                        low_x(b + 1)
                    if b == 3 and not last:
                        take_scales(c + 1)
                    if not (last and b == 3):
                        inner(v + 1, c if b < 3 else c + 1, (b + 1) % B)
                    if b == 2 and not last:
                        low_gu(c + 1)
                    add_out(v, b)
                    if b == 3 and not last:
                        low_down(c + 1)
                    if last:
                        dve.wait_ge(added, 4 * (c * B + b) + 4)
                        norm.statistics(b, b)
                        dve.wait_ge(norm.stats_ready, 2 * B + b + 1)
                        norm.aggregate(b)
                        norm.apply(dve, b, b, 2 * B + b)

            each_chunk(dve, body)


def decoder_layer(nc, x, ctx_in, Wq, Wk, Wv, Wg, Ws, Wo, gw, gate_w, up_w, down_w, gate_s, up_s, down_s, out):
    with ExitStack() as ctx:
        acc = ctx.enter_context(nc.sbuf_tensor("acc", [P, NTT, D], F32))
        ident = ctx.enter_context(nc.sbuf_tensor("ident", [P, P], F32))
        norm = Norm(ctx, nc, "norm", acc, B)
        phase_attention(nc, x, Wq, Wk, Wv, Wg, Ws, Wo, gw, acc, ident, norm)
        phase_cross(nc, ctx_in, acc, ident, norm)
        phase_ffn(nc, gate_w, up_w, down_w, gate_s, up_s, down_s, out, acc, ident, norm)


_INS = ['x', 'ctx_512', 'L0_attn_Wq', 'L0_attn_Wk', 'L0_attn_Wv', 'L0_attn_Wg', 'L0_attn_Ws', 'L0_attn_Wo',
        'L0_attn_g_norm_weight', 'L0_ffn_gate_w', 'L0_ffn_up_w', 'L0_ffn_down_w', 'L0_ffn_gate_s', 'L0_ffn_up_s',
        'L0_ffn_down_s']
_OUTS = [((4, 512, 512), 'float32')]


def kernel(**inputs):
    import numpy as _np
    import concourse.bacc as _bacc
    from concourse import mybir as _mybir
    from concourse.bass_utils import run_bass_kernel_spmd as _run

    nc = _bacc.Bacc("TRN2", target_bir_lowering=False, num_devices=1)
    arrays, args = {}, []
    for name in _INS:
        a = _np.ascontiguousarray(inputs[name])
        arrays[f"in_{name}_dram"] = a
        args.append(nc.dram_tensor(f"in_{name}_dram", a.shape, _mybir.dt.from_np(a.dtype), kind="ExternalInput").ap())
    for i, (shape, dtype) in enumerate(_OUTS):
        dt = _mybir.dt.from_np(_np.dtype(dtype))
        args.append(nc.dram_tensor(f"out_{i}_dram", shape, dt, kind="ExternalOutput").ap())
    decoder_layer(nc, *args)
    r = _run(nc, [arrays], core_ids=[0])
    return r.results[0]["out_0_dram"]
```

```python
import concourse.bass as bass
from concourse import mybir
from contextlib import ExitStack

F32 = mybir.dt.float32
F32R = mybir.dt.float32r
ALU = mybir.AluOpType
ACT = mybir.ActivationFunctionType
AX = mybir.AxisListType

P = 128
B = 4
T = 512
D = 512
KT = D // P
TT = T // P
NTT = B * TT
EPS = 1e-5

PAIRS = 8
DK = 64
DV = 128
NSTEP = PAIRS * B
QK_SCALE = DK ** -0.5
CLAMP = 32.0
PROJ = 7
S, VG, Q, K = 0, 1, 5, 6

CHUNKS = [[(0, 0, 0)], [(1, 0, P)], [(3, P, 2 * P), (2, 0, 2 * P)]]
CHUNK_AT = [0, 512, 896]
CHUNK_LEN = [512, 384, 384]
KEY_AT = [0, 512, 896, 896 + 2 * P]
CAUSAL = 1280

QH = 32
KVH = 8
DH = 16
X_SCALE = DH ** -0.5
ROWS = 64
TILES = 5
MAXROW = 3 * DH
UNITS = B * 4

INTER = 1408
IC = INTER // P


def wait(eng, sem, value):
    if isinstance(value, int) and value <= 0:
        return
    eng.wait_ge(sem, value)


def mm3(pe, out, w, x, start, stop):
    (w_hi, w_lo), (x_hi, x_lo) = w, x
    pe.matmul(out, w_lo, x_hi, start=start, stop=False)
    pe.matmul(out, w_hi, x_lo, start=False, stop=False)
    return pe.matmul(out, w_hi, x_hi, start=False, stop=stop)


class Norm:

    def __init__(self, ctx, nc, name, acc, slots):
        self.nc, self.acc = nc, acc
        self.stats = ctx.enter_context(nc.sbuf_tensor(name + "_stats", [P, slots, TT, 6], F32))
        self.mv = ctx.enter_context(nc.sbuf_tensor(name + "_mv", [P, slots, TT, 2], F32))
        self.rstd = ctx.enter_context(nc.sbuf_tensor(name + "_rstd", [P, slots, TT], F32))
        self.eps = ctx.enter_context(nc.sbuf_tensor(name + "_eps", [P, TT], F32))
        self.minus_half = ctx.enter_context(nc.sbuf_tensor(name + "_minus_half", [P, TT], F32))
        self.const_ready = ctx.enter_context(nc.semaphore(name + "_const"))
        self.stats_ready = ctx.enter_context(nc.semaphore(name + "_stats_ready"))
        self.mv_ready = ctx.enter_context(nc.semaphore(name + "_mv_ready"))
        self.var_ready = ctx.enter_context(nc.semaphore(name + "_var_ready"))
        self.rstd_ready = ctx.enter_context(nc.semaphore(name + "_rstd_ready"))
        self.done = ctx.enter_context(nc.semaphore(name + "_done"))

    def constants(self):
        self.nc.gpsimd.memset(self.eps[:, :], EPS).then_inc(self.const_ready, 1)
        self.nc.gpsimd.memset(self.minus_half[:, :], -0.5).then_inc(self.const_ready, 1)

    def rows(self, b, t):
        return self.acc[:, bass.ds(b * TT + t, 1), :].rearrange("p o d -> p (o d)")

    def statistics(self, b, slot, tiles=range(TT)):
        for t in tiles:
            done = self.nc.vector.bn_stats(self.stats[:, slot, t, :], self.rows(b, t))
            if t == TT - 1:
                done.then_inc(self.stats_ready, 1)

    def aggregate(self, slot):
        for t in range(TT):
            last = self.nc.vector.bn_aggr(self.mv[:, slot, t, :], self.stats[:, slot, t, :])
        last.then_inc(self.mv_ready, 1)

    def inverse_deviation(self, pool, slot, turn):
        nc = self.nc
        pool.wait_ge(self.mv_ready, turn + 1)
        nc.gpsimd.tensor_tensor(self.rstd[:, slot, :], self.mv[:, slot, :, 1], self.eps[:, :], ALU.add)\
            .then_inc(self.var_ready, 1)
        pool.wait_ge(self.var_ready, turn + 1)
        nc.gpsimd.tensor_tensor(self.rstd[:, slot, :], self.rstd[:, slot, :], self.minus_half[:, :], ALU.pow)\
            .then_inc(self.rstd_ready, 1)

    def apply(self, dve, b, slot, turn, tiles=range(TT)):
        if 0 in tiles:
            dve.wait_ge(self.rstd_ready, turn + 1)
        for t in tiles:
            a = self.rows(b, t)
            self.nc.vector.tensor_scalar(a, a, self.mv[:, slot, t, 0:1], self.rstd[:, slot, t:t + 1],
                                         ALU.subtract, ALU.mult).then_inc(self.done, 1)


def phase_attention(nc, x, Wq, Wk, Wv, Wg, Ws, Wo, gw, acc, ident, norm):
    with ExitStack() as ctx:
        def sb(name, shape, dt=F32):
            return ctx.enter_context(nc.sbuf_tensor("a_" + name, shape, dt))

        def sem(name):
            return ctx.enter_context(nc.semaphore("a_" + name))

        xT_hi = sb("xT_hi", [P, KT, B * T], F32R)
        xT_lo = sb("xT_lo", [P, KT, B * T], F32R)
        raw_qks = sb("raw_qks", [P, KT, 3, P])
        raw_wo = raw_qks[:, :, :, :].rearrange("p k w c -> p (k w c)")[:, 0:2 * D].rearrange("p (k c) -> p k c", k=2)
        raw_vg = sb("raw_vg", [P, KT, 2, 2 * DV])
        vg_raw = raw_vg[:, :, :, :].rearrange("p k w c -> p k (w c)")
        qks_hi = sb("qks_hi", [P, KT, 3, P], F32R)
        qks_lo = sb("qks_lo", [P, KT, 3, P], F32R)
        vg_hi = sb("vg_hi", [P, KT, 4 * DV], F32R)
        vg_lo = sb("vg_lo", [P, KT, 4 * DV], F32R)
        wo_hi = sb("wo_hi", [P, 2, D], F32R)
        wo_lo = sb("wo_lo", [P, 2, D], F32R)
        left = sb("left", [P, 2, T], F32R)
        right_hi = sb("right_hi", [P, 2, T], F32R)
        right_lo = sb("right_lo", [P, 2, T], F32R)
        eT = sb("eT", [P, T])
        e = sb("e", [P, TT, P])
        rz = sb("rz", [P, T])
        v = sb("v", [P, 2, TT, 2 * DV])
        gate = sb("gate", [P, 2, TT, 2 * DV])
        causal = sb("causal", [P, 2, CAUSAL])
        og = sb("og", [P, 2 * TT, DV])
        flat = og[:, :, :].rearrange("p g c -> p (g c)")
        okn = flat[:, 0:T]
        wT = okn
        pv = flat[:, T:2 * T].rearrange("p (g m) -> p g m", m=DK)
        squares = og[:, :, :].bitcast(mybir.dt.bfloat16)
        oT_hi = sb("oT_hi", [P, 2, T], F32R)
        oT_lo = sb("oT_lo", [P, 2, T], F32R)
        mask = sb("mask", [P, 5, P])
        gw_half = sb("gw_half", [P, 1])
        mx = sb("mx", [P, 2 * TT])
        rowsum = sb("rowsum", [P, 2 * TT])
        rs = sb("rs", [P, 2 * TT])
        ss = sb("ss", [P, 2 * TT])
        f1 = sb("f1", [P, 2 * TT])
        f2 = sb("f2", [P, 2 * TT])
        zero = sb("zero", [P, 1, 1])
        eps = sb("eps", [P, 2 * TT])
        minus_half = sb("minus_half", [P, 2 * TT])
        ps = ctx.enter_context(nc.psum_tensor("a_ps", [P, 8, 512], F32))
        pj = [ps[:, 0, :], ps[:, 1, :]]
        ch = [ps[:, 2, :], ps[:, 3, :]]
        tb = ps[:, 4, :]
        okb = ps[:, 5, :]
        ob = [ps[:, 6, :], ps[:, 7, :]]
        HALF = [slice(0, DK), slice(DK, P)]

        def x_bank(b, k):
            return (ch + ob)[k] if b == 0 else ch[k % 2]

        first_x_in = [sem(f"first_x_in{half}") for half in range(2)]
        x_in = [sem(f"x_in{b}") for b in range(B)]
        gw_in = sem("gw_in")
        gw_ready = sem("gw_ready")
        zeroed = sem("zeroed")
        const_ready = sem("const_ready")
        xt_done = sem("xt_done")
        xhi_ready = sem("xhi_ready")
        xlo_ready = sem("xlo_ready")
        raw_s_in = sem("raw_s_in")
        raw_qk_in = sem("raw_qk_in")
        raw_vg_in = sem("raw_vg_in")
        raw_wo_in = sem("raw_wo_in")
        s_hi_ready = sem("s_hi_ready")
        qk_hi_ready = sem("qk_hi_ready")
        vg_hi_ready = sem("vg_hi_ready")
        wo_hi_ready = sem("wo_hi_ready")
        s_ready = sem("s_ready")
        qk_ready = sem("qk_ready")
        vg_ready = sem("vg_ready")
        wo_ready = sem("wo_ready")
        proj_done = sem("proj_done")
        chunk_done = sem("chunk_done")
        oT_done = sem("oT_done")
        wo_done = sem("wo_done")
        okT_done = sem("okT_done")
        ok_done = sem("ok_done")
        pvT_done = sem("pvT_done")
        o_done = sem("o_done")
        e_done = sem("e_done")
        left_hi_ready = sem("left_hi_ready")
        right_hi_ready = sem("right_hi_ready")
        eT_ready = sem("eT_ready")
        v_ready = sem("v_ready")
        tanh_ready = sem("tanh_ready")
        chunk_act = sem("chunk_act")
        oThi_ready = sem("oThi_ready")
        pv_ready = sem("pv_ready")
        sq_done = sem("sq_done")
        e_ready = sem("e_ready")
        left_ready = sem("left_ready")
        right_ready = sem("right_ready")
        clip_done = sem("clip_done")
        gate_ready = sem("gate_ready")
        scan_done = sem("scan_done")
        rz_ready = sem("rz_ready")
        chunk_dve = sem("chunk_dve")
        oTlo_ready = sem("oTlo_ready")
        added = sem("added")
        okn_ready = sem("okn_ready")
        mx_ready = sem("mx_ready")
        sub_ready = sem("sub_ready")
        sum_ready = sem("sum_ready")
        rs_ready = sem("rs_ready")
        wT_ready = sem("wT_ready")
        og_ready = sem("og_ready")
        masked = sem("masked")
        fac = sem("fac")
        ogs_ready = sem("ogs_ready")

        FAC = 5

        def each_pair(eng, step):
            for j in range(B):
                step(j, 0, j, j == 0, False)
            with eng.Fori(1, PAIRS - 1) as p:
                for j in range(B):
                    step(p * B + j, p, j, False, False)
            for j in range(B):
                step((PAIRS - 1) * B + j, PAIRS - 1, j, False, j == B - 1)

        def at(n, k):
            return isinstance(n, int) and n == k

        block = ctx.enter_context(nc.Block())

        def load_s(sp, p):
            sp.dma_start(raw_qks[:, :, 0, :],
                         Ws[:, bass.ts(p, P)].rearrange("(k p) c -> p k c", p=P)).then_inc(raw_s_in, 16)

        def load_vgqk(sp, p):
            for w, m in enumerate((Wv, Wg)):
                sp.dma_start(raw_vg[:, :, w, :],
                             m[:, bass.ts(p, 2 * DV)].rearrange("(k p) c -> p k c", p=P)).then_inc(raw_vg_in, 16)
            for w, m in enumerate((Wq, Wk)):
                sp.dma_start(raw_qks[:, :, 1 + w, :],
                             m[:, bass.ts(p, P)].rearrange("(k p) c -> p k c", p=P)).then_inc(raw_qk_in, 16)

        def load_output(sp, p):
            sp.wait_ge(qk_ready, p + 1)
            sp.dma_start(raw_wo, Wo[bass.ts(p, 2 * DV), :].rearrange("(k p) c -> p k c", p=P)).then_inc(raw_wo_in, 16)

        @block.sync
        def _(sp):
            load_s(sp, 0)
            for half in range(2):
                sp.dma_start(acc[:, 2 * half:2 * half + 2, :],
                             x[0, 2 * P * half:2 * P * (half + 1)].rearrange("(t p) d -> p t d", p=P))\
                    .then_inc(first_x_in[half], 16)
            load_vgqk(sp, 0)
            for b in range(1, B):
                sp.dma_start(acc[:, TT * b:TT * (b + 1), :],
                             x[b].rearrange("(t p) d -> p t d", p=P)).then_inc(x_in[b], 16)
            sp.dma_start(gw_half[:, :], gw.rearrange("(p o) -> p o", o=1)).then_inc(gw_in, 16)
            load_output(sp, 0)
            with sp.Fori(1, PAIRS) as p:
                sp.wait_ge(wo_ready, p)
                sp.wait_ge(vg_ready, p)
                load_s(sp, p)
                load_vgqk(sp, p)
                load_output(sp, p)

        @block.gpsimd
        def _(pool):
            nc.gpsimd.memset(ident[:, :], 0.0).then_inc(zeroed, 1)
            nc.gpsimd.memset(mask[:, :, :], 1.0).then_inc(zeroed, 1)
            nc.gpsimd.memset(minus_half[:, :], -0.5).then_inc(zeroed, 1)
            nc.gpsimd.memset(zero[:, :, :], 0.0).then_inc(zeroed, 1)
            nc.gpsimd.memset(eps[:, :], EPS).then_inc(zeroed, 1)
            norm.constants()
            pool.wait_ge(zeroed, 5)
            pool.wait_ge(norm.const_ready, 2)
            nc.gpsimd.affine_select(out=ident[:, :], in_=ident[:, :], compare_op=ALU.not_equal, fill=1.0, base=0,
                                    pattern=[[-1, P]], channel_multiplier=1).then_inc(const_ready, 1)
            for m in (0, 2):
                nc.gpsimd.affine_select(out=mask[:, m, :], in_=mask[:, m, :], compare_op=ALU.is_ge, fill=0.0,
                                        base=0, pattern=[[1, P]], channel_multiplier=-1).then_inc(const_ready, 1)

            def split(raw, hi, lo, hi_ready, ready, k):
                nc.gpsimd.tensor_tensor(hi, raw, zero[:, :, :].broadcast_to(raw.shape), ALU.add).then_inc(hi_ready, 1)
                pool.wait_ge(hi_ready, k)
                nc.gpsimd.tensor_tensor(lo, raw, hi.bitcast(F32), ALU.subtract).then_inc(ready, 1)

            def split_s(p):
                pool.wait_ge(raw_s_in, (p + 1) * 16)
                split(raw_qks[:, :, 0, :], qks_hi[:, :, 0, :], qks_lo[:, :, 0, :], s_hi_ready, s_ready, p + 1)

            def split_qk(p):
                pool.wait_ge(raw_qk_in, (p + 1) * 32)
                split(raw_qks[:, :, 1:3, :].rearrange("p k w c -> p k (w c)"),
                      qks_hi[:, :, 1:3, :].rearrange("p k w c -> p k (w c)"),
                      qks_lo[:, :, 1:3, :].rearrange("p k w c -> p k (w c)"), qk_hi_ready, qk_ready, p + 1)

            def split_vg(p):
                pool.wait_ge(raw_vg_in, (p + 1) * 32)
                split(vg_raw, vg_hi[:, :, :], vg_lo[:, :, :],
                      vg_hi_ready, vg_ready, p + 1)

            def split_wo(p):
                pool.wait_ge(raw_wo_in, (p + 1) * 16)
                split(raw_wo, wo_hi[:, :, :], wo_lo[:, :, :], wo_hi_ready, wo_ready, p + 1)

            def mask_diagonals(n, which):
                for h in range(2):
                    wait(pool, chunk_act, 4 * n + 2 * which + h + 1)
                    nc.gpsimd.tensor_tensor(causal[:, h, 0:P], causal[:, h, 0:P], mask[:, 0, :],
                                            ALU.mult).then_inc(masked, 1)

            def factor(n):
                wait(pool, sq_done, 2 * n + 2)
                wait(pool, rs_ready, n + 1)
                nc.gpsimd.tensor_tensor(f1[:, :], rs[:, :], rs[:, :], ALU.mult).then_inc(fac, 1)
                pool.wait_ge(fac, FAC * n + 1)
                nc.gpsimd.tensor_tensor(f2[:, :], f1[:, :], ss[:, :], ALU.mult).then_inc(fac, 1)
                pool.wait_ge(fac, FAC * n + 2)
                nc.gpsimd.tensor_tensor(f1[:, :], f2[:, :], eps[:, :], ALU.add).then_inc(fac, 1)
                pool.wait_ge(fac, FAC * n + 3)
                nc.gpsimd.tensor_tensor(f2[:, :], f1[:, :], minus_half[:, :], ALU.pow).then_inc(fac, 1)
                pool.wait_ge(fac, FAC * n + 4)
                nc.gpsimd.tensor_tensor(f1[:, :], f2[:, :], rs[:, :], ALU.mult).then_inc(fac, 1)

            def scale_o(n):
                wait(pool, fac, FAC * n)
                wait(pool, og_ready, 2 * n)
                nc.gpsimd.tensor_tensor(og[:, :, :], og[:, :, :],
                                        f1[:, :].rearrange("p (g o) -> p g o", o=1).broadcast_to([P, 2 * TT, DV]),
                                        ALU.mult).then_inc(ogs_ready, 1)

            def step(n, p, j, first, last):
                last_pair = at(p, PAIRS - 1)
                mask_diagonals(n, 0)
                if not first:
                    scale_o(n)
                if last_pair and j:
                    norm.inverse_deviation(pool, j - 1, j - 1)
                if j == 3 and not last_pair:
                    pool.wait_ge(proj_done, PROJ * (n + 1))
                    split_qk(p + 1)
                mask_diagonals(n, 1)
                if j == 0 and not at(p, 0):
                    pool.wait_ge(wo_done, 4 * n)
                    split_wo(p)
                if j == 2 and not last_pair:
                    pool.wait_ge(proj_done, PROJ * (n + 1) + Q)
                    split_s(p + 1)
                    split_vg(p + 1)
                factor(n)

            split_s(0)
            pool.wait_ge(raw_vg_in, 32)
            nc.gpsimd.tensor_tensor(vg_hi[:, :, :], vg_raw, zero[:, :, :].broadcast_to(vg_raw.shape), ALU.add)\
                .then_inc(vg_hi_ready, 1)
            split_qk(0)
            pool.wait_ge(gw_in, 16)
            nc.gpsimd.tensor_scalar(gw_half[:, :], gw_half[:, :], 0.5, None, ALU.mult).then_inc(gw_ready, 1)
            split_wo(0)
            each_pair(pool, step)
            scale_o(NSTEP)

        @block.tensor
        def _(pe):
            def transpose4(bank, blocks):
                for i, src in enumerate(blocks):
                    last = pe.transpose(bank[:, i * P:(i + 1) * P], src, ident[:, :])
                return last

            def transpose_x(b):
                pe.wait_ge(x_in[b], 16)
                for k in range(KT):
                    wait(pe, xlo_ready, b * KT + k - 1)
                    transpose4(ch[k % 2], [acc[:, TT * b + t, k * P:(k + 1) * P] for t in range(TT)])\
                        .then_inc(xt_done, 1)

            def project(m, i, b, pair):
                bank = pj[(b + i) % 2]
                if i == S:
                    wait(pe, right_ready, 2 * m)
                    pe.wait_ge(s_ready, pair + 1)
                elif i == VG:
                    wait(pe, left_ready, 2 * m)
                    pe.wait_ge(vg_ready, pair + 1)
                elif i == VG + 1:
                    pe.wait_ge(clip_done, m + 1)
                else:
                    pe.wait_ge(gate_ready, 4 * m + i - 2)
                if i == Q:
                    pe.wait_ge(qk_ready, pair + 1)
                for k in range(KT):
                    if i in (S, Q, K):
                        w = (S, Q, K).index(i)
                        mm = mm3(pe, bank, (qks_hi[:, k, w, :], qks_lo[:, k, w, :]),
                                 (xT_hi[:, k, b * T:(b + 1) * T], xT_lo[:, k, b * T:(b + 1) * T]), k == 0, k == KT - 1)
                    else:
                        t = b * T + (i - VG) * P
                        mm = mm3(pe, bank, (xT_hi[:, k, t:t + P], xT_lo[:, k, t:t + P]),
                                 (vg_hi[:, k, :], vg_lo[:, k, :]), k == 0, k == KT - 1)
                mm.then_inc(proj_done, 1)

            def chunks(n, which):
                for c in range(3):
                    for h in range(2):
                        bank = (okb, tb)[h] if c == 1 else ch[h]
                        if c == 0:
                            wait(pe, chunk_dve, 8 * n + 4 * which - 1 + h)
                        elif c == 2:
                            pe.wait_ge(chunk_act, 4 * n + 2 * which + h + 1)
                        for i, col, first in CHUNKS[c]:
                            out = bank[:, col:col + T - first]
                            pe.matmul(out, left[:, h, i * P:(i + 1) * P], right_hi[:, h, first:T],
                                      start=True, stop=False)
                            mm = pe.matmul(out, left[:, h, i * P:(i + 1) * P], right_lo[:, h, first:T],
                                           start=False, stop=True)
                        mm.then_inc(chunk_done, 1)

            def out_rows(n):
                wait(pe, ogs_ready, n)
                for h in range(2):
                    transpose4(ob[h], [og[:, 2 * t + h, :] for t in range(TT)]).then_inc(oT_done, 1)

            def project_out(n, pair):
                pe.wait_ge(wo_ready, pair + 1)
                wait(pe, oTlo_ready, 2 * n)
                for t in range(TT):
                    if t >= 2:
                        wait(pe, added, 4 * (n - 1) + t - 1)
                    for h in range(2):
                        mm = mm3(pe, ob[t % 2], (oT_hi[:, h, t * P:(t + 1) * P], oT_lo[:, h, t * P:(t + 1) * P]),
                                 (wo_hi[:, h, :], wo_lo[:, h, :]), h == 0, h == 1)
                    mm.then_inc(wo_done, 1)

            def slots(n):
                pe.wait_ge(masked, 4 * n + 2)
                pe.wait_ge(chunk_dve, 8 * n + 4)
                for i in range(TT):
                    for h in range(2):
                        mm = pe.matmul(okb[DK * h:DK * (h + 1), i * P:T], e[:, i, DK * h:DK * (h + 1)],
                                       causal[:, h, KEY_AT[i]:KEY_AT[i] + T - i * P],
                                       start=(i == 0), stop=(i == TT - 1))
                mm.then_inc(okT_done, 1)

            def values(n, j):
                pe.wait_ge(masked, 4 * n + 4)
                pe.wait_ge(chunk_dve, 8 * n + 8)
                pe.wait_ge(v_ready, 4 * n + 4)
                wait(pe, added, 4 * n)
                for t in range(TT):
                    for h in range(2):
                        for i in range(t + 1):
                            at = KEY_AT[i] + (t - i) * P
                            c = (2 * (t % 2) + h) * P
                            mm = pe.matmul(ob[t // 2][:, c:c + P], causal[:, h, at:at + P],
                                           v[:, j % 2, i, h * DV:(h + 1) * DV], start=(i == 0), stop=(i == t))
                    if t % 2:
                        mm.then_inc(o_done, 1)

            def transpose_e(m):
                pe.wait_ge(eT_ready, m + 1)
                wait(pe, chunk_dve, 8 * m)
                transpose4(tb, [eT[:, i * P:(i + 1) * P] for i in range(TT)]).then_inc(e_done, 1)

            def step(n, p, j, first, last):
                b1, pair1 = (j + 1) % B, p if j < B - 1 else p + 1

                def next_project(*groups):
                    for i in groups:
                        if not last:
                            project(n + 1, i, b1, pair1)

                pe.wait_ge(left_ready, 2 * (2 * n) + 2)
                pe.wait_ge(right_ready, 2 * (2 * n) + 2)
                pe.wait_ge(e_ready, n + 1)
                chunks(n, 0)
                next_project(S)
                slots(n)
                if not first:
                    out_rows(n)
                next_project(VG)
                pe.wait_ge(okn_ready, n + 1)
                transpose4(tb, [okn[:, t * P:(t + 1) * P] for t in range(TT)]).then_inc(ok_done, 1)
                next_project(VG + 1)
                if at(n, 0) or at(n, 1):
                    transpose_x(n + 2)
                if not first:
                    project_out(n, p if j else p - 1)
                pe.wait_ge(pv_ready, n + 1)
                transpose4(okb, [pv[:, 2 * t:2 * t + 2, :].rearrange("p h m -> p (h m)") for t in range(TT)])\
                    .then_inc(pvT_done, 1)
                next_project(VG + 2, VG + 3)
                pe.wait_ge(left_ready, 2 * (2 * n) + 4)
                pe.wait_ge(right_ready, 2 * (2 * n) + 4)
                if at(n, 0) or at(n, 1):
                    pe.wait_ge(xlo_ready, (n + 3) * KT)
                chunks(n, 1)
                next_project(Q, K)
                if not last:
                    transpose_e(n + 1)
                values(n, j)

            pe.wait_ge(const_ready, 1)
            for half in range(2):
                pe.wait_ge(first_x_in[half], 16)
                for k in range(KT):
                    for t in (2 * half, 2 * half + 1):
                        mm = pe.transpose(x_bank(0, k)[:, t * P:(t + 1) * P], acc[:, t, k * P:(k + 1) * P], ident[:, :])
                    if half:
                        mm.then_inc(xt_done, 1)
            pe.wait_ge(xlo_ready, KT)
            for i in range(PROJ):
                project(0, i, 0, 0)
                if i == VG:
                    transpose_x(1)
            transpose_e(0)
            pe.wait_ge(xlo_ready, 2 * KT)
            each_pair(pe, step)
            out_rows(NSTEP)
            project_out(NSTEP, PAIRS - 1)

        @block.scalar
        def _(act):
            def high_x(b):
                for k in range(KT):
                    act.wait_ge(xt_done, b * KT + k + 1)
                    nc.scalar.copy(xT_hi[:, k, b * T:(b + 1) * T], x_bank(b, k)).then_inc(xhi_ready, 1)

            def high_left(src):
                for h in range(2):
                    nc.scalar.copy(left[HALF[h], h, :], src[HALF[h], :]).then_inc(left_hi_ready, 1)

            def high_right(src):
                for h in range(2):
                    for half in (h, 1 - h):
                        nc.scalar.copy(right_hi[HALF[half], h, :], src[HALF[h], :]).then_inc(right_hi_ready, 1)

            def copy_proj(m, i, b):
                act.wait_ge(proj_done, PROJ * m + i + 1)
                bank = pj[(b + i) % 2]
                if i == Q:
                    high_right(bank)
                elif i == K:
                    high_left(bank)
                elif i == S:
                    act.wait_ge(clip_done, m + 1)
                    nc.scalar.activation(eT[:, :], eT[:, :], ACT.Exp).then_inc(eT_ready, 1)
                else:
                    nc.scalar.copy(v[:, b % 2, i - VG, :], bank[:, 0:2 * DV]).then_inc(v_ready, 1)
                    wait(act, og_ready, 2 * (m - 1))
                    nc.scalar.activation(gate[:, b % 2, i - VG, :], bank[:, 2 * DV:4 * DV], ACT.Tanh,
                                         scale=0.5).then_inc(tanh_ready, 1)

            def copy_chunk0(n, which):
                for h in range(2):
                    wait(act, chunk_done, 12 * n + 6 * which + h + 1)
                    nc.scalar.copy(causal[:, h, 0:CHUNK_LEN[0]], ch[h]).then_inc(chunk_act, 1)

            def copy_oT(n):
                for h in range(2):
                    wait(act, oT_done, 2 * (n - 1) + h + 1)
                    nc.scalar.activation(oT_hi[:, h, :], ob[h], ACT.Copy,
                                         scale=gw_half[:, 0:1]).then_inc(oThi_ready, 1)

            def copy_e(m):
                act.wait_ge(e_done, m + 1)
                nc.scalar.copy(e[:, :, :].rearrange("p i c -> p (i c)"), tb).then_inc(e_ready, 1)

            def step(n, p, j, first, last):
                b1 = (j + 1) % B

                def next_proj(*groups):
                    for i in groups:
                        if not last:
                            copy_proj(n + 1, i, b1)

                copy_chunk0(n, 0)
                act.wait_ge(chunk_done, 12 * n + 6)
                high_left(eT)
                next_proj(S)
                if not first:
                    copy_oT(n)
                next_proj(VG)
                act.wait_ge(sub_ready, n + 1)
                nc.scalar.activation(pv, pv, ACT.Exp, scale=QK_SCALE).then_inc(pv_ready, 1)
                next_proj(VG + 1)
                if at(n, 0) or at(n, 1):
                    high_x(n + 2)
                act.wait_ge(wT_ready, n + 1)
                high_right(wT)
                next_proj(VG + 2, VG + 3)
                copy_chunk0(n, 1)
                act.wait_ge(chunk_done, 12 * n + 12)
                next_proj(Q, K)
                if not last:
                    copy_e(n + 1)
                for half in range(2):
                    act.wait_ge(o_done, 2 * n + half + 1)
                    for g in range(4):
                        sq = nc.scalar.activation(squares[:, 4 * half + g, 0:DV],
                                                  ob[half][:, g * P:(g + 1) * P], ACT.Square, scale=DV ** -0.5,
                                                  accum_out=ss[:, 4 * half + g:4 * half + g + 1])
                    sq.then_inc(sq_done, 1)

            high_x(0)
            for i in range(PROJ):
                copy_proj(0, i, 0)
                if i == VG:
                    high_x(1)
            copy_e(0)
            act.wait_ge(gw_ready, 1)
            each_pair(act, step)
            copy_oT(NSTEP)

        @block.vector
        def _(dve):
            def low_x(b):
                for k in range(KT):
                    dve.wait_ge(xhi_ready, b * KT + k + 1)
                    nc.vector.tensor_tensor(xT_lo[:, k, b * T:(b + 1) * T], x_bank(b, k),
                                            xT_hi[:, k, b * T:(b + 1) * T].bitcast(F32), ALU.subtract)\
                        .then_inc(xlo_ready, 1)

            def low_left(src, turn):
                for h in range(2):
                    dve.wait_ge(left_hi_ready, 2 * turn + h + 1)
                    nc.vector.tensor_tensor(left[HALF[1 - h], h, :], src[HALF[h], :],
                                            left[HALF[h], h, :].bitcast(F32), ALU.subtract).then_inc(left_ready, 1)

            def low_right(src, turn):
                for h in range(2):
                    dve.wait_ge(right_hi_ready, 4 * turn + 2 * h + 2)
                    for half in (h, 1 - h):
                        low = nc.vector.tensor_tensor(right_lo[HALF[half], h, :], src[HALF[h], :],
                                                      right_hi[HALF[h], h, :].bitcast(F32), ALU.subtract)
                    low.then_inc(right_ready, 1)

            def clip(m, b):
                dve.wait_ge(proj_done, PROJ * m + 1)
                nc.vector.tensor_scalar(eT[:, :], pj[b % 2], CLAMP, -CLAMP, ALU.min, ALU.max).then_inc(clip_done, 1)

            def gating(m, i, b):
                dve.wait_ge(tanh_ready, 4 * m + i)
                nc.vector.scalar_tensor_tensor(out=gate[:, b % 2, i - VG, :], in0=gate[:, b % 2, i - VG, :],
                                               scalar=1.0, in1=pj[(b + i) % 2][:, 2 * DV:4 * DV], op0=ALU.add,
                                               op1=ALU.mult).then_inc(gate_ready, 1)

            def inverse_z(m):
                dve.wait_ge(eT_ready, m + 1)
                nc.vector.tensor_tensor_scan(rz[:, :], eT[:, :], eT[:, :], 0.0, ALU.add, ALU.bypass)\
                    .then_inc(scan_done, 1)
                dve.wait_ge(scan_done, m + 1)
                nc.vector.reciprocal(rz[:, 0:T // 2], rz[:, 0:T // 2]).then_inc(rz_ready, 1)

            def inverse_z_rest():
                nc.vector.reciprocal(rz[:, T // 2:T], rz[:, T // 2:T]).then_inc(rz_ready, 1)

            def mask_chunks(n, which):
                for c in (1, 2):
                    for h in range(2):
                        dve.wait_ge(chunk_done, 12 * n + 6 * which + 2 * c + h + 1)
                        m = mask[:, 2:5, :] if c == 1 else mask[:, 0:3, :]
                        bank = (okb, tb)[h] if c == 1 else ch[h]
                        nc.vector.tensor_tensor(causal[:, h, CHUNK_AT[c]:CHUNK_AT[c] + CHUNK_LEN[c]],
                                                bank[:, 0:CHUNK_LEN[c]], m.rearrange("p a t -> p (a t)"),
                                                ALU.mult).then_inc(chunk_dve, 1)

            def low_oT(n):
                for h in range(2):
                    wait(dve, oThi_ready, 2 * (n - 1) + h + 1)
                    nc.vector.scalar_tensor_tensor(out=oT_lo[:, h, :], in0=ob[h],
                                                   scalar=gw_half[:, 0:1], in1=oT_hi[:, h, :].bitcast(F32),
                                                   op0=ALU.mult, op1=ALU.subtract).then_inc(oTlo_ready, 1)

            def add_out(n, b):
                for t in range(TT):
                    wait(dve, wo_done, 4 * (n - 1) + t + 1)
                    a = acc[:, TT * b + t, :]
                    nc.vector.tensor_tensor(a, a, ob[t % 2], ALU.add).then_inc(added, 1)

            def statistics(n, b):
                dve.wait_ge(added, 4 * n)
                norm.statistics(b, b)
                dve.wait_ge(norm.stats_ready, b + 1)
                norm.aggregate(b)

            def step(n, p, j, first, last):
                b1 = (j + 1) % B
                norm_now = at(p, PAIRS - 1) and j > 0
                mask_chunks(n, 0)
                low_left(eT, 2 * n + 1)
                if not last:
                    dve.wait_ge(left_ready, 4 * n + 4)
                    clip(n + 1, b1)
                if not first:
                    low_oT(n)
                dve.wait_ge(okT_done, n + 1)
                dve.wait_ge(rz_ready, 2 * n + 2)
                nc.vector.tensor_tensor(okn, okb, rz[:, :], ALU.mult).then_inc(okn_ready, 1)
                if not last:
                    gating(n + 1, VG, b1)
                dve.wait_ge(ok_done, n + 1)
                scores = tb.rearrange("p (g m) -> p g m", m=DK)
                nc.vector.tensor_reduce(mx[:, :], scores, AX.X, ALU.max).then_inc(mx_ready, 1)
                dve.wait_ge(mx_ready, n + 1)
                nc.vector.tensor_tensor(pv, scores,
                                        mx[:, :].rearrange("p (g o) -> p g o", o=1).broadcast_to([P, 2 * TT, DK]),
                                        ALU.subtract).then_inc(sub_ready, 1)
                if not last:
                    gating(n + 1, VG + 1, b1)
                if at(n, 0) or at(n, 1):
                    low_x(n + 2)
                dve.wait_ge(pv_ready, n + 1)
                nc.vector.tensor_reduce(rowsum[:, :], pv, AX.X, ALU.add).then_inc(sum_ready, 1)
                if not first:
                    add_out(n, (j - 1) % B)
                dve.wait_ge(pvT_done, n + 1)
                nc.vector.tensor_tensor(wT, okb, rz[:, :], ALU.mult).then_inc(wT_ready, 1)
                dve.wait_ge(sum_ready, n + 1)
                nc.vector.reciprocal(rs[:, :], rowsum[:, :]).then_inc(rs_ready, 1)
                dve.wait_ge(wT_ready, n + 1)
                low_right(wT, 2 * n + 1)
                if norm_now:
                    statistics(n, j - 1)
                if not last:
                    gating(n + 1, VG + 2, b1)
                    gating(n + 1, VG + 3, b1)
                mask_chunks(n, 1)
                if norm_now:
                    norm.apply(dve, j - 1, j - 1, j - 1)
                if not last:
                    inverse_z(n + 1)
                    low_right(pj[(b1 + Q) % 2], 2 * n + 2)
                    low_left(pj[(b1 + K) % 2], 2 * n + 2)
                    inverse_z_rest()
                for half in range(2):
                    dve.wait_ge(sq_done, 2 * n + half + 1)
                    nc.vector.tensor_tensor(og[:, 4 * half:4 * half + 4, :].rearrange("p g c -> p (g c)"), ob[half],
                                            gate[:, j % 2, 2 * half:2 * half + 2, :].rearrange("p t c -> p (t c)"),
                                            ALU.mult).then_inc(og_ready, 1)

            low_x(0)
            dve.wait_ge(vg_hi_ready, 1)
            nc.vector.tensor_tensor(vg_lo[:, :, :], vg_raw, vg_hi[:, :, :].bitcast(F32), ALU.subtract)\
                .then_inc(vg_ready, 1)
            clip(0, 0)
            for i in range(4):
                gating(0, VG + i, 0)
                if i == 0:
                    low_x(1)
            low_right(pj[Q % 2], 0)
            low_left(pj[K % 2], 0)
            inverse_z(0)
            inverse_z_rest()
            dve.wait_ge(const_ready, 3)
            each_pair(dve, step)
            low_oT(NSTEP)
            add_out(NSTEP, B - 1)


def phase_cross(nc, ctx_in, acc, ident, norm):
    with ExitStack() as ctx:
        def sb(name, shape, dt=F32):
            return ctx.enter_context(nc.sbuf_tensor("x_" + name, shape, dt))

        def sem(name):
            return ctx.enter_context(nc.semaphore("x_" + name))

        xrows = sb("xrows", [P, 2, TT, P])
        krows = sb("krows", [P, 2, TT, 2 * DH])
        cv = sb("cv", [P, 4, TT, 2, 32])
        xq = sb("xq", [P, 2, TT, 8, ROWS])
        kn = sb("kn", [P, 2, TT, 2, ROWS])
        qs = sb("qs", [P, 4, 4, T], F32R)
        ks = sb("ks", [P, 4, 2, 2, T], F32R)
        prob = sb("prob", [P, 4, 2, T])
        nm = sb("nm", [P, 2, TT, 2, 4])
        mhl = sb("mhl", [P, 2, TT, 2, 2, 4])
        mT = sb("mT", [16, 2, T])
        avs = sb("avs", [P, 2, T])
        rec = sb("rec", [P, 2, TT, 4])
        avn = sb("avn", [P, 2, TT, 4, DH])
        zero = sb("zero", [P, 1, 1, 1])
        ps = ctx.enter_context(nc.psum_tensor("x_ps", [P, 8, 512], F32))
        mxb = [ps[:, 0, :], ps[:, 1, :]]
        exb = [ps[:, 2:4, :], ps[:, 4:6, :]]
        avb = ps[:, 6, :]
        trb = ps[:, 7, :]
        HALF = [slice(0, ROWS), slice(ROWS, P)]

        rows_in = [sem(f"rows_in{i}") for i in range(2)]
        keys_in = [sem(f"keys_in{i}") for i in range(2)]
        cleared = sem("cleared")
        const_ready = sem("const_ready")
        halves_clear = sem("halves_clear")
        rest_clear = sem("rest_clear")
        values_ready = sem("values_ready")
        first_hi = sem("first_hi")
        first_ready = sem("first_ready")
        ops_hi = sem("ops_hi")
        ops_ready = sem("ops_ready")
        opsT_done = sem("opsT_done")
        opsT_ready = sem("opsT_ready")
        max_done = sem("max_done")
        max_read = sem("max_read")
        mhi_ready = sem("mhi_ready")
        mhl_ready = sem("mhl_ready")
        mT_done = sem("mT_done")
        mT_ready = sem("mT_ready")
        mrow_in = sem("mrow_in")
        score_done = sem("score_done")
        exp_done = sem("exp_done")
        av_done = sem("av_done")
        avs_ready = sem("avs_ready")
        avT_done = sem("avT_done")
        rec_ready = sem("rec_ready")
        avn_ready = sem("avn_ready")
        added = sem("added")

        block = ctx.enter_context(nc.Block())

        EARLY = 6

        def operand_bank(u, i):
            return ps[:, 7 - i, :] if isinstance(u, int) and u == 0 else trb

        def max_turns(first, q, s):
            if first and q == 0 and s < 8:
                catch_up = 8 - EARLY
                return [(1, 2 * s + EARLY), (1, 2 * s + EARLY + 1)] if s < catch_up else [(1, s + 8)]
            return [(1, s + 8)] if s < 8 else [(2, s - 8)]

        def max_bank(u, i, par):
            if isinstance(u, int) and u == 0:
                return ps[:, (2 * i + par) % 6, :]
            return mxb[par]

        def each_batch(eng, body):
            body(0, True, False)
            with eng.Fori(1, B - 1) as b:
                body(b, False, False)
            body(B - 1, False, True)

        @block.sync
        def _(sp):
            def put_max_rows(u, q):
                sp.wait_ge(mT_ready, u + 1)
                for par in range(2):
                    for part in range(2):
                        row = ROWS * par + MAXROW + part
                        sp.dma_start(qs[row:row + 1, q, :, :].bitcast(F32),
                                     mT[8 * par + 4 * part:8 * par + 4 * part + 4, q % 2, :]).then_inc(mrow_in, 16)

            def get_rows(u, b, q):
                wait(sp, ops_ready, u - 1)
                wait(sp, values_ready, u - 1)
                if not (isinstance(u, int) and u < 3):
                    sp.dma_start(xrows[:, q % 2, :, :], acc[:, bass.ds(b * TT, TT), P * q:P * (q + 1)])\
                        .then_inc(rows_in[q % 2], 16)
                sp.dma_start(krows[:, q % 2, :, :], keys[:, bass.ds(b * TT, TT), 2 * DH * q:2 * DH * (q + 1)])\
                    .then_inc(keys_in[q % 2], 16)

            keys = ctx_in.rearrange("b (t p) d -> p (b t) d", p=P)
            for q in range(4):
                get_rows(q, 0, q)
            put_max_rows(0, 0)

            def body(b, first, last):
                for q in range(4):
                    if not (last and q == 3):
                        put_max_rows(b * 4 + q + 1, (q + 1) % 4)
                    if not last:
                        get_rows(b * 4 + q + 4, b + 1, q)
                if first:
                    sp.wait_ge(norm.done, TT * B)

            each_batch(sp, body)

        @block.gpsimd
        def _(pool):
            nc.gpsimd.memset(zero[:, :, :, :], 0.0).then_inc(cleared, 1)
            for buf in range(2):
                nc.gpsimd.memset(xq[:, buf, :, :, MAXROW:ROWS].rearrange("p t h r -> p (t h) r"), 0.0)\
                    .then_inc(cleared, 1)
                nc.gpsimd.memset(kn[:, buf, :, :, MAXROW + 2:ROWS].rearrange("p t g r -> p (t g) r"), 0.0)\
                    .then_inc(cleared, 1)
                nc.gpsimd.memset(kn[:, buf, :, :, MAXROW:MAXROW + 2].rearrange("p t g r -> p (t g) r"), 1.0)\
                    .then_inc(cleared, 1)
            pool.wait_ge(cleared, 7)

            def plus_zero(out, in_):
                return nc.gpsimd.tensor_tensor(out, in_, zero[:, :, :, :].broadcast_to(in_.shape), ALU.add)

            def rounded(out, in_):
                return plus_zero(out.bitcast(F32R), in_)

            def operands(u, b, q):
                wait(pool, opsT_done, TILES * (u - 1))
                pool.wait_ge(keys_in[q % 2], 16 * (2 * b + q // 2 + 1))
                if isinstance(u, int) and u < 3:
                    rows = acc[:, 0:TT, P * q:P * (q + 1)]
                else:
                    pool.wait_ge(rows_in[q % 2], 16 * (2 * b + q // 2 + 1 - (2 - q % 2)))
                    rows = xrows[:, q % 2]
                rows = rows.rearrange("p t (h c) -> p t h c", c=DH)
                x = xq[:, q % 2]
                split_rows = not (isinstance(u, int) and u == 0)
                keys = krows[:, q % 2].rearrange("p t (h c) -> p t h c", c=DH)
                k = kn[:, q % 2]
                if split_rows:
                    rounded(x[:, :, :, 0:DH], rows)
                    rounded(x[:, :, :, DH:2 * DH], rows)
                rounded(k[:, :, :, 0:DH], keys)
                rounded(k[:, :, :, 2 * DH:3 * DH], keys).then_inc(ops_hi, 1)
                pool.wait_ge(ops_hi, u + 1)
                if split_rows:
                    nc.gpsimd.tensor_tensor(x[:, :, :, 2 * DH:3 * DH].bitcast(F32R), rows, x[:, :, :, 0:DH],
                                            ALU.subtract)
                nc.gpsimd.tensor_tensor(k[:, :, :, DH:2 * DH].bitcast(F32R), keys, k[:, :, :, 0:DH], ALU.subtract)\
                    .then_inc(ops_ready, 1)
                wait(pool, av_done, 8 * (u - 3))
                plus_zero(cv[:, q, :, :, 0:DH], keys).then_inc(values_ready, 1)

            def split_max(u, q):
                pool.wait_ge(max_read, 32 * (u + 1))
                wait(pool, mT_done, u - 1)
                m = mhl[:, q % 2]
                rounded(m[:, :, :, 0, :], nm[:, q % 2]).then_inc(mhi_ready, 1)
                pool.wait_ge(mhi_ready, u + 1)
                nc.gpsimd.tensor_tensor(m[:, :, :, 1, :].bitcast(F32R), nm[:, q % 2], m[:, :, :, 0, :], ALU.subtract)\
                    .then_inc(mhl_ready, 1)

            for q in range(3):
                if q == 1:
                    nc.gpsimd.memset(cv[:, :, :, :, DH + 1:32].rearrange("p q t g c -> p (q t g) c"), 0.0)\
                        .then_inc(const_ready, 1)
                    nc.gpsimd.memset(cv[:, :, :, :, DH:DH + 1].rearrange("p q t g c -> p (q t g) c"), 1.0)\
                        .then_inc(const_ready, 1)
                operands(q, 0, q)
            split_max(0, 0)
            pool.wait_ge(mhl_ready, 1)
            for c in range(2):
                nc.gpsimd.memset(ks[HALF[1 - c], 2:4, :, c, :].rearrange("p q g t -> p (q g) t").bitcast(F32), 0.0)\
                    .then_inc(rest_clear, 1)
                pool.wait_ge(rest_clear, c + 1)

            def body(b, first, last):
                for q in range(4):
                    u = b * 4 + q
                    if not (last and q == 3):
                        split_max(u + 1, (q + 1) % 4)
                    if not (last and q >= 1):
                        operands(u + 3, b if q == 0 else b + 1, (q + 3) % 4)
                    if q == 0 and not first:
                        norm.inverse_deviation(pool, 0, B + b - 1)
                    if q == 1 and first:
                        norm.inverse_deviation(pool, B - 1, B - 1)

            each_batch(pool, body)

        @block.tensor
        def _(pe):
            def transpose_operands(u, q, i):
                if i == 0:
                    pe.wait_ge(ops_ready, u + 1)
                for t in range(TT):
                    src = kn[:, q % 2, t, :, :] if i == 0 else xq[:, q % 2, t, 2 * (i - 1):2 * i, :]
                    src = src.rearrange("p h r -> p (h r)")
                    mm = pe.transpose(operand_bank(u, i)[:, t * P:(t + 1) * P], src, ident[:, :])
                mm.then_inc(opsT_done, 1)

            def max_scores(u, q, i, par):
                tile, st = i // 4, i % 4
                if st == 0 and par == 0:
                    pe.wait_ge(opsT_ready, TILES * u + tile + 2)
                wait(pe, max_read, 32 * u + 2 * i + par - (5 if isinstance(u, int) and u == 0 else 1))
                pe.matmul(max_bank(u, i, par), qs[:, q, tile, st * P:(st + 1) * P], ks[:, q, tile // 2, par, :],
                          start=True, stop=True).then_inc(max_done, 1)

            def transpose_max(u, q):
                pe.wait_ge(mhl_ready, u + 1)
                for t in range(TT):
                    mm = pe.transpose(trb[0:16, t * P:(t + 1) * P],
                                      mhl[:, q % 2, t].rearrange("p a b c -> p (a b c)"), ident[:, :])
                mm.then_inc(mT_done, 1)

            def scores(u, q, s):
                g, t, pair = s // 8, s // 2 % 4, s % 2
                if s == 0:
                    pe.wait_ge(mrow_in, 64 * (u + 1))
                wait(pe, exp_done, 16 * u + s - 1)
                for par in range(2):
                    mm = pe.matmul(exb[s % 2][:, par, :], ks[:, q, g, par, t * P:(t + 1) * P],
                                   qs[:, q, 2 * g + pair, :], start=True, stop=True)
                mm.then_inc(score_done, 1)

            def weighted(u, q, s):
                g, t = s // 8, s // 2 % 4
                pe.wait_ge(exp_done, 16 * u + s + 2)
                if s == 0:
                    pe.wait_ge(values_ready, u + 1)
                if s % 8 == 0:
                    wait(pe, avs_ready, 2 * u + g)
                for i in range(4):
                    mm = pe.matmul(avb[32 * i:32 * (i + 1), :], cv[:, q, t, g, :], prob[:, (s + i // 2) % 4, i % 2, :],
                                   start=(t == 0), stop=(t == TT - 1))
                mm.then_inc(av_done, 1)

            def transpose_weighted(u, g):
                pe.wait_ge(avs_ready, 2 * u + g + 1)
                for t in range(TT):
                    mm = pe.transpose(trb[:, t * P:(t + 1) * P], avs[:, g, t * P:(t + 1) * P], ident[:, :])
                mm.then_inc(avT_done, 1)

            for i in range(TILES):
                if i == 1:
                    pe.wait_ge(first_ready, 1)
                transpose_operands(0, 0, i)
            pe.wait_ge(halves_clear, 2)
            for i in range(16):
                if i == 1:
                    pe.wait_ge(opsT_ready, TILES)
                for par in range(2):
                    max_scores(0, 0, i, par)
                if i % 3 == 2:
                    pe.wait_ge(opsT_ready, TILES + i // 3)
                    transpose_operands(1, 1, i // 3)
            pe.wait_ge(opsT_ready, 2 * TILES)
            pe.wait_ge(halves_clear, 4)
            for i in range(EARLY):
                if i == 2:
                    transpose_max(0, 0)
                for par in range(2):
                    max_scores(1, 1, i, par)
            pe.wait_ge(const_ready, 2)

            def one_transpose(u, q, s, first, last):
                more = not (last and q > 1)
                if s == 0 and not (first and q == 0) and not (last and q == 3):
                    pe.wait_ge(opsT_ready, TILES * (u + 1) + 4)
                    transpose_operands(u + 1, (q + 1) % 4, 4)
                if s == 2 and not (first and q == 0):
                    if last and q == 3:
                        pe.wait_ge(avn_ready, 2 * u - 1)
                    else:
                        pe.wait_ge(opsT_ready, TILES * (u + 2))
                    transpose_weighted(u - 1, 1)
                if s == 4 and more:
                    wait(pe, avn_ready, 2 * u)
                    wait(pe, mT_ready, u + 1)
                    transpose_operands(u + 2, (q + 2) % 4, 0)
                if s in (6, 8) and more:
                    i = s // 2 - 2
                    pe.wait_ge(opsT_ready, TILES * (u + 2) + i)
                    transpose_operands(u + 2, (q + 2) % 4, i)
                if s == 10 and not (last and q == 3):
                    if more:
                        pe.wait_ge(opsT_ready, TILES * (u + 2) + 3)
                    else:
                        wait(pe, avn_ready, 2 * u)
                    transpose_max(u + 1, (q + 1) % 4)
                if s == 12:
                    if last and q == 3:
                        pe.wait_ge(avn_ready, 2 * u)
                    else:
                        pe.wait_ge(mT_ready, u + 2)
                    transpose_weighted(u, 0)
                if s == 14 and more:
                    pe.wait_ge(avn_ready, 2 * u + 1)
                    transpose_operands(u + 2, (q + 2) % 4, 3)

            def body(b, first, last):
                for q in range(4):
                    u = b * 4 + q
                    for s in range(16):
                        turns = [(u + ahead, (q + ahead) % 4, i, par) for ahead, i in max_turns(first, q, s)
                                 if not (last and q + ahead > 3) for par in range(2)]
                        if first and q == 0 and s == 8:
                            pe.wait_ge(rest_clear, 2)
                        for turn in turns[:1]:
                            max_scores(*turn)
                        scores(u, q, s)
                        for turn in turns[1:]:
                            max_scores(*turn)
                        one_transpose(u, q, s, first, last)
                        if s % 2 and s > 1:
                            weighted(u, q, s - 3)
                        elif s == 1 and not (first and q == 0):
                            weighted(u - 1, (q - 1) % 4, 14)

            each_batch(pe, body)
            weighted(UNITS - 1, 3, 14)
            pe.wait_ge(avn_ready, 2 * UNITS - 1)
            transpose_weighted(UNITS - 1, 1)

        @block.scalar
        def _(act):
            def copy_keys(u, q, c):
                if c == 0:
                    act.wait_ge(opsT_done, TILES * u + 1)
                for g in range(2):
                    last = nc.scalar.copy(ks[HALF[c], q, g, c, :], operand_bank(u, 0)[HALF[g], :])
                if c == 1:
                    last.then_inc(opsT_ready, 1)

            def copy_queries(u, q, i):
                act.wait_ge(opsT_done, TILES * u + i + 1)
                nc.scalar.copy(qs[:, q, i - 1, :], operand_bank(u, i)).then_inc(opsT_ready, 1)

            def copy_max(u, q):
                act.wait_ge(mT_done, u + 1)
                wait(act, mrow_in, 64 * (u - 1))
                nc.scalar.copy(mT[:, q % 2, :], trb[0:16, :]).then_inc(mT_ready, 1)

            def copy_weighted(u, g):
                act.wait_ge(av_done, 8 * u + 4 * g + 4)
                wait(act, avT_done, 2 * u + g - 1)
                nc.scalar.copy(avs[:, g, :], avb).then_inc(avs_ready, 1)

            for u in range(2):
                copy_keys(u, u, 0)
                copy_keys(u, u, 1)
                for i in range(1, TILES):
                    copy_queries(u, u, i)
            copy_max(0, 0)

            def body(b, first, last):
                for q in range(4):
                    u = b * 4 + q
                    more = not (last and q > 1)
                    for s in range(16):
                        if s == 2 and not (first and q == 0):
                            copy_weighted(u - 1, 1)
                        if s == 10:
                            copy_weighted(u, 0)
                        act.wait_ge(score_done, 16 * u + s + 1)
                        if s % 2 == 0:
                            wait(act, av_done, 8 * u + s // 2 - 1)
                        nc.scalar.activation(prob[:, s % 4, :, :], exb[s % 2], ACT.Exp, scale=X_SCALE)\
                            .then_inc(exp_done, 1)
                        if s == 0 and not (first and q == 0) and not (last and q == 3):
                            copy_queries(u + 1, (q + 1) % 4, 4)
                        if s in (4, 5) and more:
                            copy_keys(u + 2, (q + 2) % 4, s - 4)
                        if s in (6, 8) and more:
                            copy_queries(u + 2, (q + 2) % 4, s // 2 - 2)
                        if s == 10 and not (last and q == 3):
                            copy_max(u + 1, (q + 1) % 4)
                        if s == 14 and more:
                            copy_queries(u + 2, (q + 2) % 4, 3)

            each_batch(act, body)
            copy_weighted(UNITS - 1, 1)

        @block.vector
        def _(dve):
            def reduce_max(u, q, i):
                if i == 0:
                    wait(dve, mhl_ready, u - 1)
                for par in range(2):
                    dve.wait_ge(max_done, 32 * u + 2 * i + par + 1)
                    nc.vector.tensor_reduce(nm[:, q % 2, i % 4, par, i // 4:i // 4 + 1], max_bank(u, i, par), AX.X, ALU.max,
                                            negate=True).then_inc(max_read, 1)

            def normalise(u, g):
                dve.wait_ge(avT_done, 2 * u + g + 1)
                rows = trb.rearrange("p (t h c) -> p t h c", t=TT, h=4)
                nc.vector.reciprocal(rec[:, g, :, :], rows[:, :, :, DH]).then_inc(rec_ready, 1)
                dve.wait_ge(rec_ready, 2 * u + g + 1)
                nc.vector.tensor_tensor(avn[:, g], rows[:, :, :, 0:DH],
                                        rec[:, g].rearrange("p t (h o) -> p t h o", o=1).broadcast_to([P, TT, 4, DH]),
                                        ALU.mult).then_inc(avn_ready, 1)

            def add(u, b, q, g):
                dve.wait_ge(avn_ready, 2 * u + g + 1)
                a = acc[:, bass.ds(b * TT, TT), P * q + 64 * g:P * q + 64 * (g + 1)]
                nc.vector.tensor_tensor(a, a, avn[:, g].rearrange("p t h c -> p t (h c)"), ALU.add).then_inc(added, 1)

            rows = acc[:, 0:TT, 0:P].rearrange("p t (h c) -> p t h c", c=DH)
            nc.vector.tensor_copy(xq[:, 0, :, :, 0:DH].bitcast(F32R), rows).then_inc(first_hi, 1)
            nc.vector.tensor_copy(xq[:, 0, :, :, DH:2 * DH].bitcast(F32R), rows)
            dve.wait_ge(first_hi, 1)
            nc.vector.tensor_tensor(xq[:, 0, :, :, 2 * DH:3 * DH].bitcast(F32R), rows, xq[:, 0, :, :, 0:DH],
                                    ALU.subtract).then_inc(first_ready, 1)
            for unit in range(2):
                for c in range(2):
                    nc.vector.memset(ks[HALF[1 - c], unit, :, c, :].bitcast(F32), 0.0).then_inc(halves_clear, 1)
            for i in range(16):
                reduce_max(0, 0, i)
            for i in range(EARLY):
                reduce_max(1, 1, i)

            def body(b, first, last):
                for q in range(4):
                    u = b * 4 + q
                    for s in range(16):
                        stats_unit, use_unit = q == int(first), q == int(first) + 1
                        norm_of = (B - 1, B - 1, B - 1) if first else (b - 1, 0, B + b - 1)
                        if stats_unit and s == 6 and not first:
                            dve.wait_ge(added, 2 * u)
                        if stats_unit and s == 14:
                            dve.wait_ge(norm.stats_ready, norm_of[2] + 1)
                        for ahead, i in max_turns(first, q, s):
                            if not (last and q + ahead > 3):
                                reduce_max(u + ahead, (q + ahead) % 4, i)
                        if s == 3 and not (first and q == 0):
                            normalise(u - 1, 1)
                        if s == 4 and not (first and q == 0):
                            add(u - 1, b if q else b - 1, (q - 1) % 4, 1)
                        if stats_unit and s in (6, 8, 10, 12):
                            norm.statistics(*norm_of[:2], tiles=[s // 2 - 3])
                        if stats_unit and s == 14:
                            norm.aggregate(norm_of[1])
                        if use_unit and s in (6, 8, 10, 12):
                            norm.apply(dve, *norm_of, tiles=[s // 2 - 3])
                        if s == 13:
                            normalise(u, 0)
                        if s == 14:
                            add(u, b, q, 0)

            each_batch(dve, body)
            normalise(UNITS - 1, 1)
            add(UNITS - 1, B - 1, 3, 1)


def phase_ffn(nc, gate_w, up_w, down_w, gate_s, up_s, down_s, out, acc, ident, norm):
    with ExitStack() as ctx:
        def sb(name, shape, dt=F32):
            return ctx.enter_context(nc.sbuf_tensor("f_" + name, shape, dt))

        def sem(name):
            return ctx.enter_context(nc.semaphore("f_" + name))

        xT_hi = sb("xT_hi", [P, KT, B * T], F32R)
        xT_lo = sb("xT_lo", [P, KT, B * T], F32R)
        raw_gu = sb("raw_gu", [P, 2, D])
        raw_down = sb("raw_down", [P, KT, P])
        down = sb("down", [P, KT, P])
        gu_hi = sb("gu_hi", [P, 2, D], F32R)
        gu_lo = sb("gu_lo", [P, 2, D], F32R)
        down_hi = sb("down_hi", [P, D], F32R)
        down_lo = sb("down_lo", [P, D], F32R)
        gs_half = sb("gs_half", [P, IC])
        us = sb("us", [P, IC])
        both = sb("both", [P, IC])
        ds = sb("ds", [P, KT])
        half = sb("half", [P, IC])
        now = sb("now", [P, 2])
        h = sb("h", [P, 2, T])
        h_hi = sb("h_hi", [P, 2, T], F32R)
        h_lo = sb("h_lo", [P, 2, T], F32R)
        ps = ctx.enter_context(nc.psum_tensor("f_ps", [P, 8, 512], F32))
        gub = [[ps[:, 0, :], ps[:, 1, :]], [ps[:, 2, :], ps[:, 3, :]]]
        dnb = [ps[:, 4, :], ps[:, 5, :]]
        trb = [ps[:, 6, :], ps[:, 7, :]]

        def x_bank(b, k):
            return gub[k // 2][k % 2] if b == 0 else trb[k % 2]

        def down_bank(b, t):
            return trb[t - 2] if b < 2 and t >= 2 else dnb[t % 2]

        ds_in = sem("ds_in")
        scales_in = sem("scales_in")
        half_ready = sem("half_ready")
        scales_ready = sem("scales_ready")
        raw_gu_in = sem("raw_gu_in")
        raw_down_in = sem("raw_down_in")
        down_scaled = sem("down_scaled")
        scale_now = sem("scale_now")
        xt_done = sem("xt_done")
        xhi_ready = sem("xhi_ready")
        xlo_ready = sem("xlo_ready")
        guT_done = sem("guT_done")
        downT_done = sem("downT_done")
        gu_hi_ready = sem("gu_hi_ready")
        gu_lo_ready = sem("gu_lo_ready")
        down_hi_ready = sem("down_hi_ready")
        down_lo_ready = sem("down_lo_ready")
        gu_done = sem("gu_done")
        tanh_ready = sem("tanh_ready")
        silu_ready = sem("silu_ready")
        h_ready = sem("h_ready")
        h_hi_ready = sem("h_hi_ready")
        h_lo_ready = sem("h_lo_ready")
        down_done = sem("down_done")
        added = sem("added")
        stored = sem("stored")

        block = ctx.enter_context(nc.Block())

        def each_chunk(eng, body):
            body(0, True, False)
            with eng.Fori(1, IC - 1) as c:
                body(c, False, False)
            body(IC - 1, False, True)

        @block.sync
        def _(sp):
            def load(c):
                sp.dma_start(raw_down[:, :, :],
                             down_w[:, bass.ts(c, P)].rearrange("(k p) i -> p k i", p=P)).then_inc(raw_down_in, 16)
                for w, m in enumerate((gate_w, up_w)):
                    sp.dma_start(raw_gu[:, w, :], m[bass.ts(c, P), :]).then_inc(raw_gu_in, 16)

            sp.dma_start(ds[:, :], down_s.rearrange("(c p) -> p c", p=P),
                         allow_slow_non_contiguous=True).then_inc(ds_in, 16)
            load(0)
            for scale, m in ((gs_half, gate_s), (us, up_s)):
                sp.dma_start(scale[:, :], m.rearrange("(c p) -> p c", p=P),
                             allow_slow_non_contiguous=True).then_inc(scales_in, 16)
            with sp.Fori(1, IC) as c:
                sp.wait_ge(guT_done, 2 * c)
                sp.wait_ge(down_scaled, c)
                load(c)
            for b in range(B):
                for half in range(2):
                    sp.wait_ge(norm.done, TT * (2 * B + b) + 2 * half + 2)
                    tiles = slice(TT * b + 2 * half, TT * b + 2 * half + 2)
                    sp.dma_start(out[b, 2 * P * half:2 * P * (half + 1)].rearrange("(t p) d -> p t d", p=P),
                                 acc[:, tiles, :]).then_inc(stored, 16)
            sp.wait_ge(stored, 2 * 16 * B)

        @block.gpsimd
        def _(pool):
            nc.gpsimd.memset(half[:, :], 0.5).then_inc(half_ready, 1)
            def scale_down(c):
                pool.wait_ge(raw_down_in, 16 * (c + 1))
                wait(pool, downT_done, c)
                nc.gpsimd.tensor_tensor(down[:, :, :], raw_down[:, :, :],
                                        ds[:, :].rearrange("p (k o) -> p k o", o=1).broadcast_to([P, KT, P]),
                                        ALU.mult).then_inc(down_scaled, 1)

            def low_h(v, b):
                pool.wait_ge(h_hi_ready, v + 1)
                nc.gpsimd.tensor_tensor(h_lo[:, b % 2, :], h[:, b % 2, :], h_hi[:, b % 2, :].bitcast(F32),
                                        ALU.subtract).then_inc(h_lo_ready, 1)

            pool.wait_ge(ds_in, 16)
            scale_down(0)
            pool.wait_ge(half_ready, 1)
            pool.wait_ge(scales_in, 32)
            nc.gpsimd.tensor_tensor(gs_half[:, :], gs_half[:, :], half[:, :], ALU.mult).then_inc(scales_ready, 1)
            pool.wait_ge(scales_ready, 1)
            nc.gpsimd.tensor_tensor(both[:, :], gs_half[:, :], us[:, :], ALU.mult).then_inc(scales_ready, 1)
            norm.inverse_deviation(pool, 0, 2 * B - 1)

            def body(c, first, last):
                for b in range(B):
                    low_h(c * B + b, b)
                    if b == 0 and not last:
                        scale_down(c + 1)
                    if last:
                        norm.inverse_deviation(pool, b, 2 * B + b)

            each_chunk(pool, body)

        @block.tensor
        def _(pe):
            def transpose_gu(c):
                pe.wait_ge(raw_gu_in, 32 * (c + 1))
                for w in range(2):
                    if w == 0:
                        wait(pe, down_lo_ready, c)
                        if not (isinstance(c, int) and c == 0):
                            pe.wait_ge(added, 4 * (4 * c - 2))
                    else:
                        wait(pe, gu_lo_ready, 2 * c)
                    for k in range(KT):
                        mm = pe.transpose(trb[w][:, k * P:(k + 1) * P], raw_gu[:, w, k * P:(k + 1) * P], ident[:, :])
                    mm.then_inc(guT_done, 1)

            def transpose_down(c):
                pe.wait_ge(down_scaled, c + 1)
                pe.wait_ge(gu_lo_ready, 2 * c + 1)
                for k in range(KT):
                    mm = pe.transpose(trb[0][:, k * P:(k + 1) * P], down[:, k, :], ident[:, :])
                mm.then_inc(downT_done, 1)

            def gate_up(v, c, b, x_batch=None):
                if x_batch is not None:
                    transpose_x(x_batch, (0, 1))
                pe.wait_ge(gu_lo_ready, 2 * c + 2)
                wait(pe, h_ready, v - 1)
                for w in range(2):
                    if w == 1 and x_batch is not None:
                        transpose_x(x_batch, (2, 3))
                    for k in range(KT):
                        mm = mm3(pe, gub[b % 2][w],
                                 (gu_hi[:, w, k * P:(k + 1) * P], gu_lo[:, w, k * P:(k + 1) * P]),
                                 (xT_hi[:, k, b * T:(b + 1) * T], xT_lo[:, k, b * T:(b + 1) * T]), k == 0, k == KT - 1)
                    mm.then_inc(gu_done, 1)

            def project_down(v, c, b, next_chunk=None):
                pe.wait_ge(down_lo_ready, c + 1)
                pe.wait_ge(h_lo_ready, v + 1)
                for t in range(TT):
                    if b >= 2 or b == 0 and t < 2:
                        wait(pe, added, 4 * v + t - (3 if b == 2 and t < 2 else 1))
                    elif b == 1:
                        pe.wait_ge(added, 4 * v + t - 3)
                    s = slice(t * P, (t + 1) * P)
                    mm3(pe, down_bank(b, t), (h_hi[:, b % 2, s], h_lo[:, b % 2, s]), (down_hi[:, :], down_lo[:, :]),
                        True, True).then_inc(down_done, 1)
                    if t == 0 and next_chunk is not None:
                        transpose_gu(next_chunk)

            def transpose_x(b, tiles):
                if b == B - 1 and 0 in tiles:
                    pe.wait_ge(norm.done, TT * 2 * B)
                    pe.wait_ge(added, TT)
                for k in tiles:
                    u = b * KT + k
                    if u == KT:
                        pe.wait_ge(down_lo_ready, 1)
                    if b:
                        wait(pe, xlo_ready, u - 1)
                    for t in range(TT):
                        mm = pe.transpose(x_bank(b, k)[:, t * P:(t + 1) * P], acc[:, TT * b + t, k * P:(k + 1) * P],
                                          ident[:, :])
                    mm.then_inc(xt_done, 1)

            transpose_x(0, range(KT))
            transpose_gu(0)
            transpose_down(0)
            pe.wait_ge(xlo_ready, KT)
            gate_up(0, 0, 0, 1)

            def body(c, first, last):
                for b in range(B):
                    v = c * B + b
                    if first and b < B - 1:
                        pe.wait_ge(xlo_ready, (b + 2) * KT)
                    if b == 3 and not last:
                        transpose_down(c + 1)
                    if not (last and b == 3):
                        gate_up(v + 1, c if b < 3 else c + 1, (b + 1) % B, b + 2 if first and b < 2 else None)
                    if first and b < 2:
                        pe.wait_ge(xlo_ready, (b + 3) * KT)
                    project_down(v, c, b, c + 1 if b == 2 and not last else None)

            each_chunk(pe, body)

        @block.scalar
        def _(act):
            def high_gu(c):
                for w in range(2):
                    act.wait_ge(guT_done, 2 * c + w + 1)
                    nc.scalar.copy(gu_hi[:, w, :], trb[w]).then_inc(gu_hi_ready, 1)

            def high_down(c):
                act.wait_ge(downT_done, c + 1)
                wait(act, down_done, 16 * c)
                nc.scalar.copy(down_hi[:, :], trb[0]).then_inc(down_hi_ready, 1)

            def tanh(v, c, b):
                act.wait_ge(gu_done, 2 * v + 1)
                wait(act, h_lo_ready, v - 1)
                wait(act, scale_now, c + 1)
                nc.scalar.activation(h[:, b % 2, :], gub[b % 2][0], ACT.Tanh, scale=now[:, 0:1])\
                    .then_inc(tanh_ready, 1)

            def high_h(v, b):
                act.wait_ge(h_ready, v + 1)
                wait(act, down_done, 4 * (v - 1))
                nc.scalar.copy(h_hi[:, b % 2, :], h[:, b % 2, :]).then_inc(h_hi_ready, 1)

            def high_x(b):
                for k in range(KT):
                    act.wait_ge(xt_done, b * KT + k + 1)
                    nc.scalar.copy(xT_hi[:, k, b * T:(b + 1) * T], x_bank(b, k)).then_inc(xhi_ready, 1)

            high_x(0)
            high_gu(0)
            high_down(0)
            high_x(1)
            tanh(0, 0, 0)
            high_h(0, 0)

            def body(c, first, last):
                for b in range(B):
                    v = c * B + b
                    if first and b < 2:
                        high_x(b + 2)
                    if not (last and b == 3):
                        tanh(v + 1, c if b < 3 else c + 1, (b + 1) % B)
                    if b == 2 and not last:
                        high_gu(c + 1)
                    if not (last and b == 3):
                        high_h(v + 1, (b + 1) % B)
                    if b == 3 and not last:
                        high_down(c + 1)

            each_chunk(act, body)

        @block.vector
        def _(dve):
            def low_gu(c, which=(0, 1)):
                for w in which:
                    dve.wait_ge(gu_hi_ready, 2 * c + w + 1)
                    nc.vector.tensor_tensor(gu_lo[:, w, :], trb[w], gu_hi[:, w, :].bitcast(F32), ALU.subtract)\
                        .then_inc(gu_lo_ready, 1)

            def low_down(c):
                dve.wait_ge(down_hi_ready, c + 1)
                nc.vector.tensor_tensor(down_lo[:, :], trb[0], down_hi[:, :].bitcast(F32), ALU.subtract)\
                    .then_inc(down_lo_ready, 1)

            def inner(v, c, b):
                dve.wait_ge(tanh_ready, v + 1)
                nc.vector.scalar_tensor_tensor(out=h[:, b % 2, :], in0=h[:, b % 2, :], scalar=1.0,
                                               in1=gub[b % 2][0], op0=ALU.add, op1=ALU.mult).then_inc(silu_ready, 1)
                dve.wait_ge(silu_ready, v + 1)
                dve.wait_ge(gu_done, 2 * v + 2)
                nc.vector.scalar_tensor_tensor(out=h[:, b % 2, :], in0=gub[b % 2][1], scalar=now[:, 1:2],
                                               in1=h[:, b % 2, :], op0=ALU.mult, op1=ALU.mult).then_inc(h_ready, 1)

            def take_scales(c):
                nc.vector.tensor_copy(now[:, 0:1], gs_half[:, bass.ds(c, 1)])
                nc.vector.tensor_copy(now[:, 1:2], both[:, bass.ds(c, 1)]).then_inc(scale_now, 1)

            def add_out(v, b, next_chunk=None, last=False):
                for t in range(TT):
                    if next_chunk is not None and t in (1, 2):
                        low_gu(next_chunk, (t - 1,))
                    dve.wait_ge(down_done, 4 * v + t + 1)
                    a = acc[:, TT * b + t, :]
                    nc.vector.tensor_tensor(a, a, down_bank(b, t), ALU.add).then_inc(added, 1)
                    if last and t:
                        dve.wait_ge(added, 4 * v + t)
                        norm.statistics(b, b, [t - 1])
                if last:
                    dve.wait_ge(added, 4 * v + TT)
                    norm.statistics(b, b, [TT - 1])

            def low_x(b):
                for k in range(KT):
                    dve.wait_ge(xhi_ready, b * KT + k + 1)
                    nc.vector.tensor_tensor(xT_lo[:, k, b * T:(b + 1) * T], x_bank(b, k),
                                            xT_hi[:, k, b * T:(b + 1) * T].bitcast(F32), ALU.subtract)\
                        .then_inc(xlo_ready, 1)

            low_x(0)
            low_gu(0)
            low_down(0)
            dve.wait_ge(scales_ready, 2)
            take_scales(0)
            low_x(1)
            norm.statistics(B - 1, 0)
            dve.wait_ge(norm.stats_ready, 2 * B)
            norm.aggregate(0)
            inner(0, 0, 0)

            def body(c, first, last):
                for b in range(B):
                    v = c * B + b
                    if first and b == 0:
                        norm.apply(dve, B - 1, 0, 2 * B - 1)
                    if first and b < 2:
                        low_x(b + 2)
                    if b == 3 and not last:
                        take_scales(c + 1)
                    if not (last and b == 3):
                        inner(v + 1, c if b < 3 else c + 1, (b + 1) % B)
                    add_out(v, b, c + 1 if b == 2 and not last else None, last)
                    if b == 3 and not last:
                        low_down(c + 1)
                    if last:
                        dve.wait_ge(norm.stats_ready, 2 * B + b + 1)
                        norm.aggregate(b)
                        norm.apply(dve, b, b, 2 * B + b)

            each_chunk(dve, body)


def decoder_layer(nc, x, ctx_in, Wq, Wk, Wv, Wg, Ws, Wo, gw, gate_w, up_w, down_w, gate_s, up_s, down_s, out):
    with ExitStack() as ctx:
        acc = ctx.enter_context(nc.sbuf_tensor("acc", [P, NTT, D], F32))
        ident = ctx.enter_context(nc.sbuf_tensor("ident", [P, P], F32))
        norm = Norm(ctx, nc, "norm", acc, B)
        phase_attention(nc, x, Wq, Wk, Wv, Wg, Ws, Wo, gw, acc, ident, norm)
        phase_cross(nc, ctx_in, acc, ident, norm)
        phase_ffn(nc, gate_w, up_w, down_w, gate_s, up_s, down_s, out, acc, ident, norm)


_INS = ['x', 'ctx_512', 'L0_attn_Wq', 'L0_attn_Wk', 'L0_attn_Wv', 'L0_attn_Wg', 'L0_attn_Ws', 'L0_attn_Wo',
        'L0_attn_g_norm_weight', 'L0_ffn_gate_w', 'L0_ffn_up_w', 'L0_ffn_down_w', 'L0_ffn_gate_s', 'L0_ffn_up_s',
        'L0_ffn_down_s']
_OUTS = [((4, 512, 512), 'float32')]


def kernel(**inputs):
    import numpy as _np
    import concourse.bacc as _bacc
    from concourse import mybir as _mybir
    from concourse.bass_utils import run_bass_kernel_spmd as _run

    nc = _bacc.Bacc("TRN2", target_bir_lowering=False, num_devices=1)
    arrays, args = {}, []
    for name in _INS:
        a = _np.ascontiguousarray(inputs[name])
        arrays[f"in_{name}_dram"] = a
        args.append(nc.dram_tensor(f"in_{name}_dram", a.shape, _mybir.dt.from_np(a.dtype), kind="ExternalInput").ap())
    for i, (shape, dtype) in enumerate(_OUTS):
        dt = _mybir.dt.from_np(_np.dtype(dtype))
        args.append(nc.dram_tensor(f"out_{i}_dram", shape, dt, kind="ExternalOutput").ap())
    decoder_layer(nc, *args)
    r = _run(nc, [arrays], core_ids=[0])
    return r.results[0]["out_0_dram"]
```
